# Optimizing a Trainium2 kernel written in Bass

```python
import numpy as np
import jax
import jax.numpy as jnp

def _softmax(x, axis=-1):
    return jax.nn.softmax(x, axis=axis)

def _gelu(x):
    return jax.nn.gelu(x, approximate=True)

def _silu(x):
    return jax.nn.silu(x)

def _sigmoid(x):
    return jax.nn.sigmoid(x)

def _layernorm(x, axis=-1, eps=1e-05):
    m = jnp.mean(x, axis=axis, keepdims=True)
    v = jnp.var(x, axis=axis, keepdims=True)
    return (x - m) / jnp.sqrt(v + eps)

def _scatter_add(tgt, idx, src, axis=0):
    return tgt.at[idx].add(src)

def _segment_sum(src, seg, n):
    return jax.ops.segment_sum(src, seg, n)
kernel_name = 'mk_early_fusion_d2_tok_img512_r4_7e0e59'

def setup_inputs(seed: int=0):
    np.random.seed(seed)
    _w = jnp.asarray

    def _rec_inputs():
        import jax
        import jax.numpy as jnp
        _rk = jax.random.key(seed)
        x = -0.000356955 + 1 * jax.random.normal(jax.random.fold_in(_rk, 1), (32, 3, 96, 96), jnp.float32)
        txt = 0.0185972 + 1.43333 * jax.random.normal(jax.random.fold_in(_rk, 2), (32, 77, 128), jnp.float32)
        return (x, txt)
    x, txt = _rec_inputs()

    def _L0_tok_setup():
        import jax, jax.numpy as jnp
        import numpy as np
        key = jax.random.key(seed)
        k1, k2, k3 = jax.random.split(key, 3)
        B, C, H, W = (128, 3, 224, 224)
        E, p = (128, 16)
        K = C * p * p
        img = jax.random.normal(k1, (B, C, H, W), dtype=jnp.float32)
        w = jax.random.normal(k2, (E, K), dtype=jnp.float32) * (1.0 / np.sqrt(K))
        b = jax.random.normal(k3, (E,), dtype=jnp.float32)
        return {'img': img, 'w': w, 'b': b, 'patch_size': p}
    _L0_tok_all = _L0_tok_setup()
    _L0_tok_in = {k: v for k, v in _L0_tok_all.items() if k in ('w', 'b')}
    del _L0_tok_all

    def _L0_attn_setup():
        import jax, jax.numpy as jnp
        import numpy as np
        THRE = 4.0
        EPS = 1e-05

        @jax.custom_vjp
        def spike(x):
            return jnp.floor(jnp.clip(x, 0.0, THRE) + 0.5)

        def _spike_fwd(x):
            return (spike(x), x)

        def _spike_bwd(x, g):
            return (g * ((x > 0) & (x < THRE)).astype(g.dtype),)
        spike.defvjp(_spike_fwd, _spike_bwd)
        key = jax.random.key(seed)
        k0, k1, k2 = jax.random.split(key, 3)
        B, N, C = (4, 256, 128)
        x = jax.random.normal(k0, (B, N, C), jnp.float32)
        Wqkv = jax.random.normal(k1, (3 * C, C), jnp.float32) * C ** (-0.5)
        gamma = jnp.ones((3 * C,), jnp.float32)
        beta = jnp.zeros((3 * C,), jnp.float32)
        Wproj = jax.random.normal(k2, (C, C), jnp.float32) * C ** (-0.5)
        bproj = jnp.zeros((C,), jnp.float32)
        return {'x': x, 'Wqkv': Wqkv, 'gamma': gamma, 'beta': beta, 'Wproj': Wproj, 'bproj': bproj}
    _L0_attn_all = _L0_attn_setup()
    _L0_attn_in = {k: v for k, v in _L0_attn_all.items() if k in ('Wqkv', 'gamma', 'beta', 'Wproj', 'bproj')}
    del _L0_attn_all

    def _L0_ffn_setup():
        import jax, jax.numpy as jnp
        import numpy as np
        NUM_EXPERTS = 32
        GROUP_SIZE = 4
        NUM_GROUPS = NUM_EXPERTS // GROUP_SIZE
        C_CAP = 1.0
        key = jax.random.key(seed)
        ks = jax.random.split(key, 5)
        B, S, H = (16, 512, 128)
        D_FF = int(H * 4 * (2.0 / 3.0))
        x = jax.random.normal(ks[0], (B, S, H), dtype=jnp.float32)
        W_router = jax.random.normal(ks[1], (H, NUM_EXPERTS), dtype=jnp.float32) * (1.0 / np.sqrt(H))
        b_router = jnp.zeros((NUM_EXPERTS,), dtype=jnp.float32)
        W_up = jax.random.normal(ks[2], (NUM_GROUPS, H, D_FF), dtype=jnp.float32) * (1.0 / np.sqrt(H))
        b_up = jnp.zeros((NUM_GROUPS, D_FF), dtype=jnp.float32)
        W_down = jax.random.normal(ks[3], (NUM_EXPERTS, D_FF, H), dtype=jnp.float32) * (1.0 / np.sqrt(D_FF))
        b_down = jnp.zeros((NUM_EXPERTS, H), dtype=jnp.float32)
        return {'x': x, 'W_router': W_router, 'b_router': b_router, 'W_up': W_up, 'b_up': b_up, 'W_down': W_down, 'b_down': b_down}
    _L0_ffn_all = _L0_ffn_setup()
    _L0_ffn_in = {k: v for k, v in _L0_ffn_all.items() if k in ('W_router', 'b_router', 'W_up', 'b_up', 'W_down', 'b_down')}
    del _L0_ffn_all

    def _L1_attn_setup():
        import jax, jax.numpy as jnp
        import numpy as np
        N_HEADS = 8
        N_GROUPS = 4
        B, T, D = (16, 256, 128)
        GH = D // N_HEADS * N_GROUPS

        def _rope_tables(t, d):
            i = np.arange(d // 2, dtype=np.float64)
            theta = 10000.0 ** (-(2.0 * (i - 1.0))) / d
            ang = np.arange(t, dtype=np.float64)[:, None] * theta[None, :]
            return (jnp.asarray(np.cos(ang), jnp.float32), jnp.asarray(np.sin(ang), jnp.float32))

        def _apply_rope(x, cos, sin):
            xe, xo = (x[..., 0::2], x[..., 1::2])
            oe = xe * cos + xo * sin
            oo = -xe * sin + xo * cos
            return jnp.stack([oe, oo], axis=-1).reshape(x.shape)
        key = jax.random.key(seed)
        k1, k2, k3, k4 = jax.random.split(key, 4)
        x = jax.random.normal(k1, (B, T, D), dtype=jnp.float32)
        Wq = jax.random.normal(k2, (D, D), dtype=jnp.float32) * D ** (-0.5)
        Wk = jax.random.normal(k3, (D, GH), dtype=jnp.float32) * D ** (-0.5)
        Wv = jax.random.normal(k4, (D, GH), dtype=jnp.float32) * D ** (-0.5)
        return {'x': x, 'Wq': Wq, 'Wk': Wk, 'Wv': Wv}
    _L1_attn_all = _L1_attn_setup()
    _L1_attn_in = {k: v for k, v in _L1_attn_all.items() if k in ('Wq', 'Wk', 'Wv')}
    del _L1_attn_all

    def _L1_ffn_setup():
        import jax, jax.numpy as jnp
        import numpy as np
        EPS = 1e-05
        NUM_HEADS = 8
        TOP_K = 2
        CAP_FACTOR = 2

        def layernorm(x, g, b):
            m = jnp.mean(x, axis=-1, keepdims=True)
            v = jnp.var(x, axis=-1, keepdims=True)
            return (x - m) * jax.lax.rsqrt(v + EPS) * g + b
        key = jax.random.key(seed)
        ks = jax.random.split(key, 16)
        B, S, H, E, F = (2, 512, 128, 64, 512)
        s = 0.02
        return {'x': jax.random.normal(ks[0], (B, S, H), jnp.float32), 'ln1_g': jnp.ones((H,), jnp.float32), 'ln1_b': jnp.zeros((H,), jnp.float32), 'wq': jax.random.normal(ks[1], (H, H), jnp.float32) * s, 'wk': jax.random.normal(ks[2], (H, H), jnp.float32) * s, 'wv': jax.random.normal(ks[3], (H, H), jnp.float32) * s, 'wo': jax.random.normal(ks[4], (H, H), jnp.float32) * s, 'ln2_g': jnp.ones((H,), jnp.float32), 'ln2_b': jnp.zeros((H,), jnp.float32), 'wr': jax.random.normal(ks[5], (H, E), jnp.float32) * s, 'w1': jax.random.normal(ks[6], (E, H, F), jnp.float32) * s, 'b1': jnp.zeros((E, F), jnp.float32), 'w2': jax.random.normal(ks[7], (E, F, H), jnp.float32) * s, 'b2': jnp.zeros((E, H), jnp.float32)}
    _L1_ffn_all = _L1_ffn_setup()
    _L1_ffn_in = {k: v for k, v in _L1_ffn_all.items() if k in ('ln1_g', 'ln1_b', 'wq', 'wk', 'wv', 'wo', 'ln2_g', 'ln2_b', 'wr', 'w1', 'b1', 'w2', 'b2')}
    del _L1_ffn_all
    return {'x': x, 'txt': txt, 'L0_tok_w': _L0_tok_in['w'], 'L0_tok_b': _L0_tok_in['b'], 'L0_attn_Wqkv': _L0_attn_in['Wqkv'], 'L0_attn_gamma': _L0_attn_in['gamma'], 'L0_attn_beta': _L0_attn_in['beta'], 'L0_attn_Wproj': _L0_attn_in['Wproj'], 'L0_attn_bproj': _L0_attn_in['bproj'], 'L0_ffn_W_router': _L0_ffn_in['W_router'], 'L0_ffn_b_router': _L0_ffn_in['b_router'], 'L0_ffn_W_up': _L0_ffn_in['W_up'], 'L0_ffn_b_up': _L0_ffn_in['b_up'], 'L0_ffn_W_down': _L0_ffn_in['W_down'], 'L0_ffn_b_down': _L0_ffn_in['b_down'], 'L1_attn_Wq': _L1_attn_in['Wq'], 'L1_attn_Wk': _L1_attn_in['Wk'], 'L1_attn_Wv': _L1_attn_in['Wv'], 'L1_ffn_ln1_g': _L1_ffn_in['ln1_g'], 'L1_ffn_ln1_b': _L1_ffn_in['ln1_b'], 'L1_ffn_wq': _L1_ffn_in['wq'], 'L1_ffn_wk': _L1_ffn_in['wk'], 'L1_ffn_wv': _L1_ffn_in['wv'], 'L1_ffn_wo': _L1_ffn_in['wo'], 'L1_ffn_ln2_g': _L1_ffn_in['ln2_g'], 'L1_ffn_ln2_b': _L1_ffn_in['ln2_b'], 'L1_ffn_wr': _L1_ffn_in['wr'], 'L1_ffn_w1': _L1_ffn_in['w1'], 'L1_ffn_b1': _L1_ffn_in['b1'], 'L1_ffn_w2': _L1_ffn_in['w2'], 'L1_ffn_b2': _L1_ffn_in['b2']}

def reference(x, txt, L0_tok_w, L0_tok_b, L0_attn_Wqkv, L0_attn_gamma, L0_attn_beta, L0_attn_Wproj, L0_attn_bproj, L0_ffn_W_router, L0_ffn_b_router, L0_ffn_W_up, L0_ffn_b_up, L0_ffn_W_down, L0_ffn_b_down, L1_attn_Wq, L1_attn_Wk, L1_attn_Wv, L1_ffn_ln1_g, L1_ffn_ln1_b, L1_ffn_wq, L1_ffn_wk, L1_ffn_wv, L1_ffn_wo, L1_ffn_ln2_g, L1_ffn_ln2_b, L1_ffn_wr, L1_ffn_w1, L1_ffn_b1, L1_ffn_w2, L1_ffn_b2):
    import jax
    import jax.numpy as jnp

    def _L0_tok_ref(img, w, b, patch_size):
        import jax, jax.numpy as jnp
        import numpy as np
        B, C, H, W = img.shape
        p = patch_size
        Hp, Wp = (H // p, W // p)
        S = Hp * Wp
        patches = img.reshape(B, C, Hp, p, Wp, p)
        patches = patches.transpose(0, 2, 4, 1, 3, 5).reshape(B, S, C * p * p)
        out = jnp.einsum('bsk,ek->bse', patches, w) + b
        return out

    def _L0_attn_ref(x, Wqkv, gamma, beta, Wproj, bproj):
        import jax, jax.numpy as jnp
        import numpy as np
        THRE = 4.0
        EPS = 1e-05

        @jax.custom_vjp
        def spike(x):
            return jnp.floor(jnp.clip(x, 0.0, THRE) + 0.5)

        def _spike_fwd(x):
            return (spike(x), x)

        def _spike_bwd(x, g):
            return (g * ((x > 0) & (x < THRE)).astype(g.dtype),)
        spike.defvjp(_spike_fwd, _spike_bwd)
        B, N, C = x.shape
        H = 8
        hd = C // H
        scale = hd ** (-0.5)
        xs = spike(x)
        qkv = jnp.einsum('bnc,dc->bnd', xs, Wqkv)
        mu = qkv.mean(axis=(0, 1))
        var = qkv.var(axis=(0, 1))
        qkv = (qkv - mu) * jax.lax.rsqrt(var + EPS) * gamma + beta
        qkv = qkv.reshape(B, N, 3, H, hd).transpose(2, 0, 3, 1, 4)
        q = spike(qkv[0])
        k = spike(qkv[1])
        v = spike(qkv[2])
        attn = jnp.einsum('bhnd,bhmd->bhnm', q, k)
        attn = spike(attn)
        out = jnp.einsum('bhnm,bhmd->bhnd', attn, v) * scale
        out = out.transpose(0, 2, 1, 3).reshape(B, N, C)
        out = spike(out)
        return jnp.einsum('bnc,dc->bnd', out, Wproj) + bproj

    def _L0_ffn_ref(x, W_router, b_router, W_up, b_up, W_down, b_down):
        import jax, jax.numpy as jnp
        import numpy as np
        NUM_EXPERTS = 32
        GROUP_SIZE = 4
        NUM_GROUPS = NUM_EXPERTS // GROUP_SIZE
        C_CAP = 1.0
        B, S, H = x.shape
        bs = B * S
        E = NUM_EXPERTS
        k = min(int(bs * C_CAP) // E, bs)
        xf = x.reshape(bs, H)
        h = xf @ W_router + b_router
        Sm = jax.nn.softmax(h, axis=-1)
        G_ek, idx_ek = jax.lax.top_k(Sm.T, k)
        tokens = xf[idx_ek]
        D_FF = W_up.shape[-1]
        tok_g = tokens.reshape(NUM_GROUPS, GROUP_SIZE, k, H)
        up = jnp.einsum('gjkh,ghf->gjkf', tok_g, W_up) + b_up[:, None, None, :]
        act = jax.nn.silu(up).reshape(E, k, D_FF)
        Eout = jnp.einsum('ekf,efh->ekh', act, W_down) + b_down[:, None, :]
        weighted = G_ek[..., None] * Eout
        y = jnp.zeros((bs, H), dtype=x.dtype).at[idx_ek.reshape(-1)].add(weighted.reshape(-1, H))
        return y.reshape(B, S, H)

    def _L1_attn_ref(x, Wq, Wk, Wv):
        import jax, jax.numpy as jnp
        import numpy as np
        N_HEADS = 8
        N_GROUPS = 4
        B, T, D = (16, 256, 128)
        GH = D // N_HEADS * N_GROUPS

        def _rope_tables(t, d):
            i = np.arange(d // 2, dtype=np.float64)
            theta = 10000.0 ** (-(2.0 * (i - 1.0))) / d
            ang = np.arange(t, dtype=np.float64)[:, None] * theta[None, :]
            return (jnp.asarray(np.cos(ang), jnp.float32), jnp.asarray(np.sin(ang), jnp.float32))

        def _apply_rope(x, cos, sin):
            xe, xo = (x[..., 0::2], x[..., 1::2])
            oe = xe * cos + xo * sin
            oo = -xe * sin + xo * cos
            return jnp.stack([oe, oo], axis=-1).reshape(x.shape)
        b, t, c = x.shape
        n, ng = (N_HEADS, N_GROUPS)
        h = c // n
        npg = n // ng
        gh = h * ng
        cq, sq = _rope_tables(t, c)
        ck, sk = _rope_tables(t, gh)
        q = _apply_rope(x @ Wq, cq, sq)
        k = _apply_rope(x @ Wk, ck, sk)
        v = x @ Wv
        q = q.reshape(b, t, ng, npg, h)
        k = k.reshape(b, t, ng, h)
        v = v.reshape(b, t, ng, h)
        att = jnp.einsum('bigph,bjgh->bgpij', q, k) / h ** 0.5
        causal = jnp.tril(jnp.ones((t, t), dtype=bool))
        att = jnp.where(causal, att, -jnp.inf)
        att = jax.nn.softmax(att, axis=-1)
        out = jnp.einsum('bgpij,bjgh->bgpih', att, v)
        return jnp.transpose(out, (0, 2, 1, 3, 4)).reshape(b, t, c)

    def _L1_ffn_ref(x, ln1_g, ln1_b, wq, wk, wv, wo, ln2_g, ln2_b, wr, w1, b1, w2, b2):
        import jax, jax.numpy as jnp
        import numpy as np
        EPS = 1e-05
        NUM_HEADS = 8
        TOP_K = 2
        CAP_FACTOR = 2

        def layernorm(x, g, b):
            m = jnp.mean(x, axis=-1, keepdims=True)
            v = jnp.var(x, axis=-1, keepdims=True)
            return (x - m) * jax.lax.rsqrt(v + EPS) * g + b
        B, S, H = x.shape
        NH = NUM_HEADS
        dh = H // NH
        x1 = layernorm(x, ln1_g, ln1_b)
        q = (x1 @ wq).reshape(B, S, NH, dh)
        k = (x1 @ wk).reshape(B, S, NH, dh)
        v = (x1 @ wv).reshape(B, S, NH, dh)
        scores = jnp.einsum('bqhd,bkhd->bhqk', q, k) * dh ** (-0.5)
        p = jax.nn.softmax(scores, axis=-1)
        attn_out = jnp.einsum('bhqk,bkhd->bqhd', p, v).reshape(B, S, H) @ wo
        x = x + attn_out
        x2 = layernorm(x, ln2_g, ln2_b).reshape(B * S, H)
        T = B * S
        E = wr.shape[1]
        C = CAP_FACTOR * (T * TOP_K // E)
        probs = jax.nn.softmax(x2 @ wr, axis=-1)
        gate_v, gate_i = jax.lax.top_k(probs, TOP_K)
        gate_v = gate_v / jnp.sum(gate_v, axis=-1, keepdims=True)
        ef = gate_i.reshape(-1)
        gf = gate_v.reshape(-1)
        oh = jax.nn.one_hot(ef, E, dtype=x2.dtype)
        pos = jnp.sum((jnp.cumsum(oh, axis=0) - oh) * oh, axis=1).astype(jnp.int32)
        keep = (pos < C).astype(x2.dtype)
        posc = jnp.minimum(pos, C - 1)
        tok = jnp.repeat(x2, TOP_K, axis=0) * keep[:, None]
        buf = jnp.zeros((E, C, H), x2.dtype).at[ef, posc].add(tok)
        h = jax.nn.gelu(jnp.einsum('ech,ehf->ecf', buf, w1) + b1[:, None, :])
        y = jnp.einsum('ecf,efh->ech', h, w2) + b2[:, None, :]
        ys = y[ef, posc] * (gf * keep)[:, None]
        moe_out = ys.reshape(T, TOP_K, H).sum(axis=1).reshape(B, S, H)
        return x + moe_out
    h = _L0_tok_ref(x, L0_tok_w, L0_tok_b, 16)
    h = jnp.concatenate([h, txt], axis=1)
    h = h + _L0_attn_ref(_layernorm(h, axis=-1), L0_attn_Wqkv, L0_attn_gamma, L0_attn_beta, L0_attn_Wproj, L0_attn_bproj)
    h = h + _L0_ffn_ref(_layernorm(h, axis=-1), L0_ffn_W_router, L0_ffn_b_router, L0_ffn_W_up, L0_ffn_b_up, L0_ffn_W_down, L0_ffn_b_down)
    h = h + _L1_attn_ref(_layernorm(h, axis=-1), L1_attn_Wq, L1_attn_Wk, L1_attn_Wv)
    h = h + _L1_ffn_ref(_layernorm(h, axis=-1), L1_ffn_ln1_g, L1_ffn_ln1_b, L1_ffn_wq, L1_ffn_wk, L1_ffn_wv, L1_ffn_wo, L1_ffn_ln2_g, L1_ffn_ln2_b, L1_ffn_wr, L1_ffn_w1, L1_ffn_b1, L1_ffn_w2, L1_ffn_b2)
    return h

_drawn_inputs = setup_inputs


def setup_inputs(seed=0):
    import zlib

    import numpy as np

    out = dict(_drawn_inputs(seed))
    spreads = {'L0_attn_gamma': (1.0, 0.2),
     'L0_attn_beta': (0.0, 0.1),
     'L0_attn_bproj': (0.0, 0.307),
     'L0_ffn_b_router': (0.0, 0.8),
     'L0_ffn_b_up': (0.0, 0.8),
     'L0_ffn_b_down': (0.0, 0.8),
     'L1_ffn_ln1_g': (1.0, 0.6),
     'L1_ffn_ln1_b': (0.0, 0.8),
     'L1_ffn_ln2_g': (1.0, 0.6),
     'L1_ffn_ln2_b': (0.0, 0.8),
     'L1_ffn_b1': (0.0, 0.8),
     'L1_ffn_b2': (0.0, 0.8)}
    factors = {'L0_ffn_W_router': 4.458,
     'L0_ffn_W_up': 5.294,
     'L0_ffn_W_down': 4.926,
     'L1_attn_Wq': 8.0,
     'L1_attn_Wk': 8.0,
     'L1_ffn_wq': 8.0,
     'L1_ffn_wk': 8.0,
     'L1_ffn_wv': 5.587,
     'L1_ffn_wo': 5.789,
     'L1_ffn_wr': 8.0,
     'L1_ffn_w1': 8.0,
     'L1_ffn_w2': 8.0}
    for name, (base, spread) in spreads.items():
        noise = np.random.default_rng([zlib.crc32(name.encode()), seed]).standard_normal(out[name].shape)
        drawn = base * np.exp(spread * noise) if base else spread * noise
        out[name] = jnp.asarray(drawn.astype(out[name].dtype))
    for name, factor in factors.items():
        out[name] = (out[name] * factor).astype(out[name].dtype)
    return out
```

```python
from contextlib import ExitStack

import numpy as np

import concourse.bass as bass
from concourse import mybir

ALU = mybir.AluOpType
ACT = mybir.ActivationFunctionType
AXX = mybir.AxisListType.X
F32 = mybir.dt.float32
BF16 = mybir.dt.bfloat16
U32 = mybir.dt.uint32
I32 = mybir.dt.int32

B = 32
NI, NT = 36, 77
N = NI + NT
C = 128
T = B * N
HP = 6
PS = 16
W = HP * PS
KT = 6
NH, HD = 8, 16
EPS = 1e-5

E0, GRP, F0 = 32, 4, 341
K0 = T // E0
Q0 = 4
LQ = T // Q0
R8 = -(-K0 // 8)
CQ = R8 * 8
F0C = [(0, 128), (128, 128), (256, F0 - 256)]

E1, F1 = 64, 512
CAP = 2 * (T * 2 // E1)
S1 = E1 * CAP
CAPT = [(0, 128), (128, CAP - 128)]
NJ = F1 // 128

FLOOR = 8388608.0
NUDGE = 1.0 + 2.0 ** -23
NEG = -1e30
SPLIT = 112

CONST = {}
_at = 0
for _name, _w in (("ident", 128), ("tri", N), ("ones", 128), ("causal", 4 * N), ("headmask", NH),
                  ("rope_c", 4 * N), ("rope_s", 4 * N), ("quarter", 1), ("expert", 1), ("iota", E1), ("regroup", NH * 4)):
    CONST[_name] = (_at, _w)
    _at += _w
NCONST = _at


def shape_constants():
    c = np.zeros((128, NCONST), np.float32)

    def put(name, value):
        a, w = CONST[name]
        value = np.asarray(value, np.float32)
        c[:value.shape[0], a:a + w] = value.reshape(value.shape[0], w)

    p = np.arange(128)
    put("ident", np.eye(128))
    put("tri", p[:N, None] < np.arange(N)[None, :])
    put("ones", np.ones((128, 128)))
    put("causal", np.tile(np.where(np.arange(N)[None, :] > p[:N, None], NEG, 0.0), (1, 4)))
    put("headmask", p[:, None] // HD == np.arange(NH)[None, :])
    put("quarter", (p // E0 * LQ)[:, None])
    put("expert", (p[:E0] * (Q0 * CQ))[:, None])
    put("iota", np.tile(np.arange(E1), (128, 1)))
    r = 8 * p[:N, None] + np.arange(NH)[None, :]
    put("regroup", (r // N % 4)[:, :, None] == np.arange(4)[None, None, :])
    t = np.arange(N, dtype=np.float64)
    rc, rs = np.zeros((128, 4, N)), np.zeros((128, 4, N))
    for blk in range(4):
        for j in range(4):
            h = (blk % 2) * 4 + j
            for d in range(HD):
                f, width = (h * HD + d, C) if blk < 2 else (h // 2 * HD + d, C // 2)
                theta = 10000.0 ** (-(2.0 * (np.float64(f // 2) - 1.0))) / width
                rc[32 * j + d, blk] = np.cos(t * theta)
                rs[32 * j + d, blk] = np.sin(t * theta) * (1.0 if f % 2 == 0 else -1.0)
    put("rope_c", rc)
    put("rope_s", rs)
    return c


def program(nc, ins, out, consts):
    ctx = ExitStack()
    with ctx:
        def sb(name, shape, dt=F32):
            t = ctx.enter_context(nc.sbuf_tensor(name, shape, dt))
            return t[(slice(None),) * len(shape)]

        def sem(name):
            return ctx.enter_context(nc.semaphore(name))

        def dram(name, shape, dt=F32):
            return nc.dram_tensor(name, shape, dt, kind="Internal").ap()

        d_cand = dram("d_cand", [E0 * Q0 * CQ, 1], I32)
        d_x0 = dram("d_x0", [T, C])
        d_y0 = [dram(f"d_y0_{i}", [T, C]) for i in range(2)]
        d_buf = dram("d_buf", [S1, C])
        d_y1 = dram("d_y1", [S1, C])

        cst = sb("cst", [128, NCONST])
        H = sb("H", [N, B, C])
        X = sb("X", [N, B, C])
        TMP = sb("TMP", [N, B, C])
        XT = sb("XT", [128, T])
        stat = sb("stat", [N, 8, B])
        identb = sb("identb", [128, 128], BF16)
        trib = sb("trib", [N, N], BF16)
        onesb = sb("onesb", [N, N], BF16)
        causalb = sb("causalb", [N, 4 * N], BF16)
        rows = sb("rows", [N, 5, C])
        rbias = sb("rbias", [N, E0])
        tokb = sb("tokb", [128, 1])
        gb = sb("gb", [128, 6])
        bnst = sb("bnst", [128, 8, 6])
        bnag = sb("bnag", [128, 8])
        wrt0 = sb("wrt0", [128, E0])
        wrt1 = sb("wrt1", [128, E1])
        wsplit = sb("wsplit", [128, 3, 4 * C], BF16)
        wres = sb("wres", [128, 2, 4 * C])
        arena = sb("arena", [128, 30000])

        def carve(at, words, dt=F32, parts=128):
            v = arena[0:parts, at:at + words]
            return v if dt == F32 else v.bitcast(dt)

        img = [carve(i * 4608, 4608, parts=96).rearrange("p (c h w) -> p c h w", c=3, w=W) for i in range(2)]
        wtok = carve(9216, 768)
        wtokT = carve(9984, 768).rearrange("p (k e) -> p k e", k=KT)
        wqkvp = carve(10752, 512).rearrange("p (j c) -> p j c", j=4)
        patT = carve(11264, KT * B * NI).rearrange("p (k t) -> p k t", k=KT)
        embT = carve(18176, B * NI)
        imgp = [carve(19400 + i * 4608, 4608, parts=96).rearrange("p (w r x) -> p w r x", w=HP, x=PS) for i in range(2)]
        rf = [carve(i * T, T) for i in range(2)]
        qkvb = carve(2 * T, 3 * T // 2, BF16).rearrange("p (j t) -> p j t", j=3)
        qm = carve(2 * T + 3 * T // 2, NH * T // 2, BF16).rearrange("p (h t) -> p h t", h=NH)
        at = 2 * T + 3 * T // 2 + NH * T // 2
        assert at + NH * N <= 30000
        aspk = carve(at, NH * N, BF16, N).rearrange("p (u x) -> p u x", u=2)
        xst = XT[:, 0:T // 2].bitcast(BF16)
        xsb = carve(2 * T + 3 * T // 2, B * C // 2, BF16, N).rearrange("p (b c) -> p b c", b=B)
        vtok = sb("vtok", [N, B, C], BF16)
        osb = xsb
        ost = carve(0, T // 2, BF16)
        sc = carve(0, LQ)
        cv = carve(1000, CQ)
        ci = carve(1200, CQ, U32)
        cif = carve(1400, CQ)
        cii = carve(1600, CQ, I32)
        vm = carve(1800, Q0 * CQ, parts=E0)
        gv = carve(2400, CQ, parts=E0)
        gp = carve(2600, CQ, U32, E0)
        gpf = carve(2800, CQ, parts=E0)
        lg = carve(3000, B * E0, parts=N).rearrange("p (b e) -> p b e", b=B)
        pr = carve(4100, B * E0, parts=N).rearrange("p (j q e) -> p j q e", q=Q0, e=E0)
        posi = carve(5200, E0, I32, N)
        gate = carve(5300, E0, parts=N)
        itok = carve(5400, E0, I32, N)
        wu0 = [carve(6000 + 400 * u, F0) for u in range(2)]
        bu0 = [carve(6800 + 400 * u, F0, parts=1) for u in range(2)]
        wd0 = [carve(7600 + 400 * u, 384).rearrange("p (k c) -> p k c", k=3) for u in range(2)]
        bd0 = [carve(8400 + 200 * u, C, parts=1) for u in range(2)]
        xg = [carve(8800 + 200 * u, C, parts=N) for u in range(2)]
        xgT = [carve(9200 + 200 * u, N) for u in range(2)]
        act0 = [carve(9600 + 400 * u, 3 * N).rearrange("p (k t) -> p k t", k=3) for u in range(2)]
        yo0 = [carve(10400 + 200 * u, C, parts=N) for u in range(2)]
        wpad = carve(0, 8 * C).rearrange("p (k x) -> p k x", k=8)
        rt = [carve(1024 + 904 * u, 8 * N).rearrange("p (s t) -> p s t", s=2) for u in range(2)]
        qs = [carve(2900 + 452 * u, 4 * N).rearrange("p (g t) -> p g t", g=4) for u in range(2)]
        s2 = [carve(3810 + 904 * u, NH * N, parts=N).rearrange("p (h t) -> p h t", h=NH) for u in range(2)]
        pr2 = [carve(5620 + 904 * u, NH * N, parts=N).rearrange("p (h t) -> p h t", h=NH) for u in range(2)]
        ptT = [carve(7430 + 904 * u, NH * N, parts=N).rearrange("p (h t) -> p h t", h=NH) for u in range(2)]
        nmx = carve(9240, NH, parts=N)
        rsum = carve(9260, NH, parts=N)
        rrec = carve(9280, NH, parts=N)
        mg = carve(9300, 32, parts=N).rearrange("p (k g) -> p k g", g=4)
        og = carve(9340, 512, parts=N).rearrange("p (k g d) -> p k g d", k=8, g=4)
        V = carve(10800, B * C, parts=N).rearrange("p (b c) -> p b c", b=B)
        QK = carve(15000, 4 * T).rearrange("p (k t) -> p k t", k=4)
        X1 = carve(15000, B * C, parts=N).rearrange("p (b c) -> p b c", b=B)
        wraw = carve(29464, 3 * C)
        wo = carve(29464 + 3 * C, C)
        lg1 = carve(0, B * E1, parts=N).rearrange("p (b e) -> p b e", b=B)
        pr1 = carve(2048, B * E1, parts=N).rearrange("p (b e) -> p b e", b=B)
        oh = [carve(4096 + 2048 * k, B * E1, parts=N).rearrange("p (b e) -> p b e", b=B) for k in range(2)]
        mb = carve(8192, B * E1 // 2, BF16, N).rearrange("p (b e) -> p b e", b=B)
        cumb = carve(9216, B * E1 // 2, BF16, N).rearrange("p (b e) -> p b e", b=B)
        mx8 = carve(10240, B * 8, parts=N).rearrange("p (b e) -> p b e", b=B)
        ix8 = carve(10496, B * 8, U32, N).rearrange("p (b e) -> p b e", b=B)
        ef = carve(10752, B * 8, parts=N).rearrange("p (b e) -> p b e", b=B)
        route = carve(11008, 8 * B, parts=N).rearrange("p (k b) -> p k b", k=8)
        sidx = carve(11264, 2 * B, I32, N).rearrange("p (k b) -> p k b", k=2)
        gidx = carve(11328, 2 * B, I32, N).rearrange("p (k b) -> p k b", k=2)
        gk = carve(11392, 2 * B, parts=N).rearrange("p (k b) -> p k b", k=2)
        w1 = [carve(11500 + 512 * u, F1) for u in range(2)]
        w2 = [carve(12524 + 512 * u, F1).rearrange("p (k c) -> p k c", k=NJ) for u in range(2)]
        b1 = [carve(13548 + 4 * u, NJ) for u in range(2)]
        b2 = [carve(13560 + C * u, C) for u in range(2)]
        xin = [carve(13816 + 256 * u, 2 * C).rearrange("p (k c) -> p k c", k=2) for u in range(2)]
        xinT = [carve(14328 + CAP * u, CAP) for u in range(2)]
        hT = [carve(14780 + 904 * u, NJ * CAP).rearrange("p (k t) -> p k t", k=NJ) for u in range(2)]
        yo1 = [carve(16588 + 256 * u, 2 * C).rearrange("p (k c) -> p k c", k=2) for u in range(2)]
        Y = [carve(17650 + 4096 * k, B * C, parts=N).rearrange("p (b c) -> p b c", b=B) for k in range(2)]
        X2 = carve(25860, B * C, parts=N).rearrange("p (b c) -> p b c", b=B)

        def const(name, parts=128):
            a, w = CONST[name]
            return cst[0:parts, a:a + w]

        ident = const("ident")
        ones1 = cst[0:1, CONST["ones"][0]:CONST["ones"][0] + 128]

        ps = ctx.enter_context(nc.psum_tensor("ps", [128, 8, 512], F32))

        def bank(i, parts=128):
            return ps[0:parts, i, :]

        names = """cst_in img_in img_packed wtok_in txt_in wqkv_in small_in rows_in zeroed buf_zeroed
            tile_ready tile_moved dve act emb_done ln_centred ln_squared ln_var ln_std
            spk_relu spk_ready qkv_ready qkv_stats qkv_std qkv_affine qkv_moved w_split
            qm_ready sT_ready a_ready o_ready o_moved ob_ready ost_ready proj_ready proj_added
            x0_ready x0_out h_out y0_zero lg_ready lg_sub lg_exp pr_ready scT_moved
            cand_ready cand_out vm_in gp_ready pos_ready itok_in gate_ready
            g_in0 g_in1 e_w0 e_w1 e_xT e_xTc e_up e_act e_down e_out e_sc0 e_sc1
            y0_in h2_ready consts_ready
            m_route m_lg m_max m_exp m_m m_cum m_sidx m_scat m_w0 m_w1 m_xT m_xTc m_up m_act m_down m_out
            m_st0 m_st1 m_gather fin_ready fin_out""".split()
        S = {n: sem(n) for n in names}
        A = {}
        for tag in ("r", "f"):
            for n in ("w_in", "wpad", "ones", "x_in", "qk_mm", "rope", "qk_c", "q_c", "sc", "sub", "exp", "pT", "pTc", "rec",
                      "o", "o_c", "w", "w_c", "dve"):
                A[tag + n] = sem(f"{tag}_{n}")

        class Chain:

            def __init__(self, eng, s):
                self.eng, self.s, self.n, self.at = eng, s, 0, 0

            def tick(self, ins):
                ins.then_inc(self.s, 1)
                self.n += 1
                return self.n

            def link(self, ins):
                self.tick(ins)
                self.eng.wait_ge(self.s, self.at + self.n)

        def loop(eng, total, head, tail, body, step=1):
            for i in range(head):
                body(i, i % 2)
            steps = (total - head - tail) // step
            assert steps * step == total - head - tail and head % step == 0
            with eng.Fori(0, steps) as r:
                for k in range(step):
                    body(r * step + (head + k), k % 2)
            for i in range(total - tail, total):
                body(i, i % 2)

        def known(i):
            return isinstance(i, int)

        def wait(eng, s, value):
            if not known(value) or value > 0:
                eng.wait_ge(s, value)

        tiles = []

        class Tiles:
            def __init__(self):
                self.n = 0

            def pe_open(self, pe):
                if self.n >= 4:
                    pe.wait_ge(S["tile_moved"], self.n - 3)
                return self.n % 4

            def pe_close(self, ins):
                ins.then_inc(S["tile_ready"], 1)
                self.n += 1

            def act_open(self, act):
                act.wait_ge(S["tile_ready"], self.n + 1)
                return self.n % 4

            def act_close(self, ins):
                ins.then_inc(S["tile_moved"], 1)
                self.n += 1

        def tile_counts():
            c, n = {}, 0
            for name, k in (("w", 3), ("pat", 24), ("emb", 4), ("H", 8), ("xs", 8), ("v", 8), ("os", 8),
                            ("xt0", 8), ("gT", 2), ("rx", 8), ("rv", 8), ("fx", 8), ("fv", 8), ("fo", 8), ("xt1", 8)):
                n += k
                c[name] = n
            return c

        moved = tile_counts()
        tok_rows = [(0, SPLIT), (SPLIT, N)]

        def bcol(ap2, width):
            return ap2.unsqueeze(2).broadcast_to([ap2.shape[0], ap2.shape[1], width])

        def brow(ap2, count):
            return ap2.unsqueeze(1).broadcast_to([ap2.shape[0], count, ap2.shape[1]])

        block = ctx.enter_context(nc.Block())

        @block.sync
        def _(sp):
            sp.dma_start(cst[:], consts).then_inc(S["cst_in"], 16)
            sp.dma_start(wtok, ins["L0_tok_w"]).then_inc(S["wtok_in"], 16)
            imgv = ins["x"].rearrange("b c (h p) w -> b h c (p w)", h=HP)
            for i in range(2):
                for h in range(HP):
                    sp.dma_start(img[i][h * 16:(h + 1) * 16].rearrange("p c h w -> p c (h w)"), imgv[16 * i:16 * i + 16, h])\
                        .then_inc(S["img_in"], 16)
            sp.dma_start(H[NI:N, :, :], ins["txt"].rearrange("b n c -> n b c")).then_inc(S["txt_in"], 16)
            sp.dma_start(wqkvp[:, 0:3, :], ins["L0_attn_Wqkv"].rearrange("(j d) c -> d j c", j=3)).then_inc(S["wqkv_in"], 16)
            sp.dma_start(wqkvp[:, 3, :], ins["L0_attn_Wproj"]).then_inc(S["wqkv_in"], 16)
            sp.dma_start(tokb[:], ins["L0_tok_b"].rearrange("(p o) -> p o", o=1)).then_inc(S["small_in"], 16)
            sp.dma_start(gb[:, 0:3], ins["L0_attn_gamma"].rearrange("(j p) -> p j", j=3), allow_slow_non_contiguous=True).then_inc(S["small_in"], 16)
            sp.dma_start(gb[:, 3:6], ins["L0_attn_beta"].rearrange("(j p) -> p j", j=3), allow_slow_non_contiguous=True).then_inc(S["small_in"], 16)
            sp.dma_start(wrt0[:], ins["L0_ffn_W_router"]).then_inc(S["small_in"], 16)
            sp.dma_start(wrt1[:], ins["L1_ffn_wr"]).then_inc(S["small_in"], 16)
            for i, nm in enumerate(("L0_attn_bproj", "L1_ffn_ln1_g", "L1_ffn_ln1_b", "L1_ffn_ln2_g", "L1_ffn_ln2_b")):
                sp.dma_start(rows[:, i, :], ins[nm].partition_broadcast(N)).then_inc(S["rows_in"], 16)
            sp.dma_start(rbias[:], ins["L0_ffn_b_router"].partition_broadcast(N)).then_inc(S["rows_in"], 16)
            sp.wait_ge(S["zeroed"], 1)
            for i in range(4):
                sp.dma_start(d_buf.rearrange("s c -> (s c)").rearrange("(p x) -> p x", p=128)[:, i * T:(i + 1) * T], XT[:]).then_inc(S["buf_zeroed"], 16)
            sp.dma_start(d_y0[1].rearrange("s c -> (s c)").rearrange("(p x) -> p x", p=128), XT[:]).then_inc(S["y0_zero"], 16)
            sp.wait_ge(S["x0_ready"], 1)
            for a, z in tok_rows:
                sp.dma_start(d_x0.rearrange("(b n) c -> n b c", n=N)[a:z], X[a:z]).then_inc(S["x0_out"], 16)
                sp.dma_start(d_y0[0].rearrange("(b n) c -> n b c", n=N)[a:z], H[a:z]).then_inc(S["h_out"], 16)
            sp.wait_ge(S["cand_ready"], 1)
            for q in range(Q0):
                sp.dma_start(d_cand.rearrange("(e q r) o -> q e (r o)", e=E0, q=Q0)[q], cii[q * E0:(q + 1) * E0, :])\
                    .then_inc(S["cand_out"], 16)
                sp.dma_start(vm[:, q * CQ:(q + 1) * CQ], cv[q * E0:(q + 1) * E0, :]).then_inc(S["vm_in"], 16)

            for e in range(E0):
                u = e % 2
                if e >= 2:
                    sp.wait_ge(S["e_down"], e - 1)
                g = e // GRP
                sp.dma_start(wu0[u], ins["L0_ffn_W_up"][g]).then_inc(S[f"e_w{u}"], 16)
                sp.dma_start(bu0[u], ins["L0_ffn_b_up"][g:g + 1, :]).then_inc(S[f"e_w{u}"], 16)
                sp.dma_start(wd0[u][:, 0:2, :], ins["L0_ffn_W_down"][e, 0:256, :].rearrange("(k p) c -> p k c", k=2))\
                    .then_inc(S[f"e_w{u}"], 16)
                sp.dma_start(wd0[u][0:F0 - 256, 2, :], ins["L0_ffn_W_down"][e, 256:F0, :]).then_inc(S[f"e_w{u}"], 16)
                sp.dma_start(bd0[u], ins["L0_ffn_b_down"][e:e + 1, :]).then_inc(S[f"e_w{u}"], 16)
            sp.wait_ge(S["e_sc0"], 16 * (E0 // 2))
            sp.wait_ge(S["e_sc1"], 16 * (E0 // 2))
            for a, z in tok_rows:
                sp.dma_start(H[a:z], d_y0[0].rearrange("(b n) c -> n b c", n=N)[a:z]).then_inc(S["y0_in"], 16)
                sp.dma_start(TMP[a:z], d_y0[1].rearrange("(b n) c -> n b c", n=N)[a:z]).then_inc(S["y0_in"], 16)

            sp.dma_start(wraw[:, 0:128], ins["L1_attn_Wq"]).then_inc(A["rw_in"], 16)
            sp.dma_start(wraw[:, 128:192], ins["L1_attn_Wk"]).then_inc(A["rw_in"], 16)
            sp.dma_start(wraw[:, 256:320], ins["L1_attn_Wv"]).then_inc(A["rw_in"], 16)
            sp.wait_ge(A["rqk_mm"], 32)
            for i, nm in enumerate(("L1_ffn_wq", "L1_ffn_wk", "L1_ffn_wv")):
                sp.dma_start(wraw[:, i * 128:(i + 1) * 128], ins[nm]).then_inc(A["fw_in"], 16)
            sp.dma_start(wo, ins["L1_ffn_wo"]).then_inc(A["fw_in"], 16)

            def e1_io(e, u):
                wait(sp, S["m_out"], e - 1)
                if not (known(e) and e < 2):
                    for k, (a, n) in enumerate(CAPT):
                        sp.dma_start(d_y1[bass.ds((e - 2) * CAP + a, n), :], yo1[u][0:n, k, :]).then_inc(S[f"m_st{u}"], 16)
                if known(e) and e >= E1:
                    return
                w1v = ins["L1_ffn_w1"].rearrange("e c f -> (e c) f")
                w2v = ins["L1_ffn_w2"].rearrange("e (p k) c -> (e p) (k c)", k=NJ)
                b1v = ins["L1_ffn_b1"].rearrange("e (p k) -> (e p) k", k=NJ)
                sp.dma_start(w1[u], w1v[bass.ds(e * 128, 128), :]).then_inc(S[f"m_w{u}"], 16)
                sp.dma_start(w2[u].rearrange("p k c -> p (k c)"), w2v[bass.ds(e * 128, 128), :]).then_inc(S[f"m_w{u}"], 16)
                sp.dma_start(b1[u], b1v[bass.ds(e * 128, 128), :]).then_inc(S[f"m_w{u}"], 16)
                sp.dma_start(b2[u], ins["L1_ffn_b2"][bass.ds(e, 1), :].broadcast_to([128, C])).then_inc(S[f"m_w{u}"], 16)
                for k, (a, n) in enumerate(CAPT):
                    sp.dma_start(xin[u][0:n, k, :], d_buf[bass.ds(e * CAP + a, n), :]).then_inc(S[f"m_w{u}"], 16)

            sp.wait_ge(S["m_scat"], 16 * 2 * B)
            loop(sp, E1 + 2, 2, 2, e1_io, step=2)
            sp.wait_ge(S["fin_ready"], 1)
            for a, z in tok_rows:
                sp.dma_start(out.rearrange("b n c -> n b c")[a:z], X[a:z]).then_inc(S["fin_out"], 16)
            sp.wait_ge(S["fin_out"], 32)

        @block.tensor
        def _(pe):
            tl = Tiles()
            pe.wait_ge(S["cst_in"], 16)
            pe.wait_ge(S["wtok_in"], 16)
            for g in range(2):
                k0 = tl.pe_open(pe)
                for k in range(3):
                    ins_ = pe.transpose(bank(k0)[:, k * 128:(k + 1) * 128], wtok[:, (3 * g + k) * 128:(3 * g + k + 1) * 128], ident)
                tl.pe_close(ins_)
            pe.wait_ge(S["wqkv_in"], 32)
            k0 = tl.pe_open(pe)
            for j in range(4):
                ins_ = pe.transpose(bank(k0)[:, j * 128:(j + 1) * 128], wqkvp[:, j, :], ident)
            tl.pe_close(ins_)
            for t in range(2):
                pe.wait_ge(S["img_packed"], t + 1)
                for k in range(KT):
                    for half in range(2):
                        k0 = tl.pe_open(pe)
                        for w in range(3):
                            wp = half * 3 + w
                            src = imgp[t][:, wp, k * 8:(k + 1) * 8, :].rearrange("p r x -> p (r x)")
                            ins_ = pe.transpose(bank(k0)[:, w * 96:(w + 1) * 96], src, ident[0:96, 0:96])
                        tl.pe_close(ins_)
            pe.wait_ge(S["tile_moved"], moved["pat"])
            for g in range(4):
                k0 = tl.pe_open(pe)
                for k in range(KT):
                    ins_ = pe.matmul(bank(k0)[:, 0:288], wtokT[:, k, :], patT[:, k, g * 288:(g + 1) * 288],
                                     start=(k == 0), stop=(k == KT - 1))
                tl.pe_close(ins_)
            pe.wait_ge(S["tile_moved"], moved["emb"])
            for g in range(8):
                k0 = tl.pe_open(pe)
                for k in range(4):
                    b = 4 * g + k
                    ins_ = pe.transpose(bank(k0)[0:NI, k * 128:(k + 1) * 128], embT[:, b * NI:(b + 1) * NI], ident)
                tl.pe_close(ins_)

            def turn(src, dt, idm, ready=None):
                for g in range(8):
                    k0 = tl.pe_open(pe)
                    o = bank(k0) if dt == F32 else bank(k0).bitcast(BF16)
                    for k in range(4):
                        stride = N if dt == F32 else N + 1
                        x = pe.transpose(o[:, k * stride:k * stride + N], src[:, 4 * g + k, :], idm)
                    tl.pe_close(x)

            pe.wait_ge(S["spk_ready"], 1)
            pe.wait_ge(S["consts_ready"], 1)
            turn(xsb, BF16, identb[0:N, 0:N])
            pe.wait_ge(S["w_split"], 1)
            pe.wait_ge(S["tile_moved"], moved["xs"])
            for j in range(3):
                for c in range(8):
                    if j:
                        pe.wait_ge(S["qkv_moved"], 8 * (j - 1) + c + 1)
                    for p in range(3):
                        x = pe.matmul(bank(c)[:, 0:4 * N], wsplit[:, p, j * C:(j + 1) * C], xst[:, c * 4 * N:(c + 1) * 4 * N],
                                      start=(p == 0), stop=(p == 2))
                    x.then_inc(S["qkv_ready"], 1)
            pe.wait_ge(S["qkv_moved"], 24)
            pe.wait_ge(S["qm_ready"], 3)
            for g in range(8):
                k0 = tl.pe_open(pe)
                for k in range(4):
                    b = 4 * g + k
                    x = pe.transpose(bank(k0, N).bitcast(BF16)[:, k * 128:(k + 1) * 128], qkvb[:, 2, b * N:(b + 1) * N], identb)
                tl.pe_close(x)
            pe.wait_ge(S["tile_moved"], moved["v"])
            pe.wait_ge(S["qm_ready"], 4)

            def spk_scores(b, u):
                for g in range(2):
                    x = pe.matmul(bank(2 * u + g, N)[:, 0:4 * N], qkvb[:, 1, bass.ds(b * N, N)],
                                  qm[:, 4 * g:4 * g + 4, bass.ds(b * N, N)], start=True, stop=True)
                x.then_inc(S["sT_ready"], 1)

            def spk_step(b, u):
                if not (known(b) and b == B - 1):
                    wait(pe, S["a_ready"], b)
                    spk_scores(b + 1, 1 - u)
                pe.wait_ge(S["a_ready"], b + 1)
                wait(pe, S["o_moved"], b - 1)
                for h in range(NH):
                    x = pe.matmul(bank(4 + u, N)[:, h * HD:(h + 1) * HD], aspk[:, u, h * N:(h + 1) * N],
                                  vtok[:, bass.ds(b, 1), h * HD:(h + 1) * HD], start=True, stop=True)
                x.then_inc(S["o_ready"], 1)

            spk_scores(0, 0)
            loop(pe, B, 2, 2, spk_step, step=2)
            pe.wait_ge(S["ob_ready"], 1)
            turn(osb, BF16, identb[0:N, 0:N])
            pe.wait_ge(S["tile_moved"], moved["os"])
            for g in range(8):
                if g >= 4:
                    pe.wait_ge(S["proj_added"], g - 3)
                for k in range(4):
                    b = 4 * g + k
                    for p in range(3):
                        x = pe.matmul(bank(4 + g % 4, N)[:, k * C:(k + 1) * C], ost[:, b * N:(b + 1) * N],
                                      wsplit[:, p, 3 * C:4 * C], start=(p == 0), stop=(p == 2))
                x.then_inc(S["proj_ready"], 1)

            pe.wait_ge(S["x0_ready"], 1)
            pe.wait_ge(S["y0_zero"], 16)
            pe.wait_ge(S["buf_zeroed"], 64)
            turn(X, F32, ident[0:N, 0:N])
            pe.wait_ge(S["tile_moved"], moved["xt0"])
            for b in range(B):
                x = pe.matmul(bank(4 + b // 16, N)[:, (b % 16) * E0:(b % 16 + 1) * E0], XT[:, b * N:(b + 1) * N], wrt0[:],
                              start=True, stop=True)
            x.then_inc(S["lg_ready"], 1)
            pe.wait_ge(S["pr_ready"], 1)
            for j in range(B // Q0):
                x = pe.transpose(bank(6 + j // 4)[:, (j % 4) * N:(j % 4 + 1) * N],
                                 pr[:, j].rearrange("p q e -> p (q e)"), ident[0:N, 0:N])
            x.then_inc(S["lg_ready"], 1)
            pe.wait_ge(S["gp_ready"], 1)
            for src in (gpf, gv):
                k0 = tl.pe_open(pe)
                tl.pe_close(pe.transpose(bank(k0, K0)[:, 0:E0], src[:, 0:K0], ident[0:E0, 0:E0]))

            def e0_up(e):
                u = e % 2
                pe.wait_ge(S[f"g_in{u}"], 16 * (e // 2 + 1))
                if e >= 2:
                    pe.wait_ge(S["e_xTc"], e - 1)
                pe.transpose(bank(u)[:, 0:K0], xg[u], ident[0:K0, 0:K0]).then_inc(S["e_xT"], 1)
                pe.wait_ge(S[f"e_w{u}"], 80 * (e // 2 + 1))
                pe.wait_ge(S["e_xTc"], e + 1)
                if e >= 2:
                    pe.wait_ge(S["e_act"], 2 * (e - 1))
                for k, (a, n) in enumerate(F0C):
                    o = bank(2 + u, n)[:, k * K0:(k + 1) * K0]
                    pe.matmul(o, wu0[u][:, a:a + n], xgT[u], start=True, stop=False)
                    x = pe.matmul(o, bu0[u][:, a:a + n], ones1[:, 0:K0], start=False, stop=True)
                x.then_inc(S["e_up"], 1)

            def e0_down(e):
                u = e % 2
                pe.wait_ge(S["e_act"], 2 * (e + 1))
                if e >= 2:
                    pe.wait_ge(S["e_out"], e - 1)
                o = bank(4 + u, K0)[:, 0:C]
                for k, (a, n) in enumerate(F0C):
                    pe.matmul(o, act0[u][0:n, k, :], wd0[u][0:n, k, :], start=(k == 0), stop=False)
                pe.matmul(o, ones1[:, 0:K0], bd0[u], start=False, stop=True).then_inc(S["e_down"], 1)

            pe.wait_ge(S["tile_moved"], moved["gT"])
            e0_up(0)
            for e in range(E0):
                if e + 1 < E0:
                    e0_up(e + 1)
                e0_down(e)
            pe.wait_ge(S["e_out"], E0)

            def attention(tag, rope):
                a = lambda n: A[tag + n]
                nv = C // 2 if rope else C
                pe.wait_ge(a("x_in"), 1)
                turn(X if rope else X1, F32, ident[0:N, 0:N])
                pe.wait_ge(S["tile_moved"], moved[tag + "x"])
                pe.wait_ge(a("w_in"), 48 if rope else 64)
                for g in range(8):
                    k0 = tl.pe_open(pe)
                    for k in range(4):
                        b = 4 * g + k
                        x = pe.matmul(bank(k0, N)[:, k * nv:(k + 1) * nv], XT[:, b * N:(b + 1) * N],
                                      wraw[:, 2 * C:2 * C + nv], start=True, stop=True)
                    tl.pe_close(x)
                pe.wait_ge(a("wpad"), 19 if rope else 4)
                for c in range(8):
                    for k in range(4):
                        n = 4 * c + k
                        if n >= 2:
                            pe.wait_ge(a("rope") if rope else a("qk_c"), n - 1)
                        xc = XT[:, c * 4 * N:(c + 1) * 4 * N]
                        x = pe.matmul(bank(4 + 2 * (n % 2))[:, 0:4 * N], wpad[:, k, :], xc, start=True, stop=True)
                        if rope:
                            x = pe.matmul(bank(5 + 2 * (n % 2))[:, 0:4 * N], wpad[:, 4 + k, :], xc, start=True, stop=True)
                        x.then_inc(a("qk_mm"), 1)

                def scores(b, u):
                    pe.wait_ge(a("q_c"), b + 1)
                    wait(pe, a("sub"), b)
                    if rope:
                        for j in range(4):
                            pe.matmul(bank(4 + j, N)[:, 0:2 * N], identb[0:N, 0:N], causalb[:, 0:2 * N], start=True, stop=True)
                    for g in range(2):
                        for j in range(4):
                            x = pe.matmul(bank(4 + j, N)[:, g * N:(g + 1) * N], qs[u][32 * j:32 * j + 32, g, :],
                                          qs[u][32 * j:32 * j + 32, 2 + g, :], start=not rope, stop=True,
                                          skip_group_check=True)
                    x.then_inc(a("sc"), 1)

                def step(b, u):
                    if not (known(b) and b >= B - 1):
                        scores(b + 1, 1 - u)
                    pe.wait_ge(a("exp"), b + 1)
                    wait(pe, a("pTc"), b)
                    for i in range(NH):
                        h = 4 * (i % 2) + i // 2
                        o = 4 * (h % 2) + h // 2 if rope else h
                        x = pe.transpose(bank(2 + o // 4, N)[:, (o % 4) * N:(o % 4 + 1) * N], pr2[u][:, i, :], ident[0:N, 0:N])
                    x.then_inc(a("pT"), 1)
                    pe.wait_ge(a("pTc"), b + 1)
                    if rope:
                        wait(pe, a("o_c"), b)
                        rows8 = ptT[u].rearrange("p h t -> p (h t)").rearrange("p (n k) -> p k n", k=8)
                        for k in range(8):
                            x = pe.matmul(bank(k // 4, N)[:, (k % 4) * 128:(k % 4) * 128 + 65], rows8[:, k, :],
                                          V[:, bass.ds(b, 1), 0:65], start=True, stop=True)
                    else:
                        wait(pe, a("o_c"), b - 1)
                        for h in range(NH):
                            x = pe.matmul(bank(u, N)[:, h * HD:(h + 1) * HD], ptT[u][:, h, :],
                                          V[:, bass.ds(b, 1), h * HD:(h + 1) * HD], start=True, stop=True)
                    x.then_inc(a("o"), 1)

                pe.wait_ge(a("qk_c"), 32)
                pe.wait_ge(S["tile_moved"], moved[tag + "v"])
                if rope:
                    pe.wait_ge(a("ones"), 1)
                scores(0, 0)
                loop(pe, B, 2, 2, step, step=2)
                if not rope:
                    pe.wait_ge(a("o_c"), B)
                    turn(TMP, F32, ident[0:N, 0:N])
                    pe.wait_ge(S["tile_moved"], moved[tag + "o"])
                    for g in range(8):
                        if g >= 4:
                            pe.wait_ge(a("w_c"), g - 3)
                        for k in range(4):
                            b = 4 * g + k
                            x = pe.matmul(bank(4 + g % 4, N)[:, k * C:(k + 1) * C], XT[:, b * N:(b + 1) * N], wo, start=True, stop=True)
                        x.then_inc(a("w"), 1)

            attention("r", True)
            attention("f", False)

            pe.wait_ge(S["m_route"], 1)
            turn(X2, F32, ident[0:N, 0:N])
            pe.wait_ge(S["tile_moved"], moved["xt1"])
            for b in range(B):
                x = pe.matmul(bank(4 + b // 8, N)[:, (b % 8) * E1:(b % 8 + 1) * E1], XT[:, b * N:(b + 1) * N], wrt1[:],
                              start=True, stop=True)
            x.then_inc(S["m_lg"], 1)
            pe.wait_ge(S["m_m"], 1)
            for c in range(4):
                pe.matmul(bank(4 + c, N), trib[:], mb[:, 8 * c:8 * c + 8, :], start=True, stop=False)
                x = pe.matmul(bank(4 + c, N), onesb[:], cumb[:, 8 * c:8 * c + 8, :], start=False, stop=True)
            x.then_inc(S["m_cum"], 1)

            def e1_up(e, u, i):
                pe.wait_ge(S[f"m_w{u}"], 96 * (i + 1))
                wait(pe, S["m_xTc"], e - 1)
                for k, (a, n) in enumerate(CAPT):
                    x = pe.transpose(bank(u)[:, a:a + n], xin[u][0:n, k, :], ident[0:n, 0:n])
                x.then_inc(S["m_xT"], 1)
                pe.wait_ge(S["m_xTc"], e + 1)
                wait(pe, S["m_act"], (e - 1) * NJ)
                w1v = w1[u].rearrange("p (f k) -> p k f", k=NJ)
                for k in range(NJ):
                    x = pe.matmul(bank(2 + 2 * u + k // 2)[:, (k % 2) * CAP:(k % 2 + 1) * CAP], w1v[:, k, :], xinT[u],
                                  start=True, stop=True)
                x.then_inc(S["m_up"], 1)

            def e1_step(e, u):
                i = e // 2 if known(e) else None
                if known(e):
                    if e + 1 < E1:
                        e1_up(e + 1, 1 - u, (e + 1) // 2)
                else:
                    e1_up(e + 1, 1 - u, rr[0] + (1 if u == 0 else 2))
                pe.wait_ge(S["m_act"], (e + 1) * NJ)
                wait(pe, S["m_out"], e - 1)
                for k, (a, n) in enumerate(CAPT):
                    for j in range(NJ):
                        x = pe.matmul(bank(6 + u, n)[:, k * C:(k + 1) * C], hT[u][:, j, a:a + n], w2[u][:, j, :],
                                      start=(j == 0), stop=(j == NJ - 1))
                x.then_inc(S["m_down"], 1)

            rr = [None]
            pe.wait_ge(S["m_sidx"], 1)
            e1_up(0, 0, 0)
            e1_step(0, 0)
            e1_step(1, 1)
            with pe.Fori(0, E1 // 2 - 2) as r:
                rr[0] = r
                e1_step(r * 2 + 2, 0)
                e1_step(r * 2 + 3, 1)
            e1_step(E1 - 2, 0)
            e1_step(E1 - 1, 1)

        @block.scalar
        def _(act):
            tl = Tiles()
            copy = lambda o, i: act.activation(o, i, ACT.Copy)
            act.wait_ge(S["small_in"], 80)
            for g in range(2):
                k0 = tl.act_open(act)
                tl.act_close(copy(wtokT[:, 3 * g:3 * g + 3, :], bank(k0)[:, 0:384].rearrange("p (k e) -> p k e", k=3)))
            k0 = tl.act_open(act)
            tl.act_close(copy(wres[:, 0, :], bank(k0)))
            for t in range(2):
                for k in range(KT):
                    for half in range(2):
                        k0 = tl.act_open(act)
                        at_ = t * 576 + half * 288
                        tl.act_close(copy(patT[:, k, at_:at_ + 288], bank(k0)[:, 0:288]))
            ev = embT.rearrange("p (t b h w) -> p t w h b", t=2, w=HP, h=HP)
            for g in range(4):
                k0 = tl.act_open(act)
                t, half = g // 2, g % 2
                tl.act_close(act.activation(ev[:, t, 3 * half:3 * half + 3],
                                            bank(k0)[:, 0:288].rearrange("p (w h b) -> p w h b", w=3, h=HP),
                                            ACT.Identity, bias=tokb[:, 0:1]))
            for g in range(8):
                k0 = tl.act_open(act)
                tl.act_close(copy(H[0:NI, 4 * g:4 * g + 4, :], bank(k0, NI).rearrange("p (k c) -> p k c", k=4)))

            lnn = [0]

            def ln_help():
                lnn[0] += 1
                act.wait_ge(S["ln_centred"], lnn[0])
                act.activation(TMP[:], lnsrc[0], ACT.Square).then_inc(S["ln_squared"], 1)
                act.wait_ge(S["ln_var"], lnn[0])
                act.activation(stat[:, 3, :], stat[:, 2, :], ACT.Sqrt).then_inc(S["ln_std"], 1)

            lnsrc = [X[:]]
            ln_help()
            act.wait_ge(S["spk_relu"], 1)
            act.activation(TMP[:], X[:], ACT.Relu, scale=NUDGE).then_inc(S["act"], 1)

            def untile(dst):
                for g in range(8):
                    k0 = tl.act_open(act)
                    if dst.dtype == BF16:
                        src = bank(k0).bitcast(BF16)[:, 0:4 * (N + 1)].rearrange("p (k t) -> p k t", k=4)[:, :, 0:N]
                        o = dst[:, 4 * g * N:(4 * g + 4) * N].rearrange("p (k t) -> p k t", k=4)
                    else:
                        src, o = bank(k0)[:, 0:4 * N], dst[:, 4 * g * N:(4 * g + 4) * N]
                    tl.act_close(copy(o, src))

            act.wait_ge(S["buf_zeroed"], 64)
            act.wait_ge(S["y0_zero"], 16)
            untile(xst)
            for j in range(3):
                act.wait_ge(S["qkv_stats"], 2 * j + 1)
                act.activation(bnag[:, 3:4], bnag[:, 2:3], ACT.Sqrt).then_inc(S["qkv_std"], 1)
                act.wait_ge(S["qkv_stats"], 2 * j + 2)
                if j == 2:
                    act.wait_ge(S["qm_ready"], 1)
                for c in range(8):
                    act.activation(rf[j % 2][:, c * 4 * N:(c + 1) * 4 * N], bank(c)[:, 0:4 * N], ACT.Relu,
                                   bias=bnag[:, 6:7], scale=bnag[:, 5:6]).then_inc(S["qkv_moved"], 1)
            for g in range(8):
                k0 = tl.act_open(act)
                tl.act_close(copy(vtok[:, 4 * g:4 * g + 4, :],
                                  bank(k0, N).bitcast(BF16)[:, 0:512].rearrange("p (k c) -> p k c", k=4)))

            def spk_out(b, u):
                act.wait_ge(S["o_ready"], b + 1)
                act.activation(TMP[:, bass.ds(b, 1), :], bank(4 + u, N)[:, 0:C].unsqueeze(1), ACT.Relu,
                               scale=NUDGE * float(HD) ** -0.5).then_inc(S["o_moved"], 1)

            loop(act, B, 2, 2, spk_out, step=2)
            untile(ost)

            ln_help()
            untile(XT[:])
            act.wait_ge(S["lg_sub"], 1)
            act.activation(lg, lg, ACT.Exp).then_inc(S["lg_exp"], 1)
            k0 = tl.act_open(act)
            tl.act_close(copy(posi, bank(k0, K0)[:, 0:E0]))
            k0 = tl.act_open(act)
            tl.act_close(copy(gate, bank(k0, K0)[:, 0:E0]))
            for e in range(E0):
                u = e % 2
                act.wait_ge(S["e_up"], e + 1)
                if e >= 2:
                    act.wait_ge(S["e_down"], e - 1)
                act.activation(act0[u][:, 0:2, :], bank(2 + u)[:, 0:2 * K0].rearrange("p (k t) -> p k t", k=2), ACT.Silu)\
                    .then_inc(S["e_act"], 1)
                n = F0C[2][1]
                act.activation(act0[u][0:n, 2, :], bank(2 + u, n)[:, 2 * K0:3 * K0], ACT.Silu).then_inc(S["e_act"], 1)

            ln_help()

            def attention(tag, rope):
                a = lambda n: A[tag + n]
                nv = C // 2 if rope else C
                untile(XT)
                for g in range(8):
                    k0 = tl.act_open(act)
                    tl.act_close(copy(V[:, 4 * g:4 * g + 4, 0:nv], bank(k0, N)[:, 0:4 * nv].rearrange("p (k c) -> p k c", k=4)))
                if not rope:
                    for n in range(32):
                        act.wait_ge(a("qk_mm"), n + 1)
                        copy(QK[:, n % 4, (n // 4) * 4 * N:(n // 4 + 1) * 4 * N], bank(4 + 2 * (n % 2))[:, 0:4 * N])\
                            .then_inc(a("qk_c"), 1)

                def step(b, u):
                    act.wait_ge(a("sub"), b + 1)
                    wait(act, a("pT"), b - 1)
                    if not rope:
                        wait(act, a("rec"), b - 1)
                    act.activation(pr2[u], s2[u], ACT.Exp, scale=float(HD) ** -0.5).then_inc(a("exp"), 1)
                    act.wait_ge(a("pT"), b + 1)
                    wait(act, a("o"), b - 1)
                    copy(ptT[u].rearrange("p (a i) t -> p a (i t)", a=2), ps[0:N, 2:4, 0:4 * N]).then_inc(a("pTc"), 1)

                loop(act, B, 2, 2, step, step=2)
                if not rope:
                    untile(XT)

            attention("r", True)
            ln_help()
            lnsrc[0] = X1
            ln_help()
            attention("f", False)
            lnsrc[0] = X2
            ln_help()
            untile(XT[:])
            act.wait_ge(S["m_max"], 1)
            act.activation(lg1, lg1, ACT.Exp).then_inc(S["m_exp"], 1)

            def e1_gelu(e, u):
                act.wait_ge(S["m_up"], e + 1)
                wait(act, S["m_down"], e - 1)
                for k in range(NJ):
                    act.activation(hT[u][:, k, :], bank(2 + 2 * u + k // 2)[:, (k % 2) * CAP:(k % 2 + 1) * CAP],
                                   ACT.Gelu_apprx_tanh, bias=b1[u][:, k:k + 1]).then_inc(S["m_act"], 1)

            loop(act, E1, 2, 2, e1_gelu, step=2)

        @block.vector
        def _(dve):
            ch = Chain(dve, S["dve"])
            link = ch.link
            tt, ts, stt = dve.tensor_tensor, dve.tensor_scalar, dve.scalar_tensor_tensor

            dve.memset(XT[:], 0.0).then_inc(S["zeroed"], 1)
            dve.wait_ge(S["cst_in"], 16)
            link(dve.tensor_copy(identb[:], ident))
            link(dve.tensor_copy(trib[:], const("tri", N)))
            link(dve.tensor_copy(onesb[:], const("ones", N)[:, 0:N]))
            dve.tensor_copy(causalb[:], const("causal", N)).then_inc(S["consts_ready"], 1)

            dve.wait_ge(S["img_in"], 16 * 12)
            for t in range(2):
                dve.tensor_copy(imgp[t].rearrange("p w r x -> p r w x"),
                                img[t].rearrange("p c h (w x) -> p (c h) w x", x=PS)).then_inc(S["img_packed"], 1)

            dve.wait_ge(S["tile_moved"], moved["w"])
            link(dve.tensor_copy(wsplit[:, 0, :], wres[:, 0, :]))
            link(tt(wres[:, 1, :], wres[:, 0, :], wsplit[:, 0, :], ALU.subtract))
            link(dve.tensor_copy(wsplit[:, 1, :], wres[:, 1, :]))
            link(tt(wres[:, 0, :], wres[:, 1, :], wsplit[:, 1, :], ALU.subtract))
            dve.tensor_copy(wsplit[:, 2, :], wres[:, 0, :]).then_inc(S["w_split"], 1)

            lnn = [0]

            def layernorm(src, dst, gain=None):
                link(dve.tensor_reduce(stat[:, 0, :], src, AXX, ALU.add))
                link(ts(stat[:, 1, :], stat[:, 0, :], 1.0 / C, None, ALU.mult))
                tt(dst, src, bcol(stat[:, 1, :], C), ALU.subtract).then_inc(S["ln_centred"], 1)
                lnn[0] += 1
                dve.wait_ge(S["ln_squared"], lnn[0])
                link(dve.tensor_reduce(stat[:, 4, :], TMP[:], AXX, ALU.add))
                ts(stat[:, 2, :], stat[:, 4, :], 1.0 / C, EPS, ALU.mult, ALU.add).then_inc(S["ln_var"], 1)
                dve.wait_ge(S["ln_std"], lnn[0])
                link(dve.reciprocal(stat[:, 5, :], stat[:, 3, :]))
                dve.wait_ge(S["ln_centred"], lnn[0])
                last = tt(dst, dst, bcol(stat[:, 5, :], C), ALU.mult)
                if gain is not None:
                    link(last)
                    link(tt(dst, dst, brow(rows[:, gain, :], B), ALU.mult))
                    last = tt(dst, dst, brow(rows[:, gain + 1, :], B), ALU.add)
                return last

            dve.wait_ge(S["tile_moved"], moved["H"])
            dve.wait_ge(S["txt_in"], 16)
            layernorm(H[:], X[:]).then_inc(S["spk_relu"], 1)
            dve.wait_ge(S["act"], 1)

            def spikes(dst, src):
                link(ts(src, src, 4.0, FLOOR, ALU.min, ALU.add))
                return ts(dst, src, FLOOR, None, ALU.subtract)

            spikes(xsb, TMP[:]).then_inc(S["spk_ready"], 1)
            dve.wait_ge(S["small_in"], 80)
            for j in range(3):
                for c in range(8):
                    dve.wait_ge(S["qkv_ready"], 8 * j + c + 1)
                    link(dve.bn_stats(bnst[:, c, :], bank(c)[:, 0:4 * N]))
                if j:
                    dve.wait_ge(S["qkv_moved"], 8 * j)
                link(dve.bn_aggr(bnag[:, 0:2], bnst[:].rearrange("p a b -> p (a b)")))
                ts(bnag[:, 2:3], bnag[:, 1:2], EPS, None, ALU.add).then_inc(S["qkv_stats"], 1)
                dve.wait_ge(S["qkv_std"], j + 1)
                link(dve.reciprocal(bnag[:, 4:5], bnag[:, 3:4]))
                link(ts(bnag[:, 5:6], bnag[:, 4:5], gb[:, j:j + 1], NUDGE, ALU.mult, ALU.mult))
                link(tt(bnag[:, 7:8], bnag[:, 0:1], bnag[:, 5:6], ALU.mult))
                stt(out=bnag[:, 6:7], in0=gb[:, 3 + j:4 + j], scalar=NUDGE, in1=bnag[:, 7:8],
                    op0=ALU.mult, op1=ALU.subtract).then_inc(S["qkv_stats"], 1)
                if j:
                    spikes(qkvb[:, j - 1, :], rf[(j - 1) % 2]).then_inc(S["qm_ready"], 1)
            dve.wait_ge(S["qkv_moved"], 24)
            spikes(qkvb[:, 2, :], rf[0]).then_inc(S["qm_ready"], 1)
            dve.wait_ge(S["tile_moved"], moved["xs"])
            dve.wait_ge(S["qm_ready"], 3)
            for h in range(NH):
                a_ = CONST["headmask"][0] + h
                last = ts(qm[:, h, :], qkvb[:, 0, :], cst[:, a_:a_ + 1], None, ALU.mult)
            last.then_inc(S["qm_ready"], 1)

            def spk_a(b, u):
                dve.wait_ge(S["sT_ready"], b + 1)
                wait(dve, S["o_ready"], b - 1)
                ts(aspk[:, u, :].rearrange("p (g x) -> p g x", g=2), ps[0:N, 2 * u:2 * u + 2, 0:4 * N],
                   4.0, None, ALU.min).then_inc(S["a_ready"], 1)

            loop(dve, B, 2, 2, spk_a, step=2)
            dve.wait_ge(S["o_moved"], B)
            spikes(osb, TMP[:]).then_inc(S["ob_ready"], 1)
            dve.wait_ge(S["rows_in"], 96)
            link(tt(H[:], H[:], brow(rows[:, 0, :], B), ALU.add))
            for g in range(8):
                dve.wait_ge(S["proj_ready"], g + 1)
                tt(H[:, 4 * g:4 * g + 4, :], H[:, 4 * g:4 * g + 4, :],
                   bank(4 + g % 4, N).rearrange("p (k c) -> p k c", k=4), ALU.add).then_inc(S["proj_added"], 1)
            dve.wait_ge(S["proj_added"], 8)

            layernorm(H[:], X[:]).then_inc(S["x0_ready"], 1)
            dve.wait_ge(S["lg_ready"], 1)
            link(tt(lg, ps[0:N, 4:6, :].rearrange("p a (b e) -> p (a b) e", e=E0), brow(rbias[:], B), ALU.add))
            link(dve.tensor_reduce(stat[:, 6, :], lg, AXX, ALU.max))
            tt(lg, lg, bcol(stat[:, 6, :], E0), ALU.subtract).then_inc(S["lg_sub"], 1)
            dve.wait_ge(S["lg_exp"], 1)
            link(dve.tensor_reduce(stat[:, 6, :], lg, AXX, ALU.add))
            link(dve.reciprocal(stat[:, 7, :], stat[:, 6, :]))
            tt(pr.rearrange("p j q e -> p q j e"), lg.rearrange("p (q j) e -> p q j e", q=Q0),
               stat[:, 7, :].rearrange("p (q j) -> p q j", q=Q0).unsqueeze(3).broadcast_to([N, Q0, B // Q0, E0]), ALU.mult).then_inc(S["pr_ready"], 1)
            dve.wait_ge(S["lg_ready"], 2)
            link(dve.tensor_copy(sc.rearrange("p (a x) -> p a x", a=2), ps[:, 6:8, 0:4 * N]))
            for r in range(R8):
                v8, i8 = cv[:, 8 * r:8 * r + 8], ci[:, 8 * r:8 * r + 8]
                link(dve.max(v8, sc))
                link(dve.max_index(i8, v8, sc))
                link(dve.match_replace(sc, v8, sc, -1.0))
            link(dve.tensor_copy(cif, ci))
            link(ts(cif, cif, const("quarter"), None, ALU.add))
            dve.tensor_copy(cii, cif).then_inc(S["cand_ready"], 1)
            dve.wait_ge(S["vm_in"], 64)
            for r in range(R8):
                v8, i8 = gv[:, 8 * r:8 * r + 8], gp[:, 8 * r:8 * r + 8]
                link(dve.max(v8, vm))
                link(dve.max_index(i8, v8, vm))
                link(dve.match_replace(vm, v8, vm, -1.0))
            link(dve.tensor_copy(gpf, gp))
            ts(gpf, gpf, const("expert", E0), None, ALU.add).then_inc(S["gp_ready"], 1)
            dve.wait_ge(S["tile_moved"], moved["gT"])

            def e0_xT(e):
                u = e % 2
                dve.wait_ge(S["e_xT"], e + 1)
                if e >= 2:
                    dve.wait_ge(S["e_up"], e - 1)
                dve.tensor_copy(xgT[u], bank(u)[:, 0:K0]).then_inc(S["e_xTc"], 1)

            e0_xT(0)
            for e in range(E0):
                u = e % 2
                if e + 1 < E0:
                    e0_xT(e + 1)
                dve.wait_ge(S["e_down"], e + 1)
                if e >= 2:
                    dve.wait_ge(S[f"e_sc{u}"], 16 * (e // 2))
                ts(yo0[u], bank(4 + u, K0)[:, 0:C], gate[:, e:e + 1], None, ALU.mult).then_inc(S["e_out"], 1)
            dve.wait_ge(S["y0_in"], 64)
            link(tt(H[:], H[:], TMP[:], ALU.add))

            def attention(tag, rope):
                a = lambda n: A[tag + n]
                per = 3 if rope else 2
                if rope:
                    for n in range(32):
                        k, u = n % 4, n % 2
                        dve.wait_ge(a("qk_mm"), n + 1)
                        if n >= 2:
                            dve.wait_ge(a("qk_c"), n - 1)
                        for s_, nm in enumerate(("rope_c", "rope_s")):
                            x = tt(rt[u][:, s_, :].rearrange("p (b t) -> p b t", b=4),
                                   bank(4 + 2 * u + s_)[:, 0:4 * N].rearrange("p (b t) -> p b t", b=4),
                                   brow(const(nm)[:, k * N:(k + 1) * N], 4), ALU.mult)
                        x.then_inc(a("rope"), 1)

                def finish(b, u):
                    last = known(b) and b == B - 1
                    n = per * b + (2 if last else 3)
                    if rope:
                        dve.wait_ge(a("o"), b + 1)
                        o8 = ps[0:N, 0:2, :].rearrange("p a (k x) -> p (a k) x", k=4)
                        dve.reciprocal(rrec.unsqueeze(2), o8[:, :, 64:65]).then_inc(a("rec"), 1)
                        dve.wait_ge(a("rec"), b + 1)
                        tt(mg, const("regroup", N).rearrange("p (k g) -> p k g", g=4), bcol(rrec, 4), ALU.mult)\
                            .then_inc(a("dve"), 1)
                        dve.wait_ge(a("dve"), n)
                        tt(og, o8[:, :, 0:64].rearrange("p k (g d) -> p k g d", g=4),
                           mg.unsqueeze(3).broadcast_to([N, 8, 4, HD]), ALU.mult).then_inc(a("dve"), 1)
                        dve.wait_ge(a("dve"), n + 1)
                        dve.tensor_reduce(TMP[:, bass.ds(b, 1), :].rearrange("p b (k d) -> p (b k) d", k=8),
                                          og.rearrange("p k g d -> p k d g"), AXX, ALU.add).then_inc(a("o_c"), 1)
                    else:
                        dve.wait_ge(a("exp"), b + 1)
                        dve.tensor_reduce(rsum, pr2[u], AXX, ALU.add).then_inc(a("dve"), 1)
                        dve.wait_ge(a("dve"), n)
                        dve.reciprocal(rrec, rsum).then_inc(a("rec"), 1)
                        dve.wait_ge(a("rec"), b + 1)
                        dve.wait_ge(a("o"), b + 1)
                        o = bank(u, N)[:, 0:C].rearrange("p (g j d) -> p g j d", g=2, j=4)
                        rv = rrec.rearrange("p (j g) -> p g j", g=2).unsqueeze(3).broadcast_to([N, 2, 4, HD])
                        tt(TMP[:, bass.ds(b, 1), :].rearrange("p b (g j d) -> p (b g) j d", g=2, j=4), o, rv, ALU.mult)\
                            .then_inc(a("o_c"), 1)

                def step(b, u):
                    if not (known(b) and b == B):
                        dve.wait_ge(a("sc"), b + 1)
                        scv = ps[0:N, 4:8, 0:2 * N].rearrange("p j (g t) -> p j g t", g=2)
                        dve.tensor_reduce(nmx.rearrange("p (j g) -> p j g", g=2), scv, AXX, ALU.max).then_inc(a("dve"), 1)
                        dve.wait_ge(a("dve"), 1 if known(b) and b == 0 else per * b - (per - 2))
                        wait(dve, a("exp"), b - 1)
                        mv = nmx.rearrange("p (j g) -> p j g", g=2).unsqueeze(3).broadcast_to([N, 4, 2, N])
                        tt(s2[u].rearrange("p (j g) t -> p j g t", g=2), scv, mv, ALU.subtract).then_inc(a("sub"), 1)
                    if not (known(b) and b == 0):
                        finish(b - 1, 1 - u)

                loop(dve, B, 2, 2, step, step=2)
                step(B, 0)
                dve.wait_ge(a("o_c"), B)
                if rope:
                    link(tt(H[:], H[:], TMP[:], ALU.add))
                else:
                    for g in range(8):
                        dve.wait_ge(a("w"), g + 1)
                        tt(X[:, 4 * g:4 * g + 4, :], X[:, 4 * g:4 * g + 4, :],
                           bank(4 + g % 4, N).rearrange("p (k c) -> p k c", k=4), ALU.add).then_inc(a("w_c"), 1)
                    dve.wait_ge(a("w_c"), 8)

            layernorm(H[:], X[:]).then_inc(A["rx_in"], 1)
            attention("r", True)
            link(layernorm(H[:], X[:]))
            layernorm(X[:], X1, gain=1).then_inc(A["fx_in"], 1)
            attention("f", False)

            layernorm(X[:], X2, gain=3).then_inc(S["m_route"], 1)
            dve.wait_ge(S["m_lg"], 1)
            link(dve.tensor_copy(lg1, ps[0:N, 4:8, :].rearrange("p a (b e) -> p (a b) e", e=E1)))
            link(dve.tensor_reduce(stat[:, 6, :], lg1, AXX, ALU.max))
            tt(lg1, lg1, bcol(stat[:, 6, :], E1), ALU.subtract).then_inc(S["m_max"], 1)
            dve.wait_ge(S["m_exp"], 1)
            link(dve.tensor_reduce(stat[:, 6, :], lg1, AXX, ALU.add))
            link(dve.reciprocal(stat[:, 7, :], stat[:, 6, :]))
            link(tt(pr1, lg1, bcol(stat[:, 7, :], E1), ALU.mult))
            for b in range(B):
                link(dve.max(mx8[:, b, :], pr1[:, b, :]))
                last = dve.max_index(ix8[:, b, :], mx8[:, b, :], pr1[:, b, :])
            link(last)
            link(dve.tensor_copy(ef, ix8))
            iota = brow(const("iota", N), B)
            for k in range(2):
                link(tt(oh[k], iota, bcol(ef[:, :, k], E1), ALU.is_equal))
            link(tt(mb, oh[0], oh[1], ALU.add))
            link(dve.memset(cumb[:, 0:1, :], 0.0))

            for b in range(B - 1):
                link(tt(cumb[:, b + 1, :], cumb[:, b, :], mb[:, b, :], ALU.add))
            link(tt(route[:, 0, :], mx8[:, :, 0], mx8[:, :, 1], ALU.add))
            dve.reciprocal(route[:, 1, :], route[:, 0, :]).then_inc(S["m_m"], 1)
            dve.wait_ge(S["m_m"], 1)
            dve.wait_ge(S["m_cum"], 1)
            cum = ps[0:N, 4:8, :].rearrange("p a (b e) -> p (a b) e", e=E1)
            for k in range(2):
                link(tt(oh[k], cum, oh[k], ALU.mult))
                link(dve.tensor_reduce(route[:, 2, :], oh[k], AXX, ALU.add))
                link(ts(route[:, 3, :], route[:, 2, :], float(CAP), None, ALU.is_lt))
                link(ts(route[:, 4, :], route[:, 2, :], float(CAP - 1), None, ALU.min))
                link(stt(out=route[:, 5, :], in0=ef[:, :, k], scalar=float(CAP), in1=route[:, 4, :], op0=ALU.mult, op1=ALU.add))
                link(dve.tensor_copy(gidx[:, k, :], route[:, 5, :]))
                link(ts(route[:, 6, :], route[:, 3, :], -float(S1), float(S1), ALU.mult, ALU.add))
                link(tt(route[:, 5, :], route[:, 5, :], route[:, 6, :], ALU.add))
                link(dve.tensor_copy(sidx[:, k, :], route[:, 5, :]))
                link(tt(route[:, 7, :], mx8[:, :, k], route[:, 1, :], ALU.mult))
                link(tt(gk[:, k, :], route[:, 7, :], route[:, 3, :], ALU.mult))
            tt(H[:], H[:], X[:], ALU.add).then_inc(S["m_sidx"], 1)

            def e1_xT(e, u):
                dve.wait_ge(S["m_xT"], e + 1)
                wait(dve, S["m_up"], e - 1)
                dve.tensor_copy(xinT[u], bank(u)[:, 0:CAP]).then_inc(S["m_xTc"], 1)

            rr = [None]

            def e1_out(e, u):
                if not (known(e) and e == E1 - 1):
                    e1_xT(e + 1, 1 - u)
                dve.wait_ge(S["m_down"], e + 1)
                if known(e):
                    if e >= 2:
                        dve.wait_ge(S[f"m_st{u}"], 32 * (e // 2))
                else:
                    dve.wait_ge(S[f"m_st{u}"], (rr[0] + 1) * 32)
                for k, (a, n) in enumerate(CAPT):
                    x = tt(yo1[u][0:n, k, :], bank(6 + u, n)[:, k * C:(k + 1) * C], b2[u][0:n, :], ALU.add)
                x.then_inc(S["m_out"], 1)

            e1_xT(0, 0)
            e1_out(0, 0)
            e1_out(1, 1)
            with dve.Fori(0, E1 // 2 - 2) as r:
                rr[0] = r
                e1_out(r * 2 + 2, 0)
                e1_out(r * 2 + 3, 1)
            e1_out(E1 - 2, 0)
            e1_out(E1 - 1, 1)

            dve.wait_ge(S["m_gather"], 16 * 2 * B)
            dve.wait_ge(S["m_sidx"], 1)
            for k in range(2):
                link(tt(Y[k], Y[k], bcol(gk[:, k, :], C), ALU.mult))
            link(tt(Y[0], Y[0], Y[1], ALU.add))
            tt(X[:], H[:], Y[0], ALU.add).then_inc(S["fin_ready"], 1)

        @block.gpsimd
        def _(pool):
            off = lambda ap: bass.IndirectOffsetOnAxis(ap=ap, axis=0)
            pool.wait_ge(S["cand_out"], 64)
            pool.wait_ge(S["tile_moved"], moved["gT"])
            for e in range(E0):
                pool.indirect_dma_start(itok[:, e:e + 1], None, d_cand, off(posi[:, e:e + 1])).then_inc(S["itok_in"], 16)
            pool.wait_ge(S["itok_in"], 16 * E0)
            pool.wait_ge(S["x0_out"], 32)
            pool.wait_ge(S["h_out"], 32)
            pool.wait_ge(S["y0_zero"], 16)

            def gather(e):
                u = e % 2
                if e >= 2:
                    pool.wait_ge(S["e_xT"], e - 1)
                pool.indirect_dma_start(xg[u], None, d_x0, off(itok[:, e:e + 1])).then_inc(S[f"g_in{u}"], 16)

            gather(0)
            gather(1)
            for e in range(E0):
                u = e % 2
                pool.wait_ge(S["e_out"], e + 1)
                if e >= 2:
                    pool.wait_ge(S[f"e_sc{u}"], 16 * (e // 2))
                pool.indirect_dma_start(d_y0[u], off(itok[:, e:e + 1]), yo0[u], None, compute_op=ALU.add)\
                    .then_inc(S[f"e_sc{u}"], 16)
                if e + 2 < E0:
                    gather(e + 2)

            def attention(tag, rope):
                a = lambda n: A[tag + n]
                pool.wait_ge(a("w_in"), 48 if rope else 64)
                n = [0]

                def put(dst, src):
                    n[0] += 1
                    pool.tensor_copy(dst, src).then_inc(a("wpad"), 1)

                if rope:
                    n[0] += 1
                    pool.memset(wpad, 0.0).then_inc(a("wpad"), 1)
                    pool.wait_ge(a("wpad"), 1)
                wq = wraw[:, 0:C].rearrange("p (g j d) -> p g j d", g=2, j=4)
                for g in range(2):
                    dst = wpad[:, g, :].rearrange("p (j d) -> p j d", j=4)
                    put(dst[:, :, 0:HD], wq[:, g])
                    if rope:
                        d2 = wpad[:, 4 + g, :].rearrange("p (j d e) -> p j d e", j=4, e=2)
                        s2_ = wq[:, g].rearrange("p j (d e) -> p j d e", e=2)
                        for par in range(2):
                            put(d2[:, :, 0:HD // 2, par], s2_[:, :, :, 1 - par])
                if not rope:
                    wk = wraw[:, C:2 * C].rearrange("p (g j d) -> p g j d", g=2, j=4)
                    for g in range(2):
                        put(wpad[:, 2 + g, :].rearrange("p (j d) -> p j d", j=4)[:, :, 0:HD], wk[:, g])
                else:
                    wk = wraw[:, C:C + C // 2].rearrange("p (g j d) -> p g j d", g=2, j=2)
                    for g in range(2):
                        for two in range(2):
                            dst = wpad[:, 2 + g, :].rearrange("p (j t d) -> p j t d", j=2, t=2)[:, :, two, :]
                            put(dst[:, :, 0:HD], wk[:, g])
                            d2 = wpad[:, 6 + g, :].rearrange("p (j t d e) -> p j t d e", j=2, t=2, e=2)[:, :, two]
                            s2_ = wk[:, g].rearrange("p j (d e) -> p j d e", e=2)
                            for par in range(2):
                                put(d2[:, :, 0:HD // 2, par], s2_[:, :, :, 1 - par])
                assert n[0] == (19 if rope else 4)
                if rope:
                    for n in range(32):
                        u = n % 2
                        pool.wait_ge(a("rope"), n + 1)
                        pool.tensor_tensor(QK[:, n % 4, (n // 4) * 4 * N:(n // 4 + 1) * 4 * N], rt[u][:, 0, :], rt[u][:, 1, :],
                                           ALU.add).then_inc(a("qk_c"), 1)
                    pool.memset(V[:, :, 64:65], 1.0).then_inc(a("ones"), 1)
                pool.wait_ge(a("qk_c"), 32)

                def step(b, u):
                    wait(pool, a("sc"), b - 1)
                    pool.tensor_copy(qs[u], QK[:, :, bass.ds(b * N, N)]).then_inc(a("q_c"), 1)

                loop(pool, B, 2, 2, step, step=2)

            attention("r", True)
            attention("f", False)

            pool.wait_ge(S["m_sidx"], 1)
            pool.wait_ge(S["buf_zeroed"], 64)
            for b in range(B):
                for k in range(2):
                    pool.indirect_dma_start(d_buf, off(sidx[:, k, b:b + 1]), X2[:, b, :], None,
                                            bounds_check=S1 - 1, oob_is_err=False).then_inc(S["m_scat"], 16)
            for u in range(2):
                pool.wait_ge(S[f"m_st{u}"], 32 * (E1 // 2))
            for b in range(B):
                for k in range(2):
                    pool.indirect_dma_start(Y[k][:, b, :], None, d_y1, off(gidx[:, k, b:b + 1])).then_inc(S["m_gather"], 16)


_INS = ["x", "txt", "L0_tok_w", "L0_tok_b", "L0_attn_Wqkv", "L0_attn_gamma", "L0_attn_beta", "L0_attn_Wproj",
        "L0_attn_bproj", "L0_ffn_W_router", "L0_ffn_b_router", "L0_ffn_W_up", "L0_ffn_b_up", "L0_ffn_W_down",
        "L0_ffn_b_down", "L1_attn_Wq", "L1_attn_Wk", "L1_attn_Wv", "L1_ffn_ln1_g", "L1_ffn_ln1_b", "L1_ffn_wq",
        "L1_ffn_wk", "L1_ffn_wv", "L1_ffn_wo", "L1_ffn_ln2_g", "L1_ffn_ln2_b", "L1_ffn_wr", "L1_ffn_w1",
        "L1_ffn_b1", "L1_ffn_w2", "L1_ffn_b2"]


def kernel(**inputs):
    import numpy as _np
    import concourse.bacc as _bacc
    from concourse import mybir as _mybir
    from concourse.bass_utils import run_bass_kernel_spmd as _run

    nc = _bacc.Bacc("TRN2", target_bir_lowering=False, num_devices=1)
    arrays, aps = {}, {}
    for name in _INS:
        a = _np.ascontiguousarray(inputs[name])
        arrays[f"in_{name}"] = a
        aps[name] = nc.dram_tensor(f"in_{name}", a.shape, _mybir.dt.from_np(a.dtype), kind="ExternalInput").ap()
    arrays["consts"] = shape_constants()
    consts = nc.dram_tensor("consts", [128, NCONST], _mybir.dt.float32, kind="ExternalInput").ap()
    out = nc.dram_tensor("out", [B, N, C], _mybir.dt.float32, kind="ExternalOutput").ap()
    program(nc, aps, out, consts)
    r = _run(nc, [arrays], core_ids=[0])
    return r.results[0]["out"]
```

```python
from contextlib import ExitStack

import numpy as np

import concourse.bass as bass
from concourse import mybir

ALU = mybir.AluOpType
ACT = mybir.ActivationFunctionType
AXX = mybir.AxisListType.X
F32 = mybir.dt.float32
BF16 = mybir.dt.bfloat16
U32 = mybir.dt.uint32
I32 = mybir.dt.int32

B = 32
NI, NT = 36, 77
N = NI + NT
C = 128
T = B * N
HP = 6
PS = 16
W = HP * PS
KT = 6
NH, HD = 8, 16
EPS = 1e-5

E0, GRP, F0 = 32, 4, 341
K0 = T // E0
Q0 = 4
LQ = T // Q0
R8 = -(-K0 // 8)
CQ = R8 * 8
F0C = [(0, 128), (128, 128), (256, F0 - 256)]

E1, F1 = 64, 512
CAP = 2 * (T * 2 // E1)
S1 = E1 * CAP
D = 4
R1 = C + 2
CAPT = [(0, 128), (128, CAP - 128)]
NJ = F1 // 128

FLOOR = 8388608.0
NUDGE = 1.0 + 2.0 ** -23
NEG = -1e30
SPLIT = 112

CONST = {}
_at = 0
for _name, _w in (("ident", 128), ("tri", N), ("ones", 128), ("causal", 4 * N), ("headmask", NH),
                  ("rope_c", 4 * N), ("rope_s", 4 * N), ("quarter", 1), ("expert", 1), ("iota", E1), ("regroup", NH * 4), ("token", B), ("dump", 2)):
    CONST[_name] = (_at, _w)
    _at += _w
NCONST = _at


def shape_constants():
    c = np.zeros((128, NCONST), np.float32)

    def put(name, value):
        a, w = CONST[name]
        value = np.asarray(value, np.float32)
        c[:value.shape[0], a:a + w] = value.reshape(value.shape[0], w)

    p = np.arange(128)
    put("ident", np.eye(128))
    put("tri", p[:N, None] < np.arange(N)[None, :])
    put("ones", np.ones((128, 128)))
    put("causal", np.tile(np.where(np.arange(N)[None, :] > p[:N, None], NEG, 0.0), (1, 4)))
    put("headmask", p[:, None] // HD == np.arange(NH)[None, :])
    put("quarter", (p // E0 * LQ)[:, None])
    put("expert", (p[:E0] * (Q0 * CQ))[:, None])
    put("iota", np.tile(np.arange(E1), (128, 1)))
    r = 8 * p[:N, None] + np.arange(NH)[None, :]
    put("regroup", (r // N % 4)[:, :, None] == np.arange(4)[None, None, :])
    put("token", np.arange(B)[None, :] * N + p[:N, None])
    put("dump", T + p[:, None] + np.array([[0, 128]]))
    t = np.arange(N, dtype=np.float64)
    rc, rs = np.zeros((128, 4, N)), np.zeros((128, 4, N))
    for blk in range(4):
        for j in range(4):
            h = (blk % 2) * 4 + j
            for d in range(HD):
                f, width = (h * HD + d, C) if blk < 2 else (h // 2 * HD + d, C // 2)
                theta = 10000.0 ** (-(2.0 * (np.float64(f // 2) - 1.0))) / width
                rc[32 * j + d, blk] = np.cos(t * theta)
                rs[32 * j + d, blk] = np.sin(t * theta) * (1.0 if f % 2 == 0 else -1.0)
    put("rope_c", rc)
    put("rope_s", rs)
    return c


def program(nc, ins, out, consts):
    ctx = ExitStack()
    with ctx:
        def sb(name, shape, dt=F32):
            t = ctx.enter_context(nc.sbuf_tensor(name, shape, dt))
            return t[(slice(None),) * len(shape)]

        def sem(name):
            return ctx.enter_context(nc.semaphore(name))

        def dram(name, shape, dt=F32):
            return nc.dram_tensor(name, shape, dt, kind="Internal").ap()

        d_cand = dram("d_cand", [E0 * Q0 * CQ, 1], I32)
        d_x0 = dram("d_x0", [T, C])
        d_y0 = [dram(f"d_y0_{i}", [T, C]) for i in range(2)]
        d_buf = dram("d_buf", [S1, R1])
        d_acc = [dram(f"d_acc_{i}", [T + CAP, C]) for i in range(2)]

        cst = sb("cst", [128, NCONST])
        H = sb("H", [N, B, C])
        X = sb("X", [N, B, C])
        TMP = sb("TMP", [N, B, C])
        XT = sb("XT", [128, T])
        stat = sb("stat", [N, 8, B])
        identb = sb("identb", [128, 128], BF16)
        trib = sb("trib", [N, N], BF16)
        onesb = sb("onesb", [N, N], BF16)
        causalb = sb("causalb", [N, 4 * N], BF16)
        rows = sb("rows", [N, 5, C])
        idle = sb("idle", [1, 4])
        rbias = sb("rbias", [N, E0])
        tokb = sb("tokb", [128, 1])
        gb = sb("gb", [128, 6])
        bnst = sb("bnst", [128, 8, 6])
        bnag = sb("bnag", [128, 8])
        bup_in = sb("bup_in", [E0 // GRP, F0])
        b1T = sb("b1T", [128, NJ, E1])
        zrow = sb("zrow", [128, 2, R1])
        zrowi = zrow.bitcast(I32)
        wrt0 = sb("wrt0", [128, E0])
        wrt1 = sb("wrt1", [128, E1])
        wsplit = sb("wsplit", [128, 3, 4 * C], BF16)
        wres = sb("wres", [128, 2, 4 * C])
        arena = sb("arena", [128, 30024])

        def carve(at, words, dt=F32, parts=128):
            v = arena[0:parts, at:at + words]
            return v if dt == F32 else v.bitcast(dt)

        img = [carve(i * 4608, 4608, parts=96).rearrange("p (c h w) -> p c h w", c=3, w=W) for i in range(2)]
        wtok = carve(9216, 768)
        wtokT = carve(9984, 768).rearrange("p (k e) -> p k e", k=KT)
        wqkvp = carve(10752, 512).rearrange("p (j c) -> p j c", j=4)
        patT = carve(11264, KT * B * NI).rearrange("p (k t) -> p k t", k=KT)
        embT = carve(18176, B * NI)
        imgp = [carve(19400 + i * 4608, 4608, parts=96).rearrange("p (w r x) -> p w r x", w=HP, x=PS) for i in range(2)]
        rf = [carve(i * T, T) for i in range(2)]
        qkvb = carve(2 * T, 3 * T // 2, BF16).rearrange("p (j t) -> p j t", j=3)
        qm = carve(2 * T + 3 * T // 2, NH * T // 2, BF16).rearrange("p (h t) -> p h t", h=NH)
        at = 2 * T + 3 * T // 2 + NH * T // 2
        assert at + NH * N <= 30000
        aspk = carve(at, NH * N, BF16, N).rearrange("p (u x) -> p u x", u=2)
        xst = XT[:, 0:T // 2].bitcast(BF16)
        xsb = carve(2 * T + 3 * T // 2, B * C // 2, BF16, N).rearrange("p (b c) -> p b c", b=B)
        vtok = X.rearrange("p b c -> p (b c)")[:, 0:B * C // 2].bitcast(BF16).rearrange("p (b c) -> p b c", b=B)
        osb = xsb
        ost = carve(0, T // 2, BF16)
        sc = carve(0, LQ)
        cv = carve(1000, CQ)
        ci = carve(1200, CQ, U32)
        cif = carve(1400, CQ)
        cii = carve(1600, CQ, I32)
        vm = carve(1800, Q0 * CQ, parts=E0)
        gv = carve(2400, CQ, parts=E0)
        gp = carve(2600, CQ, U32, E0)
        gpf = carve(2800, CQ, parts=E0)
        lg = carve(3000, B * E0, parts=N).rearrange("p (b e) -> p b e", b=B)
        pr = carve(4100, B * E0, parts=N).rearrange("p (j q e) -> p j q e", q=Q0, e=E0)
        posi = carve(5200, E0, I32, N)
        gate = carve(5300, E0, parts=N)
        itok = carve(5400, E0, I32, N)
        wu0 = [carve(6000 + F0 * u, F0) for u in range(D)]
        wd0 = [carve(7400 + 384 * u, 384).rearrange("p (k c) -> p k c", k=3) for u in range(D)]
        b1row = carve(12000, F1, parts=E1)
        xg = [carve(9000 + C * u, C, parts=N) for u in range(D)]
        xgT = [carve(9600 + N * u, N) for u in range(2)]
        act0 = [carve(9900 + 3 * N * u, 3 * N).rearrange("p (k t) -> p k t", k=3) for u in range(2)]
        yo0 = [carve(10600 + C * u, C, parts=N) for u in range(D)]
        bupT = carve(11200, 3 * (E0 // GRP)).rearrange("p (k g) -> p k g", k=3)
        wpad = carve(0, 8 * C).rearrange("p (k x) -> p k x", k=8)
        rt = [carve(1024 + 904 * u, 8 * N).rearrange("p (s t) -> p s t", s=2) for u in range(2)]
        qs = [carve(2900 + 452 * u, 2 * N).rearrange("p (g t) -> p g t", g=2) for u in range(2)]
        kz = [carve(1024 + 904 * u, NH * N).rearrange("p (g x) -> p g x", g=2) for u in range(2)]
        s2 = [carve(3810 + 904 * u, NH * N, parts=N).rearrange("p (h t) -> p h t", h=NH) for u in range(2)]
        pr2 = [carve(5620 + 904 * u, NH * N, parts=N).rearrange("p (h t) -> p h t", h=NH) for u in range(2)]
        ptT = [carve(7430 + 904 * u, NH * N, parts=N).rearrange("p (h t) -> p h t", h=NH) for u in range(2)]
        nmx = [carve(9240 + NH * u, NH, parts=N) for u in range(2)]
        rrec = [carve(9280 + NH * u, NH, parts=N) for u in range(2)]
        mg = carve(9300, 32, parts=N).rearrange("p (k g) -> p k g", g=4)
        og = carve(9340, 512, parts=N).rearrange("p (k g d) -> p k g d", k=8, g=4)
        VW = HD + 1
        Vf = carve(10600, B * NH * VW, parts=N).rearrange("p (b h d) -> p b h d", b=B, h=NH)
        V = carve(10800, B * C, parts=N).rearrange("p (b c) -> p b c", b=B)
        QK = carve(15000, 4 * T).rearrange("p (k t) -> p k t", k=4)
        X1 = carve(15000, B * C, parts=N).rearrange("p (b c) -> p b c", b=B)
        wraw = carve(29464, 3 * C)
        wo = carve(29464 + 3 * C, C)
        xinT = [carve(0 + CAP * u, CAP) for u in range(2)]
        hT = [carve(500 + 904 * u, NJ * CAP).rearrange("p (k t) -> p k t", k=NJ) for u in range(2)]
        lg1 = carve(0, B * E1, parts=N).rearrange("p (b e) -> p b e", b=B)
        pr1 = carve(2048, B * E1, parts=N).rearrange("p (b e) -> p b e", b=B)
        oh = [carve(4096 + 2048 * k, B * E1, parts=N).rearrange("p (b e) -> p b e", b=B) for k in range(2)]
        mb = carve(8192, B * E1 // 2, BF16, N).rearrange("p (b e) -> p b e", b=B)
        cumb = carve(9216, B * E1 // 2, BF16, N).rearrange("p (b e) -> p b e", b=B)
        mx8 = carve(10240, B * 8, parts=N).rearrange("p (b e) -> p b e", b=B)
        ix8 = carve(10496, B * 8, U32, N).rearrange("p (b e) -> p b e", b=B)
        ef = carve(10752, B * 8, parts=N).rearrange("p (b e) -> p b e", b=B)
        route = carve(11008, 8 * B, parts=N).rearrange("p (k b) -> p k b", k=8)
        sidx = carve(11264, 2 * B, I32, N).rearrange("p (k b) -> p k b", k=2)
        gidx = carve(11328, 2 * B, I32, N).rearrange("p (k b) -> p k b", k=2)
        gk = carve(11392, 2 * B, parts=N).rearrange("p (k b) -> p k b", k=2)
        w1 = [carve(11500 + 512 * u, F1) for u in range(D)]
        w2 = [carve(13548 + 512 * u, F1).rearrange("p (k c) -> p k c", k=NJ) for u in range(D)]
        xin = [carve(15596 + 2 * R1 * u, 2 * R1).rearrange("p (k c) -> p k c", k=2) for u in range(D)]
        yo1 = [carve(16640 + 256 * u, 2 * C).rearrange("p (k c) -> p k c", k=2) for u in range(D)]
        b2 = carve(17670, E1 * C)
        X2r = carve(25862, B * R1, parts=N).rearrange("p (b c) -> p b c", b=B)
        X2i = carve(25862, B * R1, I32, N).rearrange("p (b c) -> p b c", b=B)
        xini = [carve(15596 + 2 * R1 * u, 2 * R1, I32).rearrange("p (k c) -> p k c", k=2) for u in range(D)]
        fsum = carve(17670, T)
        X2 = X2r[:, :, 0:C]

        def const(name, parts=128):
            a, w = CONST[name]
            return cst[0:parts, a:a + w]

        ident = const("ident")
        ones1 = cst[0:1, CONST["ones"][0]:CONST["ones"][0] + 128]

        ps = ctx.enter_context(nc.psum_tensor("ps", [128, 8, 512], F32))

        def bank(i, parts=128):
            return ps[0:parts, i, :]

        names = """cst_in img_in img_packed wtok_in txt_in wqkv_in small_in rows_in zeroed zrow_ready buf_zeroed b1_in
            tile_ready tile_moved dve act ln_centred ln_squared ln_var ln_std
            spk_relu spk_ready qkv_ready qkv_stats qkv_std qkv_moved w_split
            qm_ready sT_ready a_ready o_ready o_moved ob_ready proj_ready proj_added
            x0_ready x0_out h_out y0_zero lg_ready lg_sub lg_exp pr_ready
            cand_ready cand_out vm_in gp_ready itok_in0 itok_in1 itok_in2 itok_in3 ones_in
            g_in0 g_in1 g_in2 g_in3 e_w0 e_w1 e_w2 e_w3 e_xT e_xTc e_up e_act e_down e_out e_sc0 e_sc1
            y0_in consts_ready
            m_route m_lg m_max m_exp m_m m_cum m_sidx m_rows m_scat0 m_scat1 acc_in b2_in m_biased m_sc0 m_sc1 m_w0 m_w1 m_w2 m_w3 m_x0 m_x1 m_x2 m_x3 m_xT m_xTc m_up m_act m_down m_out
            fin_in0 fin_in1 fin_in2 fin_in3 fin_ready fin_out""".split()
        S = {n: sem(n) for n in names}
        A = {}
        for tag in ("r", "f"):
            for n in ("w_in", "wpad", "ones", "x_in", "qk_mm", "rope", "qk_c", "q_c", "kz", "k_in0", "k_in1", "sc", "max", "sub", "exp", "pT",
                      "pTc", "rec", "o", "mask", "group", "o_c", "w", "w_c"):
                A[tag + n] = sem(f"{tag}_{n}")

        class Chain:

            def __init__(self, eng, s):
                self.eng, self.s, self.n, self.at = eng, s, 0, 0

            def tick(self, ins):
                ins.then_inc(self.s, 1)
                self.n += 1
                return self.n

            def link(self, ins):
                self.tick(ins)
                self.eng.wait_ge(self.s, self.at + self.n)

        def loop(eng, total, head, tail, body, step=1):
            for i in range(head):
                body(i, i % step, i // step)
            steps = (total - head - tail) // step
            assert steps * step == total - head - tail and head % step == 0
            with eng.Fori(0, steps) as r:
                for k in range(step):
                    body(r * step + (head + k), k, r + head // step)
            for i in range(total - tail, total):
                body(i, i % step, i // step)

        def known(i):
            return isinstance(i, int)

        def wait(eng, s, value):
            if not known(value) or value > 0:
                eng.wait_ge(s, value)

        tiles = []

        class Tiles:
            def __init__(self):
                self.n = 0

            def pe_open(self, pe):
                if self.n >= 4:
                    pe.wait_ge(S["tile_moved"], self.n - 3)
                return self.n % 4

            def pe_close(self, ins):
                ins.then_inc(S["tile_ready"], 1)
                self.n += 1

            def act_open(self, act):
                act.wait_ge(S["tile_ready"], self.n + 1)
                return self.n % 4

            def act_close(self, ins):
                ins.then_inc(S["tile_moved"], 1)
                self.n += 1

        def tile_counts():
            c, n = {}, 0
            for name, k in (("w", 3), ("pat", 24), ("emb", 4), ("H", 8), ("xs", 8), ("v", 8), ("os", 8),
                            ("xt0", 8), ("gT", 4), ("rx", 8), ("rv", 8), ("fx", 8), ("fv", 8), ("fo", 8), ("xt1", 8)):
                n += k
                c[name] = n
            return c

        moved = tile_counts()
        tok_rows = [(0, SPLIT), (SPLIT, N)]

        def bcol(ap2, width):
            return ap2.unsqueeze(2).broadcast_to([ap2.shape[0], ap2.shape[1], width])

        def brow(ap2, count):
            return ap2.unsqueeze(1).broadcast_to([ap2.shape[0], count, ap2.shape[1]])

        block = ctx.enter_context(nc.Block())

        @block.sync
        def _(sp):
            sp.dma_start(cst[:], consts).then_inc(S["cst_in"], 16)
            sp.dma_start(wtok, ins["L0_tok_w"]).then_inc(S["wtok_in"], 16)
            imgv = ins["x"].rearrange("b c (h p) w -> b h c (p w)", h=HP)
            for i in range(2):
                for h in range(HP):
                    sp.dma_start(img[i][h * 16:(h + 1) * 16].rearrange("p c h w -> p c (h w)"), imgv[16 * i:16 * i + 16, h])\
                        .then_inc(S["img_in"], 16)
            sp.dma_start(H[NI:N, :, :], ins["txt"].rearrange("b n c -> n b c")).then_inc(S["txt_in"], 16)
            sp.dma_start(wqkvp[:, 0:3, :], ins["L0_attn_Wqkv"].rearrange("(j d) c -> d j c", j=3)).then_inc(S["wqkv_in"], 16)
            sp.dma_start(wqkvp[:, 3, :], ins["L0_attn_Wproj"]).then_inc(S["wqkv_in"], 16)
            sp.dma_start(tokb[:], ins["L0_tok_b"].rearrange("(p o) -> p o", o=1)).then_inc(S["small_in"], 16)
            sp.dma_start(gb[:, 0:3], ins["L0_attn_gamma"].rearrange("(j p) -> p j", j=3), allow_slow_non_contiguous=True).then_inc(S["small_in"], 16)
            sp.dma_start(gb[:, 3:6], ins["L0_attn_beta"].rearrange("(j p) -> p j", j=3), allow_slow_non_contiguous=True).then_inc(S["small_in"], 16)
            sp.dma_start(wrt0[:], ins["L0_ffn_W_router"]).then_inc(S["small_in"], 16)
            sp.dma_start(wrt1[:], ins["L1_ffn_wr"]).then_inc(S["small_in"], 16)
            for i, nm in enumerate(("L0_attn_bproj", "L1_ffn_ln1_g", "L1_ffn_ln1_b", "L1_ffn_ln2_g", "L1_ffn_ln2_b")):
                sp.dma_start(rows[:, i, :], ins[nm].partition_broadcast(N)).then_inc(S["rows_in"], 16)
            sp.dma_start(bup_in, ins["L0_ffn_b_up"]).then_inc(S["rows_in"], 16)
            sp.dma_start(rbias[:], ins["L0_ffn_b_router"].partition_broadcast(N)).then_inc(S["rows_in"], 16)
            sp.wait_ge(S["zeroed"], 1)
            flat = lambda ap: ap.rearrange("s c -> (s c)").rearrange("(p x) -> p x", p=128)
            sp.dma_start(flat(d_y0[1]), XT).then_inc(S["y0_zero"], 16)
            sp.dma_start(flat(d_acc[1][0:T]), XT).then_inc(S["y0_zero"], 16)
            for i in range(2):
                sp.dma_start(flat(d_acc[i][T:T + CAP]), XT[:, 0:CAP]).then_inc(S["y0_zero"], 16)
            sp.wait_ge(S["zrow_ready"], 1)
            for k, (a, n) in enumerate(CAPT):
                sp.dma_start(d_buf.rearrange("(e s) c -> s e c", s=CAP)[a:a + n],
                             zrow[0:n, k, :].unsqueeze(1).broadcast_to([n, E1, R1])).then_inc(S["buf_zeroed"], 16)
            sp.wait_ge(S["x0_ready"], 1)
            for a, z in tok_rows:
                sp.dma_start(d_x0.rearrange("(b n) c -> n b c", n=N)[a:z], X[a:z]).then_inc(S["x0_out"], 16)
                sp.dma_start(d_y0[0].rearrange("(b n) c -> n b c", n=N)[a:z], H[a:z]).then_inc(S["h_out"], 16)
            sp.dma_start(b1row, ins["L1_ffn_b1"]).then_inc(S["b1_in"], 16)
            sp.wait_ge(S["cand_ready"], 1)
            for q in range(Q0):
                sp.dma_start(d_cand.rearrange("(e q r) o -> q e (r o)", e=E0, q=Q0)[q], cii[q * E0:(q + 1) * E0, :])\
                    .then_inc(S["cand_out"], 16)
                sp.dma_start(vm[:, q * CQ:(q + 1) * CQ], cv[q * E0:(q + 1) * E0, :]).then_inc(S["vm_in"], 16)

            def e0_load(e, u, turn):
                wait(sp, S["e_down"], e - D + 1)
                wdv = ins["L0_ffn_W_down"].rearrange("e f c -> (e f) c")
                g = e // GRP if known(e) else turn
                sp.dma_start(wu0[u], ins["L0_ffn_W_up"].rearrange("g c f -> (g c) f")[bass.ds(g * C, C), :])\
                    .then_inc(S[f"e_w{u}"], 16)
                sp.dma_start(wd0[u][:, 0:2, :], wdv[bass.ds(e * F0, 256), :].rearrange("(k p) c -> p k c", k=2))\
                    .then_inc(S[f"e_w{u}"], 16)
                sp.dma_start(wd0[u][0:F0 - 256, 2, :], wdv[bass.ds(e * F0 + 256, F0 - 256), :]).then_inc(S[f"e_w{u}"], 16)
                sp.dma_start(wd0[u][F0 - 256:F0 - 255, 2, :], ins["L0_ffn_b_down"][bass.ds(e, 1), :])\
                    .then_inc(S[f"e_w{u}"], 16)

            loop(sp, E0, D, 0, e0_load, step=D)
            for u in range(2):
                sp.wait_ge(S[f"e_sc{u}"], 16 * (E0 // 2))
            for a, z in tok_rows:
                sp.dma_start(H[a:z], d_y0[0].rearrange("(b n) c -> n b c", n=N)[a:z]).then_inc(S["y0_in"], 16)
                sp.dma_start(TMP[a:z], d_y0[1].rearrange("(b n) c -> n b c", n=N)[a:z]).then_inc(S["y0_in"], 16)

            sp.dma_start(wraw[:, 0:128], ins["L1_attn_Wq"]).then_inc(A["rw_in"], 16)
            sp.dma_start(wraw[:, 128:192], ins["L1_attn_Wk"]).then_inc(A["rw_in"], 16)
            sp.dma_start(wraw[:, 256:320], ins["L1_attn_Wv"]).then_inc(A["rw_in"], 16)
            sp.wait_ge(A["rqk_mm"], 32)
            sp.wait_ge(S["tile_moved"], moved["rv"])
            for i, nm in enumerate(("L1_ffn_wq", "L1_ffn_wk", "L1_ffn_wv")):
                sp.dma_start(wraw[:, i * 128:(i + 1) * 128], ins[nm]).then_inc(A["fw_in"], 16)
            sp.dma_start(wo, ins["L1_ffn_wo"]).then_inc(A["fw_in"], 16)

            def keys(tag):
                a = lambda n: A[tag + n]

                def step(b, u, _turn):
                    wait(sp, a("sc"), b - 1)
                    for j in range(4):
                        rows_ = slice(32 * j, 32 * j + 32)
                        sp.dma_start(kz[u][rows_, :, j * N:(j + 1) * N], QK[rows_, 2:4, bass.ds(b * N, N)])\
                            .then_inc(a(f"k_in{u}"), 16)

                loop(sp, B, 2, 2, step, step=2)

            sp.wait_ge(A["rkz"], 2)
            keys("r")
            sp.wait_ge(A["fqk_c"], 32)
            keys("f")

            sp.wait_ge(A["fo_c"], B)
            sp.dma_start(b2.rearrange("p (e c) -> p e c", e=E1), ins["L1_ffn_b2"].partition_broadcast(128)).then_inc(S["b2_in"], 16)
            w1v = ins["L1_ffn_w1"].rearrange("e c f -> (e c) f")
            w2v = ins["L1_ffn_w2"].rearrange("e (p k) c -> (e p) (k c)", k=NJ)

            def e1_weights(e, u, turn):
                wait(sp, S["m_down"], e - D + 1)
                sp.dma_start(w1[u], w1v[bass.ds(e * 128, 128), :]).then_inc(S[f"m_w{u}"], 16)
                sp.dma_start(w2[u].rearrange("p k c -> p (k c)"), w2v[bass.ds(e * 128, 128), :]).then_inc(S[f"m_w{u}"], 16)

            def e1_tokens(e, u, turn):
                for k in range(2):
                    wait(sp, S[f"m_sc{k}"], (e - D + 1) * 16)
                for k, (a, n) in enumerate(CAPT):
                    sp.dma_start(xin[u][0:n, k, :], d_buf[bass.ds(e * CAP + a, n), :]).then_inc(S[f"m_x{u}"], 16)

            for e in range(D):
                e1_weights(e, e, 0)
            sp.wait_ge(S["m_sidx"], 1)
            for a, z in tok_rows:
                sp.dma_start(d_acc[0][0:T].rearrange("(b n) c -> n b c", n=N)[a:z], H[a:z]).then_inc(S["acc_in"], 16)
            for k in range(2):
                sp.wait_ge(S[f"m_scat{k}"], 16 * B)
            for e in range(D):
                e1_tokens(e, e, 0)

            def e1_io(e, u, turn):
                e1_weights(e, u, turn)
                e1_tokens(e, u, turn)

            with sp.Fori(1, E1 // D) as r:
                for u in range(D):
                    e1_io(r * D + u, u, r)
            for k in range(2):
                sp.wait_ge(S[f"m_sc{k}"], 16 * E1)
            q = T // 4
            for i in range(4):
                sp.dma_start(XT[:, i * q:(i + 1) * q], flat(d_acc[0][0:T])[:, i * q:(i + 1) * q]).then_inc(S[f"fin_in{i}"], 16)
                sp.dma_start(fsum[:, i * q:(i + 1) * q], flat(d_acc[1][0:T])[:, i * q:(i + 1) * q]).then_inc(S[f"fin_in{i}"], 16)
            for i in range(4):
                sp.wait_ge(S["fin_ready"], i + 1)
                sp.dma_start(flat(out.rearrange("b n c -> (b n) c"))[:, i * q:(i + 1) * q], XT[:, i * q:(i + 1) * q])\
                    .then_inc(S["fin_out"], 16)
            sp.wait_ge(S["fin_out"], 64)

        @block.tensor
        def _(pe):
            tl = Tiles()
            pe.wait_ge(S["cst_in"], 16)
            pe.wait_ge(S["wtok_in"], 16)
            for g in range(2):
                k0 = tl.pe_open(pe)
                for k in range(3):
                    ins_ = pe.transpose(bank(k0)[:, k * 128:(k + 1) * 128], wtok[:, (3 * g + k) * 128:(3 * g + k + 1) * 128], ident)
                tl.pe_close(ins_)
            pe.wait_ge(S["wqkv_in"], 32)
            k0 = tl.pe_open(pe)
            for j in range(4):
                ins_ = pe.transpose(bank(k0)[:, j * 128:(j + 1) * 128], wqkvp[:, j, :], ident)
            tl.pe_close(ins_)
            for t in range(2):
                pe.wait_ge(S["img_packed"], t + 1)
                for k in range(KT):
                    for half in range(2):
                        k0 = tl.pe_open(pe)
                        for w in range(3):
                            wp = half * 3 + w
                            src = imgp[t][:, wp, k * 8:(k + 1) * 8, :].rearrange("p r x -> p (r x)")
                            ins_ = pe.transpose(bank(k0)[:, w * 96:(w + 1) * 96], src, ident[0:96, 0:96])
                        tl.pe_close(ins_)
            pe.wait_ge(S["tile_moved"], moved["pat"])
            for g in range(4):
                k0 = tl.pe_open(pe)
                for k in range(KT):
                    ins_ = pe.matmul(bank(k0)[:, 0:288], wtokT[:, k, :], patT[:, k, g * 288:(g + 1) * 288],
                                     start=(k == 0), stop=(k == KT - 1))
                tl.pe_close(ins_)
            pe.wait_ge(S["tile_moved"], moved["emb"])
            for g in range(8):
                k0 = tl.pe_open(pe)
                for k in range(4):
                    b = 4 * g + k
                    ins_ = pe.transpose(bank(k0)[0:NI, k * 128:(k + 1) * 128], embT[:, b * NI:(b + 1) * NI], ident)
                tl.pe_close(ins_)

            def turn(src, dt, idm, ready=None):
                for g in range(8):
                    k0 = tl.pe_open(pe)
                    o = bank(k0) if dt == F32 else bank(k0).bitcast(BF16)
                    for k in range(4):
                        stride = N if dt == F32 else N + 1
                        x = pe.transpose(o[:, k * stride:k * stride + N], src[:, 4 * g + k, :], idm)
                    tl.pe_close(x)

            pe.wait_ge(S["spk_ready"], 1)
            pe.wait_ge(S["consts_ready"], 1)
            turn(xsb, BF16, identb[0:N, 0:N])
            pe.wait_ge(S["w_split"], 1)
            pe.wait_ge(S["tile_moved"], moved["xs"])
            for j in range(3):
                for c in range(8):
                    if j:
                        pe.wait_ge(S["qkv_moved"], 8 * (j - 1) + c + 1)
                    for p in range(3):
                        x = pe.matmul(bank(c)[:, 0:4 * N], wsplit[:, p, j * C:(j + 1) * C], xst[:, c * 4 * N:(c + 1) * 4 * N],
                                      start=(p == 0), stop=(p == 2))
                    x.then_inc(S["qkv_ready"], 1)
            pe.wait_ge(S["qkv_moved"], 24)
            pe.wait_ge(S["qm_ready"], 3)
            for g in range(8):
                k0 = tl.pe_open(pe)
                for k in range(4):
                    b = 4 * g + k
                    x = pe.transpose(bank(k0, N).bitcast(BF16)[:, k * 128:(k + 1) * 128], qkvb[:, 2, b * N:(b + 1) * N], identb)
                tl.pe_close(x)
            pe.wait_ge(S["tile_moved"], moved["v"])
            pe.wait_ge(S["qm_ready"], 4)

            def spk_scores(b, u):
                for g in range(2):
                    x = pe.matmul(bank(2 * u + g, N)[:, 0:4 * N], qkvb[:, 1, bass.ds(b * N, N)],
                                  qm[:, 4 * g:4 * g + 4, bass.ds(b * N, N)], start=True, stop=True)
                x.then_inc(S["sT_ready"], 1)

            def spk_step(b, u, _turn):
                if not (known(b) and b == B - 1):
                    wait(pe, S["a_ready"], b)
                    spk_scores(b + 1, 1 - u)
                pe.wait_ge(S["a_ready"], b + 1)
                wait(pe, S["o_moved"], b - 1)
                for h in range(NH):
                    x = pe.matmul(bank(4 + u, N)[:, h * HD:(h + 1) * HD], aspk[:, u, h * N:(h + 1) * N],
                                  vtok[:, bass.ds(b, 1), h * HD:(h + 1) * HD], start=True, stop=True)
                x.then_inc(S["o_ready"], 1)

            spk_scores(0, 0)
            loop(pe, B, 2, 2, spk_step, step=2)
            pe.wait_ge(S["ob_ready"], 1)
            turn(osb, BF16, identb[0:N, 0:N])
            pe.wait_ge(S["tile_moved"], moved["os"])
            for g in range(8):
                if g >= 4:
                    pe.wait_ge(S["proj_added"], g - 3)
                for k in range(4):
                    b = 4 * g + k
                    for p in range(3):
                        x = pe.matmul(bank(4 + g % 4, N)[:, k * C:(k + 1) * C], ost[:, b * N:(b + 1) * N],
                                      wsplit[:, p, 3 * C:4 * C], start=(p == 0), stop=(p == 2))
                x.then_inc(S["proj_ready"], 1)

            pe.wait_ge(S["x0_ready"], 1)
            pe.wait_ge(S["y0_zero"], 64)
            turn(X, F32, ident[0:N, 0:N])
            pe.wait_ge(S["tile_moved"], moved["xt0"])
            for b in range(B):
                x = pe.matmul(bank(4 + b // 16, N)[:, (b % 16) * E0:(b % 16 + 1) * E0], XT[:, b * N:(b + 1) * N], wrt0[:],
                              start=True, stop=True)
            x.then_inc(S["lg_ready"], 1)
            pe.wait_ge(S["pr_ready"], 1)
            for j in range(B // Q0):
                x = pe.transpose(bank(6 + j // 4)[:, (j % 4) * N:(j % 4 + 1) * N],
                                 pr[:, j].rearrange("p q e -> p (q e)"), ident[0:N, 0:N])
            x.then_inc(S["lg_ready"], 1)
            pe.wait_ge(S["gp_ready"], 1)
            for src in (gpf, gv):
                k0 = tl.pe_open(pe)
                tl.pe_close(pe.transpose(bank(k0, K0)[:, 0:E0], src[:, 0:K0], ident[0:E0, 0:E0]))

            k0 = tl.pe_open(pe)
            for k, (a, n) in enumerate(F0C):
                x = pe.transpose(bank(k0, n)[:, 8 * k:8 * k + 8], bup_in[:, a:a + n], ident[0:E0 // GRP, 0:E0 // GRP])
            tl.pe_close(x)
            pe.wait_ge(S["b1_in"], 16)
            k0 = tl.pe_open(pe)
            for k in range(NJ):
                x = pe.transpose(bank(k0)[:, k * E1:(k + 1) * E1], b1row.rearrange("e (p k) -> e k p", k=NJ)[:, k, :],
                                 ident[0:E1, 0:E1])
            tl.pe_close(x)
            pe.wait_ge(S["tile_moved"], moved["gT"])

            def e0_turn(e, u, turn):
                v = u % 2
                pe.wait_ge(S[f"g_in{u}"], (turn + 1) * 16)
                wait(pe, S["e_xTc"], e - 1)
                pe.transpose(bank(v)[:, 0:K0], xg[u], ident[0:K0, 0:K0]).then_inc(S["e_xT"], 1)

            def e0_up(e, u, turn):
                v = u % 2
                pe.wait_ge(S[f"e_w{u}"], (turn + 1) * 64)
                pe.wait_ge(S["e_xTc"], e + 1)
                wait(pe, S["e_act"], (e - 1) * 3)
                for k, (a, n) in enumerate(F0C):
                    x = pe.matmul(bank(2 + v, n)[:, k * K0:(k + 1) * K0], wu0[u][:, a:a + n], xgT[v], start=True, stop=True)
                x.then_inc(S["e_up"], 1)

            def e0_down(e, u, turn):
                v = u % 2
                pe.wait_ge(S["e_act"], (e + 1) * 3)
                wait(pe, S["e_out"], e - 1)
                o = bank(4 + v, K0)[:, 0:C]
                for k, (a, n) in enumerate(F0C):
                    rows_ = n if k < 2 else n + 1
                    x = pe.matmul(o, act0[v][0:rows_, k, :], wd0[u][0:rows_, k, :], start=(k == 0), stop=(k == 2))
                x.then_inc(S["e_down"], 1)

            def ahead(e, u, turn, k, f, total):
                if not known(e) or e + k < total:
                    f(e + k, (u + k) % D, turn + (u + k) // D)

            def e0_step(e, u, turn):
                ahead(e, u, turn, 1, e0_up, E0)
                ahead(e, u, turn, 2, e0_turn, E0)
                e0_down(e, u, turn)

            pe.wait_ge(S["ones_in"], 1)
            e0_turn(0, 0, 0)
            e0_up(0, 0, 0)
            e0_turn(1, 1, 0)
            loop(pe, E0, D, D, e0_step, step=D)
            pe.wait_ge(S["e_out"], E0)

            def attention(tag, rope):
                a = lambda n: A[tag + n]
                nv = C // 2 if rope else C
                pe.wait_ge(a("x_in"), 1)
                turn(X if rope else X1, F32, ident[0:N, 0:N])
                pe.wait_ge(S["tile_moved"], moved[tag + "x"])
                pe.wait_ge(a("w_in"), 48 if rope else 64)
                for g in range(8):
                    k0 = tl.pe_open(pe)
                    for k in range(4):
                        b = 4 * g + k
                        x = pe.matmul(bank(k0, N)[:, k * nv:(k + 1) * nv], XT[:, b * N:(b + 1) * N],
                                      wraw[:, 2 * C:2 * C + nv], start=True, stop=True)
                    tl.pe_close(x)
                pe.wait_ge(a("wpad"), 19 if rope else 4)
                for c in range(8):
                    for k in range(4):
                        n = 4 * c + k
                        if n >= 2:
                            pe.wait_ge(a("rope") if rope else a("qk_c"), n - 1)
                        xc = XT[:, c * 4 * N:(c + 1) * 4 * N]
                        x = pe.matmul(bank(4 + 2 * (n % 2))[:, 0:4 * N], wpad[:, k, :], xc, start=True, stop=True)
                        if rope:
                            x = pe.matmul(bank(5 + 2 * (n % 2))[:, 0:4 * N], wpad[:, 4 + k, :], xc, start=True, stop=True)
                        x.then_inc(a("qk_mm"), 1)

                def scores(b, u, turn):
                    pe.wait_ge(a("q_c"), b + 1)
                    pe.wait_ge(a(f"k_in{u}"), (turn + 1) * 64)
                    wait(pe, a("sub"), b - 1)
                    for g in range(2):
                        o = bank(4 + 2 * u + g, N)[:, 0:4 * N]
                        if rope:
                            pe.matmul(o, identb[0:N, 0:N], causalb[:], start=True, stop=False)
                        x = pe.matmul(o, qs[u][:, g, :], kz[u][:, g, :], start=not rope, stop=True)
                    x.then_inc(a("sc"), 1)

                def turn_p(b, u):
                    pe.wait_ge(a("exp"), b + 1)
                    wait(pe, a("pTc"), b)
                    for h in range(NH):
                        o = 4 * (h % 2) + h // 2 if rope else h
                        x = pe.transpose(bank(2 + o // 4, N)[:, (o % 4) * N:(o % 4 + 1) * N], pr2[u][:, h, :], ident[0:N, 0:N])
                    x.then_inc(a("pT"), 1)

                def step(b, u, turn):
                    if not known(b) or b + 2 < B:
                        scores(b + 2, u, turn + 1)
                    if not known(b) or b + 1 < B:
                        turn_p(b + 1, 1 - u)
                    pe.wait_ge(a("pTc"), b + 1)
                    if rope:
                        wait(pe, a("o_c"), b)
                        rows8 = ptT[u].rearrange("p h t -> p (h t)").rearrange("p (n k) -> p k n", k=8)
                        for k in range(8):
                            x = pe.matmul(bank(k // 4, N)[:, (k % 4) * 128:(k % 4) * 128 + 65], rows8[:, k, :],
                                          V[:, bass.ds(b, 1), 0:65], start=True, stop=True)
                    else:
                        wait(pe, a("o_c"), b - 1)
                        for h in range(NH):
                            x = pe.matmul(bank(u, N)[:, h * VW:(h + 1) * VW], ptT[u][:, h, :],
                                          Vf[:, bass.ds(b, 1), h, :], start=True, stop=True)
                    x.then_inc(a("o"), 1)

                pe.wait_ge(a("qk_c"), 32)
                pe.wait_ge(S["tile_moved"], moved[tag + "v"])
                pe.wait_ge(a("ones"), 1)
                scores(0, 0, 0)
                scores(1, 1, 0)
                turn_p(0, 0)
                loop(pe, B, 2, 2, step, step=2)
                if not rope:
                    pe.wait_ge(a("o_c"), B)
                    turn(TMP, F32, ident[0:N, 0:N])
                    pe.wait_ge(S["tile_moved"], moved[tag + "o"])
                    for g in range(8):
                        if g >= 4:
                            pe.wait_ge(a("w_c"), g - 3)
                        for k in range(4):
                            b = 4 * g + k
                            x = pe.matmul(bank(4 + g % 4, N)[:, k * C:(k + 1) * C], XT[:, b * N:(b + 1) * N], wo, start=True, stop=True)
                        x.then_inc(a("w"), 1)

            attention("r", True)
            attention("f", False)

            pe.wait_ge(S["m_route"], 1)
            turn(X2, F32, ident[0:N, 0:N])
            pe.wait_ge(S["tile_moved"], moved["xt1"])
            for b in range(B):
                x = pe.matmul(bank(4 + b // 8, N)[:, (b % 8) * E1:(b % 8 + 1) * E1], XT[:, b * N:(b + 1) * N], wrt1[:],
                              start=True, stop=True)
            x.then_inc(S["m_lg"], 1)
            pe.wait_ge(S["m_m"], 1)
            for c in range(4):
                pe.matmul(bank(4 + c, N), trib[:], mb[:, 8 * c:8 * c + 8, :], start=True, stop=False)
                x = pe.matmul(bank(4 + c, N), onesb[:], cumb[:, 8 * c:8 * c + 8, :], start=False, stop=True)
            x.then_inc(S["m_cum"], 1)

            def e1_turn(e, u, turn):
                v = u % 2
                pe.wait_ge(S[f"m_x{u}"], (turn + 1) * 32)
                wait(pe, S["m_xTc"], e - 1)
                for k, (a, n) in enumerate(CAPT):
                    x = pe.transpose(bank(v)[:, a:a + n], xin[u][0:n, k, 0:C], ident[0:n, 0:n])
                x.then_inc(S["m_xT"], 1)

            def e1_up(e, u, turn):
                v = u % 2
                pe.wait_ge(S[f"m_w{u}"], (turn + 1) * 32)
                pe.wait_ge(S["m_xTc"], e + 1)
                wait(pe, S["m_act"], (e - 1) * NJ)
                w1k = w1[u].rearrange("p (f k) -> p k f", k=NJ)
                for k in range(NJ):
                    x = pe.matmul(bank(2 + 2 * v + k // 2)[:, (k % 2) * CAP:(k % 2 + 1) * CAP], w1k[:, k, :], xinT[v],
                                  start=True, stop=True)
                x.then_inc(S["m_up"], 1)

            def e1_step(e, u, turn):
                v = u % 2
                ahead(e, u, turn, 1, e1_up, E1)
                ahead(e, u, turn, 2, e1_turn, E1)
                pe.wait_ge(S["m_act"], (e + 1) * NJ)
                wait(pe, S["m_out"], e - 1)
                for k, (a, n) in enumerate(CAPT):
                    for j in range(NJ):
                        x = pe.matmul(bank(6 + v, n)[:, k * C:(k + 1) * C], hT[v][:, j, a:a + n], w2[u][:, j, :],
                                      start=(j == 0), stop=(j == NJ - 1))
                x.then_inc(S["m_down"], 1)

            e1_turn(0, 0, 0)
            e1_up(0, 0, 0)
            e1_turn(1, 1, 0)
            loop(pe, E1, D, D, e1_step, step=D)

        @block.scalar
        def _(act):
            tl = Tiles()
            copy = lambda o, i: act.activation(o, i, ACT.Copy)
            act.wait_ge(S["small_in"], 80)
            for g in range(2):
                k0 = tl.act_open(act)
                tl.act_close(copy(wtokT[:, 3 * g:3 * g + 3, :], bank(k0)[:, 0:384].rearrange("p (k e) -> p k e", k=3)))
            k0 = tl.act_open(act)
            tl.act_close(copy(wres[:, 0, :], bank(k0)))
            for t in range(2):
                for k in range(KT):
                    for half in range(2):
                        k0 = tl.act_open(act)
                        at_ = t * 576 + half * 288
                        tl.act_close(copy(patT[:, k, at_:at_ + 288], bank(k0)[:, 0:288]))
            ev = embT.rearrange("p (t b h w) -> p t w h b", t=2, w=HP, h=HP)
            for g in range(4):
                k0 = tl.act_open(act)
                t, half = g // 2, g % 2
                tl.act_close(act.activation(ev[:, t, 3 * half:3 * half + 3],
                                            bank(k0)[:, 0:288].rearrange("p (w h b) -> p w h b", w=3, h=HP),
                                            ACT.Identity, bias=tokb[:, 0:1]))
            for g in range(8):
                k0 = tl.act_open(act)
                tl.act_close(copy(H[0:NI, 4 * g:4 * g + 4, :], bank(k0, NI).rearrange("p (k c) -> p k c", k=4)))

            lnn = [0]

            def ln_help():
                lnn[0] += 1
                act.wait_ge(S["ln_centred"], lnn[0])
                act.activation(TMP[:], lnsrc[0], ACT.Square).then_inc(S["ln_squared"], 1)
                act.wait_ge(S["ln_var"], lnn[0])
                act.activation(stat[:, 3, :], stat[:, 2, :], ACT.Sqrt).then_inc(S["ln_std"], 1)

            lnsrc = [X[:]]
            ln_help()
            act.wait_ge(S["spk_relu"], 1)
            act.activation(TMP[:], X[:], ACT.Relu, scale=NUDGE).then_inc(S["act"], 1)

            def untile(dst):
                for g in range(8):
                    k0 = tl.act_open(act)
                    if dst.dtype == BF16:
                        src = bank(k0).bitcast(BF16)[:, 0:4 * (N + 1)].rearrange("p (k t) -> p k t", k=4)[:, :, 0:N]
                        o = dst[:, 4 * g * N:(4 * g + 4) * N].rearrange("p (k t) -> p k t", k=4)
                    else:
                        src, o = bank(k0)[:, 0:4 * N], dst[:, 4 * g * N:(4 * g + 4) * N]
                    tl.act_close(copy(o, src))

            act.wait_ge(S["y0_zero"], 64)
            untile(xst)
            for j in range(3):
                act.wait_ge(S["qkv_stats"], 2 * j + 1)
                act.activation(bnag[:, 3:4], bnag[:, 2:3], ACT.Sqrt).then_inc(S["qkv_std"], 1)
                act.wait_ge(S["qkv_stats"], 2 * j + 2)
                if j == 2:
                    act.wait_ge(S["qm_ready"], 1)
                for c in range(8):
                    act.activation(rf[j % 2][:, c * 4 * N:(c + 1) * 4 * N], bank(c)[:, 0:4 * N], ACT.Relu,
                                   bias=bnag[:, 6:7], scale=bnag[:, 5:6]).then_inc(S["qkv_moved"], 1)
            for g in range(8):
                k0 = tl.act_open(act)
                tl.act_close(copy(vtok[:, 4 * g:4 * g + 4, :],
                                  bank(k0, N).bitcast(BF16)[:, 0:512].rearrange("p (k c) -> p k c", k=4)))

            def spk_out(b, u, _turn):
                act.wait_ge(S["o_ready"], b + 1)
                act.activation(TMP[:, bass.ds(b, 1), :], bank(4 + u, N)[:, 0:C].unsqueeze(1), ACT.Relu,
                               scale=NUDGE * float(HD) ** -0.5).then_inc(S["o_moved"], 1)

            loop(act, B, 2, 2, spk_out, step=2)
            untile(ost)

            ln_help()
            untile(XT[:])
            act.wait_ge(S["lg_sub"], 1)
            act.activation(lg, lg, ACT.Exp).then_inc(S["lg_exp"], 1)
            k0 = tl.act_open(act)
            tl.act_close(copy(posi, bank(k0, K0)[:, 0:E0]))
            k0 = tl.act_open(act)
            tl.act_close(copy(gate, bank(k0, K0)[:, 0:E0]))
            k0 = tl.act_open(act)
            copy(bupT[:, 0:2, :], bank(k0)[:, 0:16].rearrange("p (k g) -> p k g", k=2))
            tl.act_close(copy(bupT[0:F0 - 256, 2, :], bank(k0, F0 - 256)[:, 16:24]))

            k0 = tl.act_open(act)
            tl.act_close(copy(b1T, bank(k0)[:, 0:NJ * E1].rearrange("p (k e) -> p k e", k=NJ)))

            def gather_waits(i):
                copy(idle[0:1, i:i + 1], cst[0:1, 0:1])

            def e0_silu(e, u, turn):
                v = u % 2
                act.wait_ge(S["e_up"], e + 1)
                wait(act, S["e_down"], e - 1)
                gather_waits(v)
                g = e // GRP if known(e) else turn
                for k, (a, n) in enumerate(F0C):
                    act.activation(act0[v][0:n, k, :], bank(2 + v, n)[:, k * K0:(k + 1) * K0], ACT.Silu,
                                   bias=bupT[0:n, k, bass.ds(g, 1)]).then_inc(S["e_act"], 1)

            act.wait_ge(S["ones_in"], 1)
            loop(act, E0, D, 0, e0_silu, step=D)

            ln_help()

            def attention(tag, rope):
                a = lambda n: A[tag + n]
                nv = C // 2 if rope else C
                untile(XT)
                for g in range(8):
                    k0 = tl.act_open(act)
                    if rope:
                        tl.act_close(copy(V[:, 4 * g:4 * g + 4, 0:nv], bank(k0, N)[:, 0:4 * nv].rearrange("p (k c) -> p k c", k=4)))
                    else:
                        tl.act_close(copy(Vf[:, 4 * g:4 * g + 4, :, 0:HD],
                                          bank(k0, N).rearrange("p (k h d) -> p k h d", k=4, h=NH)))
                if not rope:
                    for n in range(32):
                        act.wait_ge(a("qk_mm"), n + 1)
                        copy(QK[:, n % 4, (n // 4) * 4 * N:(n // 4 + 1) * 4 * N], bank(4 + 2 * (n % 2))[:, 0:4 * N])\
                            .then_inc(a("qk_c"), 1)

                def step(b, u, _turn):
                    act.wait_ge(a("sub"), b + 1)
                    wait(act, a("pT"), b - 1)
                    act.activation(pr2[u], s2[u], ACT.Exp, scale=float(HD) ** -0.5).then_inc(a("exp"), 1)
                    act.wait_ge(a("pT"), b + 1)
                    wait(act, a("o"), b - 1)
                    copy(ptT[u].rearrange("p (a i) t -> p a (i t)", a=2), ps[0:N, 2:4, 0:4 * N]).then_inc(a("pTc"), 1)

                loop(act, B, 2, 2, step, step=2)
                if not rope:
                    untile(XT)

            attention("r", True)
            ln_help()
            lnsrc[0] = X1
            ln_help()
            attention("f", False)
            lnsrc[0] = X2
            ln_help()
            untile(XT[:])
            act.wait_ge(S["m_max"], 1)
            act.activation(lg1, lg1, ACT.Exp).then_inc(S["m_exp"], 1)

            def e1_gelu(e, u, turn):
                v = u % 2
                act.wait_ge(S["m_up"], e + 1)
                wait(act, S["m_down"], e - 1)
                gather_waits(2 + v)
                for k in range(NJ):
                    act.activation(hT[v][:, k, :], bank(2 + 2 * v + k // 2)[:, (k % 2) * CAP:(k % 2 + 1) * CAP],
                                   ACT.Gelu_apprx_tanh, bias=b1T[:, k, bass.ds(e, 1)]).then_inc(S["m_act"], 1)

            loop(act, E1, 2, 0, e1_gelu, step=2)

        @block.vector
        def _(dve):
            ch = Chain(dve, S["dve"])
            link = ch.link
            tt, ts, stt = dve.tensor_tensor, dve.tensor_scalar, dve.scalar_tensor_tensor

            dve.memset(XT[:], 0.0).then_inc(S["zeroed"], 1)
            link(dve.memset(zrow, 0.0))
            dve.wait_ge(S["cst_in"], 16)
            dve.tensor_copy(zrowi[:, :, C], const("dump")).then_inc(S["zrow_ready"], 1)
            link(dve.tensor_copy(identb[:], ident))
            link(dve.tensor_copy(trib[:], const("tri", N)))
            link(dve.tensor_copy(onesb[:], const("ones", N)[:, 0:N]))
            dve.tensor_copy(causalb[:], const("causal", N)).then_inc(S["consts_ready"], 1)

            dve.wait_ge(S["img_in"], 16 * 12)
            for t in range(2):
                dve.tensor_copy(imgp[t].rearrange("p w r x -> p r w x"),
                                img[t].rearrange("p c h (w x) -> p (c h) w x", x=PS)).then_inc(S["img_packed"], 1)

            dve.wait_ge(S["tile_moved"], moved["w"])
            link(dve.tensor_copy(wsplit[:, 0, :], wres[:, 0, :]))
            link(tt(wres[:, 1, :], wres[:, 0, :], wsplit[:, 0, :], ALU.subtract))
            link(dve.tensor_copy(wsplit[:, 1, :], wres[:, 1, :]))
            link(tt(wres[:, 0, :], wres[:, 1, :], wsplit[:, 1, :], ALU.subtract))
            dve.tensor_copy(wsplit[:, 2, :], wres[:, 0, :]).then_inc(S["w_split"], 1)

            lnn = [0]

            def layernorm(src, dst, gain=None):
                link(dve.tensor_reduce(stat[:, 0, :], src, AXX, ALU.add))
                link(ts(stat[:, 1, :], stat[:, 0, :], 1.0 / C, None, ALU.mult))
                tt(dst, src, bcol(stat[:, 1, :], C), ALU.subtract).then_inc(S["ln_centred"], 1)
                lnn[0] += 1
                dve.wait_ge(S["ln_squared"], lnn[0])
                link(dve.tensor_reduce(stat[:, 4, :], TMP[:], AXX, ALU.add))
                ts(stat[:, 2, :], stat[:, 4, :], 1.0 / C, EPS, ALU.mult, ALU.add).then_inc(S["ln_var"], 1)
                dve.wait_ge(S["ln_std"], lnn[0])
                link(dve.reciprocal(stat[:, 5, :], stat[:, 3, :]))
                dve.wait_ge(S["ln_centred"], lnn[0])
                last = tt(dst, dst, bcol(stat[:, 5, :], C), ALU.mult)
                if gain is not None:
                    link(last)
                    link(tt(dst, dst, brow(rows[:, gain, :], B), ALU.mult))
                    last = tt(dst, dst, brow(rows[:, gain + 1, :], B), ALU.add)
                return last

            dve.wait_ge(S["tile_moved"], moved["H"])
            dve.wait_ge(S["txt_in"], 16)
            layernorm(H[:], X[:]).then_inc(S["spk_relu"], 1)
            dve.wait_ge(S["act"], 1)

            def spikes(dst, src):
                link(ts(src, src, 4.0, FLOOR, ALU.min, ALU.add))
                return ts(dst, src, FLOOR, None, ALU.subtract)

            spikes(xsb, TMP[:]).then_inc(S["spk_ready"], 1)
            dve.wait_ge(S["small_in"], 80)
            for j in range(3):
                for c in range(8):
                    dve.wait_ge(S["qkv_ready"], 8 * j + c + 1)
                    link(dve.bn_stats(bnst[:, c, :], bank(c)[:, 0:4 * N]))
                if j:
                    dve.wait_ge(S["qkv_moved"], 8 * j)
                link(dve.bn_aggr(bnag[:, 0:2], bnst[:].rearrange("p a b -> p (a b)")))
                ts(bnag[:, 2:3], bnag[:, 1:2], EPS, None, ALU.add).then_inc(S["qkv_stats"], 1)
                dve.wait_ge(S["qkv_std"], j + 1)
                link(dve.reciprocal(bnag[:, 4:5], bnag[:, 3:4]))
                link(ts(bnag[:, 5:6], bnag[:, 4:5], gb[:, j:j + 1], NUDGE, ALU.mult, ALU.mult))
                link(tt(bnag[:, 7:8], bnag[:, 0:1], bnag[:, 5:6], ALU.mult))
                stt(out=bnag[:, 6:7], in0=gb[:, 3 + j:4 + j], scalar=NUDGE, in1=bnag[:, 7:8],
                    op0=ALU.mult, op1=ALU.subtract).then_inc(S["qkv_stats"], 1)
                if j:
                    spikes(qkvb[:, j - 1, :], rf[(j - 1) % 2]).then_inc(S["qm_ready"], 1)
            dve.wait_ge(S["qkv_moved"], 24)
            spikes(qkvb[:, 2, :], rf[0]).then_inc(S["qm_ready"], 1)
            dve.wait_ge(S["tile_moved"], moved["xs"])
            dve.wait_ge(S["qm_ready"], 3)
            for h in range(NH):
                a_ = CONST["headmask"][0] + h
                last = ts(qm[:, h, :], qkvb[:, 0, :], cst[:, a_:a_ + 1], None, ALU.mult)
            last.then_inc(S["qm_ready"], 1)

            def spk_a(b, u, _turn):
                dve.wait_ge(S["sT_ready"], b + 1)
                wait(dve, S["o_ready"], b - 1)
                ts(aspk[:, u, :].rearrange("p (g x) -> p g x", g=2), ps[0:N, 2 * u:2 * u + 2, 0:4 * N],
                   4.0, None, ALU.min).then_inc(S["a_ready"], 1)

            loop(dve, B, 2, 2, spk_a, step=2)
            dve.wait_ge(S["o_moved"], B)
            spikes(osb, TMP[:]).then_inc(S["ob_ready"], 1)
            dve.wait_ge(S["rows_in"], 112)
            link(tt(H[:], H[:], brow(rows[:, 0, :], B), ALU.add))
            for g in range(8):
                dve.wait_ge(S["proj_ready"], g + 1)
                tt(H[:, 4 * g:4 * g + 4, :], H[:, 4 * g:4 * g + 4, :],
                   bank(4 + g % 4, N).rearrange("p (k c) -> p k c", k=4), ALU.add).then_inc(S["proj_added"], 1)
            dve.wait_ge(S["proj_added"], 8)

            layernorm(H[:], X[:]).then_inc(S["x0_ready"], 1)
            dve.wait_ge(S["lg_ready"], 1)
            link(tt(lg, ps[0:N, 4:6, :].rearrange("p a (b e) -> p (a b) e", e=E0), brow(rbias[:], B), ALU.add))
            link(dve.tensor_reduce(stat[:, 6, :], lg, AXX, ALU.max))
            tt(lg, lg, bcol(stat[:, 6, :], E0), ALU.subtract).then_inc(S["lg_sub"], 1)
            dve.wait_ge(S["lg_exp"], 1)
            link(dve.tensor_reduce(stat[:, 6, :], lg, AXX, ALU.add))
            link(dve.reciprocal(stat[:, 7, :], stat[:, 6, :]))
            tt(pr.rearrange("p j q e -> p q j e"), lg.rearrange("p (q j) e -> p q j e", q=Q0),
               stat[:, 7, :].rearrange("p (q j) -> p q j", q=Q0).unsqueeze(3).broadcast_to([N, Q0, B // Q0, E0]), ALU.mult).then_inc(S["pr_ready"], 1)
            dve.wait_ge(S["lg_ready"], 2)
            link(dve.tensor_copy(sc.rearrange("p (a x) -> p a x", a=2), ps[:, 6:8, 0:4 * N]))
            for r in range(R8):
                v8, i8 = cv[:, 8 * r:8 * r + 8], ci[:, 8 * r:8 * r + 8]
                link(dve.max(v8, sc))
                link(dve.max_index(i8, v8, sc))
                link(dve.match_replace(sc, v8, sc, -1.0))
            link(dve.tensor_copy(cif, ci))
            link(ts(cif, cif, const("quarter"), None, ALU.add))
            dve.tensor_copy(cii, cif).then_inc(S["cand_ready"], 1)
            dve.wait_ge(S["vm_in"], 64)
            for r in range(R8):
                v8, i8 = gv[:, 8 * r:8 * r + 8], gp[:, 8 * r:8 * r + 8]
                link(dve.max(v8, vm))
                link(dve.max_index(i8, v8, vm))
                link(dve.match_replace(vm, v8, vm, -1.0))
            link(dve.tensor_copy(gpf, gp))
            ts(gpf, gpf, const("expert", E0), None, ALU.add).then_inc(S["gp_ready"], 1)
            dve.wait_ge(S["tile_moved"], moved["gT"])

            link(dve.memset(act0[0][64:128, 2, :], 1.0))
            dve.memset(act0[1][64:128, 2, :], 1.0).then_inc(S["ones_in"], 1)

            def e0_move(e, u, turn):
                v = u % 2
                dve.wait_ge(S["e_xT"], e + 1)
                wait(dve, S["e_up"], e - 1)
                dve.tensor_copy(xgT[v], bank(v)[:, 0:K0]).then_inc(S["e_xTc"], 1)

            def e0_out(e, u, turn):
                if not known(e) or e + 2 < E0:
                    e0_move(e + 2, (u + 2) % D, None)
                dve.wait_ge(S["e_down"], e + 1)
                wait(dve, S[f"e_sc{u % 2}"], (e // 2 - 1) * 16 if known(e) else (turn * 2 + (u // 2 - 1)) * 16)
                ts(yo0[u], bank(4 + u % 2, K0)[:, 0:C], gate[:, bass.ds(e, 1)], None, ALU.mult).then_inc(S["e_out"], 1)

            e0_move(0, 0, None)
            e0_move(1, 1, None)
            loop(dve, E0, D, D, e0_out, step=D)
            dve.wait_ge(S["y0_in"], 64)
            link(tt(H[:], H[:], TMP[:], ALU.add))

            def attention(tag, rope):
                a = lambda n: A[tag + n]
                if rope:
                    for n in range(32):
                        k, u = n % 4, n % 2
                        dve.wait_ge(a("qk_mm"), n + 1)
                        if n >= 2:
                            dve.wait_ge(a("qk_c"), n - 1)
                        for s_, nm in enumerate(("rope_c", "rope_s")):
                            x = tt(rt[u][:, s_, :].rearrange("p (b t) -> p b t", b=4),
                                   bank(4 + 2 * u + s_)[:, 0:4 * N].rearrange("p (b t) -> p b t", b=4),
                                   brow(const(nm)[:, k * N:(k + 1) * N], 4), ALU.mult)
                        x.then_inc(a("rope"), 1)

                def finish(b, u):
                    dve.wait_ge(a("o"), b + 1)
                    if rope:
                        o8 = ps[0:N, 0:2, :].rearrange("p a (k x) -> p (a k) x", k=4)
                        dve.reciprocal(rrec[u].unsqueeze(2), o8[:, :, 64:65]).then_inc(a("rec"), 1)
                        dve.wait_ge(a("rec"), b + 1)
                        tt(mg, const("regroup", N).rearrange("p (k g) -> p k g", g=4), bcol(rrec[u], 4), ALU.mult)\
                            .then_inc(a("mask"), 1)
                        dve.wait_ge(a("mask"), b + 1)
                        tt(og, o8[:, :, 0:64].rearrange("p k (g d) -> p k g d", g=4),
                           mg.unsqueeze(3).broadcast_to([N, 8, 4, HD]), ALU.mult).then_inc(a("group"), 1)
                        dve.wait_ge(a("group"), b + 1)
                        dve.tensor_reduce(TMP[:, bass.ds(b, 1), :].rearrange("p b (k d) -> p (b k) d", k=8),
                                          og.rearrange("p k g d -> p k d g"), AXX, ALU.add).then_inc(a("o_c"), 1)
                    else:
                        o = bank(u, N)[:, 0:NH * VW].rearrange("p (h d) -> p h d", h=NH)
                        dve.reciprocal(rrec[u].unsqueeze(2), o[:, :, HD:VW]).then_inc(a("rec"), 1)
                        dve.wait_ge(a("rec"), b + 1)
                        tt(TMP[:, bass.ds(b, 1), :].rearrange("p b (h d) -> p (b h) d", h=NH), o[:, :, 0:HD],
                           rrec[u].unsqueeze(2).broadcast_to([N, NH, HD]), ALU.mult).then_inc(a("o_c"), 1)

                def step(b, u, _turn):
                    if not known(b) or b < B:
                        dve.wait_ge(a("sc"), b + 1)
                        scv = ps[0:N, 4 + 2 * u:6 + 2 * u, 0:4 * N].rearrange("p g (j t) -> p g j t", j=4)
                        dve.tensor_reduce(nmx[u].rearrange("p (g j) -> p g j", g=2), scv, AXX, ALU.max).then_inc(a("max"), 1)
                        dve.wait_ge(a("max"), b + 1)
                        wait(dve, a("exp"), b - 1)
                        mv = nmx[u].rearrange("p (g j) -> p g j", g=2).unsqueeze(3).broadcast_to([N, 2, 4, N])
                        tt(s2[u].rearrange("p (g j) t -> p g j t", g=2), scv, mv, ALU.subtract).then_inc(a("sub"), 1)
                    if not known(b) or b >= 2:
                        finish(b - 2, u)

                loop(dve, B, 2, 2, step, step=2)
                step(B, 0, None)
                step(B + 1, 1, None)
                dve.wait_ge(a("o_c"), B)
                if rope:
                    link(tt(H[:], H[:], TMP[:], ALU.add))
                else:
                    for g in range(8):
                        dve.wait_ge(a("w"), g + 1)
                        tt(X[:, 4 * g:4 * g + 4, :], X[:, 4 * g:4 * g + 4, :],
                           bank(4 + g % 4, N).rearrange("p (k c) -> p k c", k=4), ALU.add).then_inc(a("w_c"), 1)
                    dve.wait_ge(a("w_c"), 8)

            layernorm(H[:], X[:]).then_inc(A["rx_in"], 1)
            attention("r", True)
            link(layernorm(H[:], X[:]))
            layernorm(X[:], X1, gain=1).then_inc(A["fx_in"], 1)
            attention("f", False)

            layernorm(X[:], X2, gain=3).then_inc(S["m_route"], 1)
            dve.wait_ge(S["m_lg"], 1)
            link(dve.tensor_copy(lg1, ps[0:N, 4:8, :].rearrange("p a (b e) -> p (a b) e", e=E1)))
            link(dve.tensor_reduce(stat[:, 6, :], lg1, AXX, ALU.max))
            tt(lg1, lg1, bcol(stat[:, 6, :], E1), ALU.subtract).then_inc(S["m_max"], 1)
            dve.wait_ge(S["m_exp"], 1)
            link(dve.tensor_reduce(stat[:, 6, :], lg1, AXX, ALU.add))
            link(dve.reciprocal(stat[:, 7, :], stat[:, 6, :]))
            link(tt(pr1, lg1, bcol(stat[:, 7, :], E1), ALU.mult))
            for b in range(B):
                link(dve.max(mx8[:, b, :], pr1[:, b, :]))
                last = dve.max_index(ix8[:, b, :], mx8[:, b, :], pr1[:, b, :])
            link(last)
            link(dve.tensor_copy(ef, ix8))
            iota = brow(const("iota", N), B)
            for k in range(2):
                link(tt(oh[k], iota, bcol(ef[:, :, k], E1), ALU.is_equal))
            link(tt(mb, oh[0], oh[1], ALU.add))
            link(dve.memset(cumb[:, 0:1, :], 0.0))

            for b in range(B - 1):
                link(tt(cumb[:, b + 1, :], cumb[:, b, :], mb[:, b, :], ALU.add))
            link(tt(route[:, 0, :], mx8[:, :, 0], mx8[:, :, 1], ALU.add))
            dve.reciprocal(route[:, 1, :], route[:, 0, :]).then_inc(S["m_m"], 1)
            dve.wait_ge(S["m_m"], 1)
            dve.wait_ge(S["m_cum"], 1)
            cum = ps[0:N, 4:8, :].rearrange("p a (b e) -> p (a b) e", e=E1)
            for k in range(2):
                link(tt(oh[k], cum, oh[k], ALU.mult))
                link(dve.tensor_reduce(route[:, 2, :], oh[k], AXX, ALU.add))
                link(ts(route[:, 3, :], route[:, 2, :], float(CAP), None, ALU.is_lt))
                link(ts(route[:, 4, :], route[:, 2, :], float(CAP - 1), None, ALU.min))
                link(stt(out=route[:, 5, :], in0=ef[:, :, k], scalar=float(CAP), in1=route[:, 4, :], op0=ALU.mult, op1=ALU.add))
                
                link(ts(route[:, 6, :], route[:, 3, :], -float(S1), float(S1), ALU.mult, ALU.add))
                link(tt(route[:, 5, :], route[:, 5, :], route[:, 6, :], ALU.add))
                link(dve.tensor_copy(sidx[:, k, :], route[:, 5, :]))
                link(tt(route[:, 7, :], mx8[:, :, k], route[:, 1, :], ALU.mult))
                link(tt(gk[:, k, :], route[:, 7, :], route[:, 3, :], ALU.mult))
            link(dve.tensor_copy(X2i[:, :, C], const("token", N)))
            dve.tensor_copy(X2r[:, :, C + 1], gk[:, 0, :]).then_inc(S["m_rows"], 1)
            tt(H[:], H[:], X[:], ALU.add).then_inc(S["m_sidx"], 1)

            dve.wait_ge(S["m_scat0"], 16 * B)
            dve.tensor_copy(X2r[:, :, C + 1], gk[:, 1, :]).then_inc(S["m_rows"], 1)
            dve.wait_ge(S["b2_in"], 16)

            def e1_move(e, u, turn):
                dve.wait_ge(S["m_xT"], e + 1)
                wait(dve, S["m_up"], e - 1)
                dve.tensor_copy(xinT[u % 2], bank(u % 2)[:, 0:CAP]).then_inc(S["m_xTc"], 1)

            def e1_out(e, u, turn):
                if not known(e) or e + 2 < E1:
                    e1_move(e + 2, u + 2, None)
                dve.wait_ge(S["m_down"], e + 1)
                for k in range(2):
                    wait(dve, S[f"m_sc{k}"], (e - D + 1) * 16)
                for k, (a, n) in enumerate(CAPT):
                    tt(yo1[u][0:n, k, :], bank(6 + u % 2, n)[:, k * C:(k + 1) * C], b2[0:n, bass.ds(e * C, C)], ALU.add)\
                        .then_inc(S["m_biased"], 1)
                dve.wait_ge(S["m_biased"], e * 2 + 2)
                for k, (a, n) in enumerate(CAPT):
                    x = ts(yo1[u][0:n, k, :], yo1[u][0:n, k, :], xin[u][0:n, k, C + 1:C + 2], None, ALU.mult)
                x.then_inc(S["m_out"], 1)

            e1_move(0, 0, None)
            e1_move(1, 1, None)
            loop(dve, E1, D, D, e1_out, step=D)

            for i in range(4):
                q = T // 4
                dve.wait_ge(S[f"fin_in{i}"], 32)
                tt(XT[:, i * q:(i + 1) * q], XT[:, i * q:(i + 1) * q], fsum[:, i * q:(i + 1) * q], ALU.add)\
                    .then_inc(S["fin_ready"], 1)

        @block.gpsimd
        def _(pool):
            off = lambda ap: bass.IndirectOffsetOnAxis(ap=ap, axis=0)
            pool.wait_ge(S["cand_out"], 64)
            pool.wait_ge(S["tile_moved"], moved["gT"])
            def lookup(e):
                pool.indirect_dma_start(itok[:, e:e + 1], None, d_cand, off(posi[:, e:e + 1])).then_inc(S[f"itok_in{e % D}"], 16)

            def gather(e):
                pool.wait_ge(S[f"itok_in{e % D}"], 16 * (e // D + 1))
                if e >= D:
                    pool.wait_ge(S["e_xT"], e - D + 1)
                pool.indirect_dma_start(xg[e % D], None, d_x0, off(itok[:, e:e + 1])).then_inc(S[f"g_in{e % D}"], 16)

            for e in range(D):
                lookup(e)
            pool.wait_ge(S["x0_out"], 32)
            pool.wait_ge(S["h_out"], 32)
            pool.wait_ge(S["y0_zero"], 64)
            for e in range(E0 + 2):
                if e < E0:
                    gather(e)
                    if e + D < E0:
                        lookup(e + D)
                if e >= 2:
                    f = e - 2
                    pool.wait_ge(S["e_out"], f + 1)
                    if f >= 2:
                        pool.wait_ge(S[f"e_sc{f % 2}"], 16 * (f // 2))
                    pool.indirect_dma_start(d_y0[f % 2], off(itok[:, f:f + 1]), yo0[f % D], None, compute_op=ALU.add)\
                        .then_inc(S[f"e_sc{f % 2}"], 16)

            def attention(tag, rope):
                a = lambda n: A[tag + n]
                pool.wait_ge(a("w_in"), 48 if rope else 64)
                n = [0]

                def put(dst, src):
                    n[0] += 1
                    pool.tensor_copy(dst, src).then_inc(a("wpad"), 1)

                if rope:
                    n[0] += 1
                    pool.memset(wpad, 0.0).then_inc(a("wpad"), 1)
                    pool.wait_ge(a("wpad"), 1)
                wq = wraw[:, 0:C].rearrange("p (g j d) -> p g j d", g=2, j=4)
                for g in range(2):
                    dst = wpad[:, g, :].rearrange("p (j d) -> p j d", j=4)
                    put(dst[:, :, 0:HD], wq[:, g])
                    if rope:
                        d2 = wpad[:, 4 + g, :].rearrange("p (j d e) -> p j d e", j=4, e=2)
                        s2_ = wq[:, g].rearrange("p j (d e) -> p j d e", e=2)
                        for par in range(2):
                            put(d2[:, :, 0:HD // 2, par], s2_[:, :, :, 1 - par])
                if not rope:
                    wk = wraw[:, C:2 * C].rearrange("p (g j d) -> p g j d", g=2, j=4)
                    for g in range(2):
                        put(wpad[:, 2 + g, :].rearrange("p (j d) -> p j d", j=4)[:, :, 0:HD], wk[:, g])
                else:
                    wk = wraw[:, C:C + C // 2].rearrange("p (g j d) -> p g j d", g=2, j=2)
                    for g in range(2):
                        for two in range(2):
                            dst = wpad[:, 2 + g, :].rearrange("p (j t d) -> p j t d", j=2, t=2)[:, :, two, :]
                            put(dst[:, :, 0:HD], wk[:, g])
                            d2 = wpad[:, 6 + g, :].rearrange("p (j t d e) -> p j t d e", j=2, t=2, e=2)[:, :, two]
                            s2_ = wk[:, g].rearrange("p j (d e) -> p j d e", e=2)
                            for par in range(2):
                                put(d2[:, :, 0:HD // 2, par], s2_[:, :, :, 1 - par])
                assert n[0] == (19 if rope else 4)
                if rope:
                    for n in range(32):
                        u = n % 2
                        pool.wait_ge(a("rope"), n + 1)
                        pool.tensor_tensor(QK[:, n % 4, (n // 4) * 4 * N:(n // 4 + 1) * 4 * N], rt[u][:, 0, :], rt[u][:, 1, :],
                                           ALU.add).then_inc(a("qk_c"), 1)
                    pool.memset(V[:, :, 64:65], 1.0).then_inc(a("ones"), 1)
                    pool.wait_ge(a("qk_c"), 32)
                    for u in range(2):
                        pool.memset(kz[u], 0.0).then_inc(a("kz"), 1)
                else:
                    pool.wait_ge(A["ro_c"], B)
                    pool.memset(Vf[:, :, :, HD:VW], 1.0).then_inc(a("ones"), 1)
                pool.wait_ge(a("qk_c"), 32)

                def step(b, u, _turn):
                    wait(pool, a("sc"), b - 1)
                    pool.tensor_copy(qs[u], QK[:, 0:2, bass.ds(b * N, N)]).then_inc(a("q_c"), 1)

                loop(pool, B, 2, 2, step, step=2)

            attention("r", True)
            attention("f", False)

            pool.wait_ge(S["buf_zeroed"], 32)
            for k in range(2):
                pool.wait_ge(S["m_rows"], k + 1)
                for b in range(B):
                    pool.indirect_dma_start(d_buf, off(sidx[:, k, b:b + 1]), X2r[:, b, :], None,
                                            bounds_check=S1 - 1, oob_is_err=False).then_inc(S[f"m_scat{k}"], 16)
            pool.wait_ge(S["acc_in"], 32)
            for e in range(E1):
                pool.wait_ge(S["m_out"], e + 1)
                for k, (a, n) in enumerate(CAPT):
                    if e:
                        pool.wait_ge(S[f"m_sc{k}"], 16 * e)
                    pool.indirect_dma_start(d_acc[k], off(xini[e % D][0:n, k, C:C + 1]), yo1[e % D][0:n, k, :], None,
                                            compute_op=ALU.add).then_inc(S[f"m_sc{k}"], 16)


_INS = ["x", "txt", "L0_tok_w", "L0_tok_b", "L0_attn_Wqkv", "L0_attn_gamma", "L0_attn_beta", "L0_attn_Wproj",
        "L0_attn_bproj", "L0_ffn_W_router", "L0_ffn_b_router", "L0_ffn_W_up", "L0_ffn_b_up", "L0_ffn_W_down",
        "L0_ffn_b_down", "L1_attn_Wq", "L1_attn_Wk", "L1_attn_Wv", "L1_ffn_ln1_g", "L1_ffn_ln1_b", "L1_ffn_wq",
        "L1_ffn_wk", "L1_ffn_wv", "L1_ffn_wo", "L1_ffn_ln2_g", "L1_ffn_ln2_b", "L1_ffn_wr", "L1_ffn_w1",
        "L1_ffn_b1", "L1_ffn_w2", "L1_ffn_b2"]


def kernel(**inputs):
    import numpy as _np
    import concourse.bacc as _bacc
    from concourse import mybir as _mybir
    from concourse.bass_utils import run_bass_kernel_spmd as _run

    nc = _bacc.Bacc("TRN2", target_bir_lowering=False, num_devices=1)
    arrays, aps = {}, {}
    for name in _INS:
        a = _np.ascontiguousarray(inputs[name])
        arrays[f"in_{name}"] = a
        aps[name] = nc.dram_tensor(f"in_{name}", a.shape, _mybir.dt.from_np(a.dtype), kind="ExternalInput").ap()
    arrays["consts"] = shape_constants()
    consts = nc.dram_tensor("consts", [128, NCONST], _mybir.dt.float32, kind="ExternalInput").ap()
    out = nc.dram_tensor("out", [B, N, C], _mybir.dt.float32, kind="ExternalOutput").ap()
    program(nc, aps, out, consts)
    r = _run(nc, [arrays], core_ids=[0])
    return r.results[0]["out"]
```

```python
from contextlib import ExitStack

import numpy as np

import concourse.bass as bass
from concourse import mybir

ALU = mybir.AluOpType
ACT = mybir.ActivationFunctionType
AXX = mybir.AxisListType.X
F32 = mybir.dt.float32
BF16 = mybir.dt.bfloat16
U32 = mybir.dt.uint32
I32 = mybir.dt.int32

B = 32
NI, NT = 36, 77
N = NI + NT
C = 128
T = B * N
HP = 6
PS = 16
W = HP * PS
KT = 6
NH, HD = 8, 16
EPS = 1e-5

E0, GRP, F0 = 32, 4, 341
K0 = T // E0
Q0 = 4
LQ = T // Q0
R8 = -(-K0 // 8)
CQ = R8 * 8
F0C = [(0, 128), (128, 128), (256, F0 - 256)]

E1, F1 = 64, 512
CAP = 2 * (T * 2 // E1)
S1 = E1 * CAP
D = 4
DX = 2 * D
R1 = C + 2
CAPT = [(0, 128), (128, CAP - 128)]
NJ = F1 // 128

FLOOR = 8388608.0
NUDGE = 1.0 + 2.0 ** -23
NEG = -1e30
SPLIT = 112

CONST = {}
_at = 0
for _name, _w in (("ident", 128), ("tri", N), ("ones", 128), ("causal", 4 * N), ("headmask", NH),
                  ("rope_c", 3 * N), ("rope_s", 3 * N), ("quarter", 1), ("expert", 1), ("iota", E1), ("regroup", NH * 4), ("token", 2 * B)):
    CONST[_name] = (_at, _w)
    _at += _w
NCONST = _at


def shape_constants():
    c = np.zeros((128, NCONST), np.float32)

    def put(name, value):
        a, w = CONST[name]
        value = np.asarray(value, np.float32)
        c[:value.shape[0], a:a + w] = value.reshape(value.shape[0], w)

    p = np.arange(128)
    put("ident", np.eye(128))
    put("tri", p[:N, None] < np.arange(N)[None, :])
    put("ones", np.ones((128, 128)))
    put("causal", np.tile(np.where(np.arange(N)[None, :] > p[:N, None], NEG, 0.0), (1, 4)))
    put("headmask", p[:, None] // HD == np.arange(NH)[None, :])
    put("quarter", (p // E0 * LQ)[:, None])
    put("expert", (p[:E0] * (Q0 * CQ))[:, None])
    put("iota", np.tile(np.arange(E1), (128, 1)))
    r = 8 * p[:N, None] + np.arange(NH)[None, :]
    put("regroup", (r // N % 4)[:, :, None] == np.arange(4)[None, None, :])
    put("token", np.arange(B)[None, None, :] * N + np.array([0, T])[None, :, None] + p[:N, None, None])
    t = np.arange(N, dtype=np.float64)
    rc, rs = np.zeros((128, 3, N)), np.zeros((128, 3, N))
    for blk in range(3):
        for j in range(4):
            for d in range(HD):
                f, width = ((2 * j + blk) * HD + d, C) if blk < 2 else (j * HD + d, C // 2)
                theta = 10000.0 ** (-(2.0 * (np.float64(f // 2) - 1.0))) / width
                rc[32 * j + d, blk] = np.cos(t * theta)
                rs[32 * j + d, blk] = np.sin(t * theta) * (1.0 if f % 2 == 0 else -1.0)
    put("rope_c", rc)
    put("rope_s", rs)
    return c


def program(nc, ins, out, consts):
    ctx = ExitStack()
    with ctx:
        def sb(name, shape, dt=F32):
            t = ctx.enter_context(nc.sbuf_tensor(name, shape, dt))
            return t[(slice(None),) * len(shape)]

        def sem(name):
            return ctx.enter_context(nc.semaphore(name))

        def dram(name, shape, dt=F32):
            return nc.dram_tensor(name, shape, dt, kind="Internal").ap()

        d_cand = dram("d_cand", [E0 * Q0 * CQ, 1], I32)
        d_x0 = dram("d_x0", [T, C])
        d_y0 = [dram(f"d_y0_{i}", [T, C]) for i in range(2)]
        d_buf = dram("d_buf", [S1, R1])
        d_acc = dram("d_acc", [2 * T, C])

        cst = sb("cst", [128, NCONST])
        H = sb("H", [N, B, C])
        X = sb("X", [N, B, C])
        TMP = sb("TMP", [N, B, C])
        XT = sb("XT", [128, T])
        stat = sb("stat", [N, 8, B])
        identb = sb("identb", [128, 128], BF16)
        trib = sb("trib", [N, N], BF16)
        onesb = sb("onesb", [N, N], BF16)
        causalb = sb("causalb", [N, 4 * N], BF16)
        bproj = sb("bproj", [N, C])
        gains = sb("gains", [128, 4])
        bst = sb("bst", [N, B, 6])
        mv = sb("mv", [N, B, 2])
        idle = sb("idle", [1, 4])
        rbias = sb("rbias", [N, E0])
        tokb = sb("tokb", [128, 1])
        gb = sb("gb", [128, 6])
        bnst = sb("bnst", [128, 8, 6])
        bnag = sb("bnag", [128, 8])
        bup_in = sb("bup_in", [E0 // GRP, F0])
        b1T = sb("b1T", [128, NJ, E1])
        zrow = sb("zrow", [128, 2, R1])
        zrowi = zrow.bitcast(I32)
        wrt0 = sb("wrt0", [128, E0])
        wrt1 = sb("wrt1", [128, E1])
        wsplit = sb("wsplit", [128, 3, 4 * C], BF16)
        wres = sb("wres", [128, 2, 4 * C])
        arena = sb("arena", [128, 30024])

        def carve(at, words, dt=F32, parts=128):
            v = arena[0:parts, at:at + words]
            return v if dt == F32 else v.bitcast(dt)

        img = [carve(i * 4608, 4608, parts=96).rearrange("p (c h w) -> p c h w", c=3, w=W) for i in range(2)]
        wtok = carve(9216, 768)
        wtokT = carve(9984, 768).rearrange("p (k e) -> p k e", k=KT)
        wqkvp = carve(10752, 512).rearrange("p (j c) -> p j c", j=4)
        patT = carve(11264, KT * B * NI).rearrange("p (k t) -> p k t", k=KT)
        embT = carve(18176, B * NI)
        imgp = [carve(19400 + i * 4608, 4608, parts=96).rearrange("p (w r x) -> p w r x", w=HP, x=PS) for i in range(2)]
        rf = [carve(i * T, T) for i in range(2)]
        qkvb = carve(2 * T, 3 * T // 2, BF16).rearrange("p (j t) -> p j t", j=3)
        qm = carve(2 * T + 3 * T // 2, NH * T // 2, BF16).rearrange("p (h t) -> p h t", h=NH)
        at = 2 * T + 3 * T // 2 + NH * T // 2
        assert at + NH * N <= 30000
        aspk = carve(at, NH * N, BF16, N).rearrange("p (u x) -> p u x", u=2)
        xst = XT[:, 0:T // 2].bitcast(BF16)
        xsb = carve(2 * T + 3 * T // 2, B * C // 2, BF16, N).rearrange("p (b c) -> p b c", b=B)
        vtok = X.rearrange("p b c -> p (b c)")[:, 0:B * C // 2].bitcast(BF16).rearrange("p (b c) -> p b c", b=B)
        osb = xsb
        ost = carve(0, T // 2, BF16)
        sc = [carve(0, LQ), carve(3000, LQ)]
        cv = carve(1000, CQ)
        ci = carve(1200, CQ, U32)
        cif = carve(1400, CQ)
        cii = carve(1600, CQ, I32)
        vm = [carve(1800, Q0 * CQ, parts=E0), carve(4100, Q0 * CQ, parts=E0)]
        gv = carve(2400, CQ, parts=E0)
        gp = carve(2600, CQ, U32, E0)
        gpf = carve(2800, CQ, parts=E0)
        lg = carve(3000, B * E0, parts=N).rearrange("p (b e) -> p b e", b=B)
        pr = carve(4100, B * E0, parts=N).rearrange("p (j q e) -> p j q e", q=Q0, e=E0)
        posi = carve(5200, E0, I32, N)
        gate = carve(5300, E0, parts=N)
        itok = carve(5400, E0, I32, N)
        wu0 = [carve(6000 + F0 * u, F0) for u in range(D)]
        wd0 = [carve(7400 + 384 * u, 384).rearrange("p (k c) -> p k c", k=3) for u in range(D)]
        b1row = carve(12000, F1, parts=E1)
        xg = [carve(9000 + C * u, C, parts=N) for u in range(D)]
        xgT = [carve(9600 + N * u, N) for u in range(2)]
        act0 = [carve(9900 + 3 * N * u, 3 * N).rearrange("p (k t) -> p k t", k=3) for u in range(2)]
        yo0 = [carve(10600 + C * u, C, parts=N) for u in range(D)]
        bupT = carve(11200, 3 * (E0 // GRP)).rearrange("p (k g) -> p k g", k=3)
        wpad = carve(0, 8 * C).rearrange("p (k x) -> p k x", k=8)
        rt = [carve(3810 + 904 * u, 8 * N).rearrange("p (s t) -> p s t", s=2) for u in range(2)]
        qs = [carve(2900 + 452 * u, 2 * N).rearrange("p (g t) -> p g t", g=2) for u in range(2)]
        kz = [carve(1024 + 904 * u, NH * N).rearrange("p (g x) -> p g x", g=2) for u in range(2)]
        s2 = [carve(3810 + 904 * u, NH * N, parts=N).rearrange("p (h t) -> p h t", h=NH) for u in range(2)]
        pr2 = [carve(5620 + 904 * u, NH * N, parts=N).rearrange("p (h t) -> p h t", h=NH) for u in range(2)]
        ptT = [carve(7430 + 904 * u, NH * N, parts=N).rearrange("p (h t) -> p h t", h=NH) for u in range(2)]
        nmx = [carve(9240 + NH * u, NH, parts=N) for u in range(2)]
        rrec = [carve(9280 + NH * u, NH, parts=N) for u in range(2)]
        mg = carve(9300, 32, parts=N).rearrange("p (k g) -> p k g", g=4)
        og = carve(9340, 512, parts=N).rearrange("p (k g d) -> p k g d", k=8, g=4)
        VW = HD + 1
        Vf = carve(10600, B * NH * VW, parts=N).rearrange("p (b h d) -> p b h d", b=B, h=NH)
        V = carve(10800, B * C, parts=N).rearrange("p (b c) -> p b c", b=B)
        QK = carve(15000, 4 * T).rearrange("p (k t) -> p k t", k=4)
        X1 = TMP[:]
        wraw = carve(29464, 3 * C)
        wo = carve(29464 + 3 * C, C)
        xinT = [carve(0 + CAP * u, CAP) for u in range(2)]
        hT = [carve(500 + 904 * u, NJ * CAP).rearrange("p (k t) -> p k t", k=NJ) for u in range(2)]
        lg1 = carve(0, B * E1, parts=N).rearrange("p (b e) -> p b e", b=B)
        pr1 = carve(2048, B * E1, parts=N).rearrange("p (b e) -> p b e", b=B)
        oh = carve(4096, 2 * 8 * E1, parts=N).rearrange("p (k b e) -> p k b e", k=2, b=8)
        mb = carve(5120, B * E1 // 2, BF16, N).rearrange("p (b e) -> p b e", b=B)
        cumb = carve(6144, B * E1 // 2, BF16, N).rearrange("p (b e) -> p b e", b=B)
        X2s = carve(7168, B * R1, parts=N).rearrange("p (b c) -> p b c", b=B)
        X2si = carve(7168, B * R1, I32, N).rearrange("p (b c) -> p b c", b=B)
        mx8 = carve(15596, B * 8, parts=N).rearrange("p (b e) -> p b e", b=B)
        ix8 = carve(15852, B * 8, U32, N).rearrange("p (b e) -> p b e", b=B)
        ef = carve(16108, B * 8, parts=N).rearrange("p (b e) -> p b e", b=B)
        sidx = carve(16364, 2 * B, I32, N).rearrange("p (k b) -> p k b", k=2)
        route = carve(16428, 6 * 16, parts=N).rearrange("p (i k b) -> p i k b", i=6, k=2)
        wsum = carve(16530, 16, parts=N).rearrange("p (i b) -> p i b", i=2)
        w1 = [carve(11500 + 512 * u, F1) for u in range(D)]
        w2 = [carve(13548 + 512 * u, F1).rearrange("p (k c) -> p k c", k=NJ) for u in range(D)]
        xin = [carve(2400 + 2 * R1 * u, 2 * R1).rearrange("p (k c) -> p k c", k=2) for u in range(DX)]
        yo1 = [carve(16640 + 256 * u, 2 * C).rearrange("p (k c) -> p k c", k=2) for u in range(D)]
        b2 = carve(17670, E1 * C)
        X2r = carve(25862, B * R1, parts=N).rearrange("p (b c) -> p b c", b=B)
        X2i = carve(25862, B * R1, I32, N).rearrange("p (b c) -> p b c", b=B)
        xini = [carve(2400 + 2 * R1 * u, 2 * R1, I32).rearrange("p (k c) -> p k c", k=2) for u in range(DX)]
        X2 = X2r[:, :, 0:C]

        def const(name, parts=128):
            a, w = CONST[name]
            return cst[0:parts, a:a + w]

        ident = const("ident")

        ps = ctx.enter_context(nc.psum_tensor("ps", [128, 8, 512], F32))

        def bank(i, parts=128):
            return ps[0:parts, i, :]

        names = """cst_in img_in0 img_in1 img_packed wtok_in txt_in wqkv_in small_in rows_in zeroed zrow_ready buf_zeroed b1_in
            tile_ready tile_moved dve ln_var ln_std ln_affine ln_dve ln_act
            spk_relu spk_ready qkv_ready qkv_stats qkv_std qkv_moved w_split
            qm_ready sT_ready a_ready o_ready o_moved ob_ready h_biased h_added proj_ready proj_added
            x0_out h_out y0_zero lg_ready lg_sub lg_exp pr_ready
            cand_ready cand_out vm_in gp_ready itok_in0 itok_in1 itok_in2 itok_in3 ones_in
            g_in0 g_in1 g_in2 g_in3 e_w0 e_w1 e_w2 e_w3 e_xT e_xTc e_up e_act e_down e_out e_sc0 e_sc1
            y0_in0 y0_in1 y0_in2 y0_in3 consts_ready
            m_lg m_max m_exp m_m m_cum m_copied m_rows m_scat0 m_scat1 b2_in m_biased m_sc0 m_sc1 m_sc2 m_sc3 m_w0 m_w1 m_w2 m_w3 m_x0 m_x1 m_x2 m_x3 m_x4 m_x5 m_x6 m_x7 m_xT m_xTc m_up m_act m_down m_out
            fin_in0 fin_in1 fin_in2 fin_in3 fin_ready fin_out""".split()
        S = {n: sem(n) for n in names}
        A = {}
        for tag in ("r", "f"):
            for n in ("w_in", "wpad", "ones", "qk_mm", "qk_c", "q_c", "k_in0", "k_in1", "sc", "max", "sub", "exp",
                      "pT", "pTc", "rec", "o", "o_c") + (("rope", "kz", "mask", "group") if tag == "r" else ("w", "w_c")):
                A[tag + n] = sem(f"{tag}_{n}")

        class Chain:

            def __init__(self, eng, s):
                self.eng, self.s, self.n, self.at = eng, s, 0, 0

            def tick(self, ins):
                ins.then_inc(self.s, 1)
                self.n += 1
                return self.n

            def link(self, ins):
                self.tick(ins)
                self.eng.wait_ge(self.s, self.at + self.n)

        def loop(eng, total, head, tail, body, step=1):
            for i in range(head):
                body(i, i % step, i // step)
            steps = (total - head - tail) // step
            assert steps * step == total - head - tail and head % step == 0
            with eng.Fori(0, steps) as r:
                for k in range(step):
                    body(r * step + (head + k), k, r + head // step)
            for i in range(total - tail, total):
                body(i, i % step, i // step)

        def known(i):
            return isinstance(i, int)

        def wait(eng, s, value):
            if not known(value) or value > 0:
                eng.wait_ge(s, value)

        class Tiles:
            def __init__(self):
                self.n = 0

            def pe_open(self, pe):
                if self.n >= 4:
                    pe.wait_ge(S["tile_moved"], self.n - 3)
                return self.n % 4

            def pe_close(self, ins):
                ins.then_inc(S["tile_ready"], 1)
                self.n += 1

            def act_open(self, act):
                act.wait_ge(S["tile_ready"], self.n + 1)
                return self.n % 4

            def act_close(self, ins):
                ins.then_inc(S["tile_moved"], 1)
                self.n += 1

        def tile_counts():
            c, n = {}, 0
            for name, k in (("w", 3), ("pat", 24), ("emb", 4), ("H", 8), ("xs", 8), ("v", 8), ("os", 8),
                            ("xt0", 8), ("gT", 4), ("rx", 8), ("rv", 8), ("fx", 8), ("fv", 8), ("fo", 8), ("xt1", 8)):
                n += k
                c[name] = n
            return c

        moved = tile_counts()

        WPAD = {"r": 10, "f": 4}
        NB = {"r": 3, "f": 4}

        LNC, LND = 4, (2, 2, 2, 4)
        chunk = lambda c: slice(c * (B // LNC), (c + 1) * (B // LNC))

        def normalised(eng, k, c=LNC - 1):
            eng.wait_ge(S["ln_dve"], LNC * k + c + 1)
            eng.wait_ge(S["ln_act"], LNC * k + c + 1)

        tok_rows = [(0, SPLIT), (SPLIT, N)]

        def bcol(ap2, width):
            return ap2.unsqueeze(2).broadcast_to([ap2.shape[0], ap2.shape[1], width])

        def brow(ap2, count):
            return ap2.unsqueeze(1).broadcast_to([ap2.shape[0], count, ap2.shape[1]])

        token_rows = lambda ap: ap.rearrange("(b n) c -> n b c", n=N)

        def y0_load(eng, y, dst):
            for u in range(2):
                eng.wait_ge(S[f"e_sc{u}"], 16 * (E0 // 2))
            for c in range(LNC):
                for a, z in tok_rows:
                    eng.dma_start(dst[a:z, chunk(c)], token_rows(y)[a:z, chunk(c)]).then_inc(S[f"y0_in{c}"], 16)

        def acc_load(eng, k, dst):
            for u in range(D):
                eng.wait_ge(S[f"m_sc{u}"], 32 * (E1 // D))
            for c in range(LNC):
                for a, z in tok_rows:
                    eng.dma_start(dst[a:z, chunk(c)], token_rows(d_acc[k * T:(k + 1) * T])[a:z, chunk(c)])\
                        .then_inc(S[f"fin_in{c}"], 16)

        block = ctx.enter_context(nc.Block())

        @block.sync
        def _(sp):
            sp.dma_start(cst[:], consts).then_inc(S["cst_in"], 16)
            sp.dma_start(wtok, ins["L0_tok_w"]).then_inc(S["wtok_in"], 16)
            imgv = ins["x"].rearrange("b c (h p) w -> b h c (p w)", h=HP)
            for i in range(2):
                for h in range(HP):
                    sp.dma_start(img[i][h * 16:(h + 1) * 16].rearrange("p c h w -> p c (h w)"), imgv[16 * i:16 * i + 16, h])\
                        .then_inc(S[f"img_in{i}"], 16)
            sp.dma_start(H[NI:N, :, :], ins["txt"].rearrange("b n c -> n b c")).then_inc(S["txt_in"], 16)
            sp.dma_start(wqkvp[:, 0:3, :], ins["L0_attn_Wqkv"].rearrange("(j d) c -> d j c", j=3)).then_inc(S["wqkv_in"], 16)
            sp.dma_start(wqkvp[:, 3, :], ins["L0_attn_Wproj"]).then_inc(S["wqkv_in"], 16)
            sp.dma_start(tokb[:], ins["L0_tok_b"].rearrange("(p o) -> p o", o=1)).then_inc(S["small_in"], 16)
            sp.dma_start(gb[:, 0:3], ins["L0_attn_gamma"].rearrange("(j p) -> p j", j=3), allow_slow_non_contiguous=True).then_inc(S["small_in"], 16)
            sp.dma_start(gb[:, 3:6], ins["L0_attn_beta"].rearrange("(j p) -> p j", j=3), allow_slow_non_contiguous=True).then_inc(S["small_in"], 16)
            sp.dma_start(wrt0[:], ins["L0_ffn_W_router"]).then_inc(S["small_in"], 16)
            sp.dma_start(wrt1[:], ins["L1_ffn_wr"]).then_inc(S["small_in"], 16)
            sp.dma_start(bproj[:], ins["L0_attn_bproj"].partition_broadcast(N)).then_inc(S["rows_in"], 16)
            for i, nm in enumerate(("L1_ffn_ln1_g", "L1_ffn_ln1_b", "L1_ffn_ln2_g", "L1_ffn_ln2_b")):
                sp.dma_start(gains[:, i:i + 1], ins[nm].rearrange("(p o) -> p o", o=1)).then_inc(S["rows_in"], 16)
            sp.dma_start(bup_in, ins["L0_ffn_b_up"]).then_inc(S["rows_in"], 16)
            sp.dma_start(rbias[:], ins["L0_ffn_b_router"].partition_broadcast(N)).then_inc(S["rows_in"], 16)
            sp.wait_ge(S["zeroed"], 1)
            flat = lambda ap: ap.rearrange("s c -> (s c)").rearrange("(p x) -> p x", p=128)
            sp.dma_start(flat(d_y0[1]), XT).then_inc(S["y0_zero"], 16)
            for i in range(2):
                sp.dma_start(flat(d_acc[i * T:(i + 1) * T]), XT).then_inc(S["y0_zero"], 16)
            sp.wait_ge(S["zrow_ready"], 1)
            for k, (a, n) in enumerate(CAPT):
                sp.dma_start(d_buf.rearrange("(e s) c -> s e c", s=CAP)[a:a + n],
                             zrow[0:n, k, :].unsqueeze(1).broadcast_to([n, E1, R1])).then_inc(S["buf_zeroed"], 16)
            normalised(sp, 1)
            for a, z in tok_rows:
                sp.dma_start(d_x0.rearrange("(b n) c -> n b c", n=N)[a:z], X[a:z]).then_inc(S["x0_out"], 16)
                sp.dma_start(d_y0[0].rearrange("(b n) c -> n b c", n=N)[a:z], H[a:z]).then_inc(S["h_out"], 16)
            sp.dma_start(b1row, ins["L1_ffn_b1"]).then_inc(S["b1_in"], 16)
            sp.wait_ge(S["cand_ready"], 1)
            for q in range(Q0):
                sp.dma_start(d_cand.rearrange("(e q r) o -> q e (r o)", e=E0, q=Q0)[q], cii[q * E0:(q + 1) * E0, :])\
                    .then_inc(S["cand_out"], 16)
                sp.dma_start(vm[0][:, q * CQ:(q + 1) * CQ], cv[q * E0:(q + 1) * E0, :]).then_inc(S["vm_in"], 16)

            def e0_load(e, u, turn):
                wait(sp, S["e_down"], e - D + 1)
                wdv = ins["L0_ffn_W_down"].rearrange("e f c -> (e f) c")
                g = e // GRP if known(e) else turn
                sp.dma_start(wu0[u], ins["L0_ffn_W_up"].rearrange("g c f -> (g c) f")[bass.ds(g * C, C), :])\
                    .then_inc(S[f"e_w{u}"], 16)
                sp.dma_start(wd0[u][:, 0:2, :], wdv[bass.ds(e * F0, 256), :].rearrange("(k p) c -> p k c", k=2))\
                    .then_inc(S[f"e_w{u}"], 16)
                sp.dma_start(wd0[u][0:F0 - 256, 2, :], wdv[bass.ds(e * F0 + 256, F0 - 256), :]).then_inc(S[f"e_w{u}"], 16)
                sp.dma_start(wd0[u][F0 - 256:F0 - 255, 2, :], ins["L0_ffn_b_down"][bass.ds(e, 1), :])\
                    .then_inc(S[f"e_w{u}"], 16)

            loop(sp, E0, D, 0, e0_load, step=D)
            y0_load(sp, d_y0[0], H)

            sp.dma_start(wraw[:, 0:128], ins["L1_attn_Wq"]).then_inc(A["rw_in"], 16)
            sp.dma_start(wraw[:, 128:192], ins["L1_attn_Wk"]).then_inc(A["rw_in"], 16)
            sp.dma_start(wraw[:, 256:320], ins["L1_attn_Wv"]).then_inc(A["rw_in"], 16)
            sp.wait_ge(A["rqk_mm"], 24)
            sp.wait_ge(S["tile_moved"], moved["rv"])
            for i, nm in enumerate(("L1_ffn_wq", "L1_ffn_wk", "L1_ffn_wv")):
                sp.dma_start(wraw[:, i * 128:(i + 1) * 128], ins[nm]).then_inc(A["fw_in"], 16)
            sp.dma_start(wo, ins["L1_ffn_wo"]).then_inc(A["fw_in"], 16)

            def keys(tag):
                a = lambda n: A[tag + n]

                def step(b, u, _turn):
                    if known(b) and b == 0:
                        sp.wait_ge(a("qk_c"), NB[tag])
                    wait(sp, a("sc"), b - 1)
                    for j in range(4):
                        rows_ = slice(32 * j, 32 * j + 32)
                        src = QK[rows_, 2:NB[tag], bass.ds(b * N, N)]
                        if tag == "r":
                            src = src.broadcast_to([32, 2, N])
                        sp.dma_start(kz[u][rows_, :, j * N:(j + 1) * N], src)\
                            .then_inc(a(f"k_in{u}"), 16)
                    if known(b) and b == 1:
                        sp.wait_ge(a("qk_c"), 8 * NB[tag])

                loop(sp, B, 2, 2, step, step=2)

            sp.wait_ge(A["rkz"], 2)
            keys("r")
            keys("f")

            sp.wait_ge(A["fo_c"], B)
            sp.dma_start(b2.rearrange("p (e c) -> p e c", e=E1), ins["L1_ffn_b2"].partition_broadcast(128)).then_inc(S["b2_in"], 16)
            w1v = ins["L1_ffn_w1"].rearrange("e c f -> (e c) f")
            w2v = ins["L1_ffn_w2"].rearrange("e (p k) c -> (e p) (k c)", k=NJ)

            def e1_weights(e, u, turn):
                wait(sp, S["m_down"], e - D + 1)
                sp.dma_start(w1[u], w1v[bass.ds(e * 128, 128), :]).then_inc(S[f"m_w{u}"], 16)
                sp.dma_start(w2[u].rearrange("p k c -> p (k c)"), w2v[bass.ds(e * 128, 128), :]).then_inc(S[f"m_w{u}"], 16)

            def e1_tokens(e, u, turn):
                wait(sp, S[f"m_sc{u % D}"], (2 * (turn - 1) + u // D + 1) * 32 if not known(turn) or turn > 0 else 0)
                for k, (a, n) in enumerate(CAPT):
                    sp.dma_start(xin[u][0:n, k, :], d_buf[bass.ds(e * CAP + a, n), :]).then_inc(S[f"m_x{u}"], 16)

            for e in range(D):
                e1_weights(e, e, 0)
            for k in range(2):
                sp.wait_ge(S[f"m_scat{k}"], 16 * B)
            for e in range(DX):
                e1_tokens(e, e, 0)
            for e in range(D, DX):
                e1_weights(e, e % D, 1)

            def e1_io(e, u, turn):
                e1_tokens(e, u, turn)
                e1_weights(e, u % D, turn)

            with sp.Fori(1, E1 // DX) as r:
                for u in range(DX):
                    e1_io(r * DX + u, u, r)
            acc_load(sp, 0, X)
            for c in range(LNC):
                sp.wait_ge(S["fin_ready"], c + 1)
                for a, z in tok_rows:
                    sp.dma_start(out.rearrange("b n c -> n b c")[a:z, chunk(c)], H[a:z, chunk(c)]).then_inc(S["fin_out"], 16)
            sp.wait_ge(S["fin_out"], 128)

        @block.tensor
        def _(pe):
            tl = Tiles()
            pe.wait_ge(S["cst_in"], 16)
            pe.wait_ge(S["wtok_in"], 16)
            for g in range(2):
                k0 = tl.pe_open(pe)
                for k in range(3):
                    ins_ = pe.transpose(bank(k0)[:, k * 128:(k + 1) * 128], wtok[:, (3 * g + k) * 128:(3 * g + k + 1) * 128], ident)
                tl.pe_close(ins_)
            pe.wait_ge(S["wqkv_in"], 32)
            k0 = tl.pe_open(pe)
            for j in range(4):
                ins_ = pe.transpose(bank(k0)[:, j * 128:(j + 1) * 128], wqkvp[:, j, :], ident)
            tl.pe_close(ins_)
            for t in range(2):
                pe.wait_ge(S["img_packed"], t + 1)
                for k in range(KT):
                    for half in range(2):
                        k0 = tl.pe_open(pe)
                        for w in range(3):
                            wp = half * 3 + w
                            src = imgp[t][:, wp, k * 8:(k + 1) * 8, :].rearrange("p r x -> p (r x)")
                            ins_ = pe.transpose(bank(k0)[:, w * 96:(w + 1) * 96], src, ident[0:96, 0:96])
                        tl.pe_close(ins_)
                pe.wait_ge(S["tile_moved"], moved["w"] + t * 14 + 12)
                for g in range(2 * t, 2 * t + 2):
                    k0 = tl.pe_open(pe)
                    for k in range(KT):
                        ins_ = pe.matmul(bank(k0)[:, 0:288], wtokT[:, k, :], patT[:, k, g * 288:(g + 1) * 288],
                                         start=(k == 0), stop=(k == KT - 1))
                    tl.pe_close(ins_)
            pe.wait_ge(S["tile_moved"], moved["emb"])
            for g in range(8):
                k0 = tl.pe_open(pe)
                for k in range(4):
                    b = 4 * g + k
                    ins_ = pe.transpose(bank(k0)[0:NI, k * 128:(k + 1) * 128], embT[:, b * NI:(b + 1) * NI], ident)
                tl.pe_close(ins_)

            def turn(src, dt, idm, ready=None, groups=range(8)):
                for g in groups:
                    if ready and g % 2 == 0:
                        ready(g // 2)
                    k0 = tl.pe_open(pe)
                    o = bank(k0) if dt == F32 else bank(k0).bitcast(BF16)
                    for k in range(4):
                        stride = N if dt == F32 else N + 1
                        x = pe.transpose(o[:, k * stride:k * stride + N], src[:, 4 * g + k, :], idm)
                    tl.pe_close(x)

            pe.wait_ge(S["consts_ready"], 1)
            turn(xsb, BF16, identb[0:N, 0:N], lambda c: pe.wait_ge(S["spk_ready"], c + 1))
            pe.wait_ge(S["w_split"], 1)
            pe.wait_ge(S["tile_moved"], moved["xs"])
            for j in range(3):
                for c in range(8):
                    if j:
                        pe.wait_ge(S["qkv_moved"], 8 * (j - 1) + c + 1)
                    for p in range(3):
                        x = pe.matmul(bank(c)[:, 0:4 * N], wsplit[:, p, j * C:(j + 1) * C], xst[:, c * 4 * N:(c + 1) * 4 * N],
                                      start=(p == 0), stop=(p == 2))
                    x.then_inc(S["qkv_ready"], 1)
            pe.wait_ge(S["qkv_moved"], 24)
            pe.wait_ge(S["qm_ready"], 3)
            for g in range(8):
                k0 = tl.pe_open(pe)
                for k in range(4):
                    b = 4 * g + k
                    x = pe.transpose(bank(k0, N).bitcast(BF16)[:, k * 128:(k + 1) * 128], qkvb[:, 2, b * N:(b + 1) * N], identb)
                tl.pe_close(x)
            pe.wait_ge(S["tile_moved"], moved["v"])
            pe.wait_ge(S["qm_ready"], 4)

            def spk_scores(b, u):
                for g in range(2):
                    x = pe.matmul(bank(2 * u + g, N)[:, 0:4 * N], qkvb[:, 1, bass.ds(b * N, N)],
                                  qm[:, 4 * g:4 * g + 4, bass.ds(b * N, N)], start=True, stop=True)
                x.then_inc(S["sT_ready"], 1)

            def spk_values(b, u):
                pe.wait_ge(S["a_ready"], b + 1)
                wait(pe, S["o_moved"], b - 1)
                for h in range(NH):
                    x = pe.matmul(bank(4 + u, N)[:, h * HD:(h + 1) * HD], aspk[:, u, h * N:(h + 1) * N],
                                  vtok[:, bass.ds(b, 1), h * HD:(h + 1) * HD], start=True, stop=True)
                x.then_inc(S["o_ready"], 1)

            def spk_step(b, u, _turn):
                if not (known(b) and b == B - 1):
                    wait(pe, S["a_ready"], b)
                    spk_scores(b + 1, 1 - u)
                if not (known(b) and b == 0):
                    spk_values(b - 1, 1 - u)

            spk_scores(0, 0)
            loop(pe, B, 2, 2, spk_step, step=2)
            spk_values(B - 1, 1)
            pe.wait_ge(S["ob_ready"], 1)
            turn(osb, BF16, identb[0:N, 0:N])
            pe.wait_ge(S["tile_moved"], moved["os"])
            for g in range(8):
                if g >= 4:
                    pe.wait_ge(S["proj_added"], g - 3)
                for k in range(4):
                    b = 4 * g + k
                    for p in range(3):
                        x = pe.matmul(bank(4 + g % 4, N)[:, k * C:(k + 1) * C], ost[:, b * N:(b + 1) * N],
                                      wsplit[:, p, 3 * C:4 * C], start=(p == 0), stop=(p == 2))
                x.then_inc(S["proj_ready"], 1)

            pe.wait_ge(S["y0_zero"], 48)
            def logits0(c):
                pe.wait_ge(S["tile_moved"], moved["os"] + 2 * (c + 1))
                pe.wait_ge(S["proj_added"], 8)
                for b in range(8 * c, 8 * c + 8):
                    x = pe.matmul(bank(4 + b // 16, N)[:, (b % 16) * E0:(b % 16 + 1) * E0], XT[:, b * N:(b + 1) * N], wrt0[:],
                                  start=True, stop=True)
                return x

            for c in range(LNC):
                normalised(pe, 1, c)
                turn(X, F32, ident[0:N, 0:N], groups=(2 * c, 2 * c + 1))
                if c:
                    logits0(c - 1)
            x = logits0(LNC - 1)
            x.then_inc(S["lg_ready"], 1)
            pe.wait_ge(S["pr_ready"], 1)
            for j in range(B // Q0):
                x = pe.transpose(bank(6 + j // 4)[:, (j % 4) * N:(j % 4 + 1) * N],
                                 pr[:, j].rearrange("p q e -> p (q e)"), ident[0:N, 0:N])
            x.then_inc(S["lg_ready"], 1)
            pe.wait_ge(S["gp_ready"], 1)
            for src in (gpf, gv):
                k0 = tl.pe_open(pe)
                tl.pe_close(pe.transpose(bank(k0, K0)[:, 0:E0], src[:, 0:K0], ident[0:E0, 0:E0]))

            k0 = tl.pe_open(pe)
            for k, (a, n) in enumerate(F0C):
                x = pe.transpose(bank(k0, n)[:, 8 * k:8 * k + 8], bup_in[:, a:a + n], ident[0:E0 // GRP, 0:E0 // GRP])
            tl.pe_close(x)
            pe.wait_ge(S["b1_in"], 16)
            k0 = tl.pe_open(pe)
            for k in range(NJ):
                x = pe.transpose(bank(k0)[:, k * E1:(k + 1) * E1], b1row.rearrange("e (p k) -> e k p", k=NJ)[:, k, :],
                                 ident[0:E1, 0:E1])
            tl.pe_close(x)
            pe.wait_ge(S["tile_moved"], moved["gT"])

            def e0_turn(e, u, turn):
                v = u % 2
                pe.wait_ge(S[f"g_in{u}"], (turn + 1) * 16)
                wait(pe, S["e_xTc"], e - 1)
                pe.transpose(bank(v)[:, 0:K0], xg[u], ident[0:K0, 0:K0]).then_inc(S["e_xT"], 1)

            def e0_up(e, u, turn):
                v = u % 2
                pe.wait_ge(S[f"e_w{u}"], (turn + 1) * 64)
                pe.wait_ge(S["e_xTc"], e + 1)
                wait(pe, S["e_act"], (e - 1) * 3)
                for k, (a, n) in enumerate(F0C):
                    x = pe.matmul(bank(2 + v, n)[:, k * K0:(k + 1) * K0], wu0[u][:, a:a + n], xgT[v], start=True, stop=True)
                x.then_inc(S["e_up"], 1)

            def e0_down(e, u, turn):
                v = u % 2
                pe.wait_ge(S["e_act"], (e + 1) * 3)
                wait(pe, S["e_out"], e - 1)
                o = bank(4 + v, K0)[:, 0:C]
                for k, (a, n) in enumerate(F0C):
                    rows_ = n if k < 2 else n + 1
                    x = pe.matmul(o, act0[v][0:rows_, k, :], wd0[u][0:rows_, k, :], start=(k == 0), stop=(k == 2))
                x.then_inc(S["e_down"], 1)

            def ahead(e, u, turn, k, f, total, step):
                if not known(e) or e + k < total:
                    f(e + k, (u + k) % step, turn + (u + k) // step)

            def e0_step(e, u, turn):
                ahead(e, u, turn, 1, e0_up, E0, D)
                ahead(e, u, turn, 2, e0_turn, E0, D)
                e0_down(e, u, turn)

            pe.wait_ge(S["ones_in"], 1)
            e0_turn(0, 0, 0)
            e0_up(0, 0, 0)
            e0_turn(1, 1, 0)
            loop(pe, E0, D, D, e0_step, step=D)
            pe.wait_ge(S["e_out"], E0)

            def attention(tag, rope):
                a = lambda n: A[tag + n]
                nv = C // 2 if rope else C

                def values(c):
                    for g in (2 * c, 2 * c + 1):
                        k0 = tl.pe_open(pe)
                        for k in range(4):
                            b = 4 * g + k
                            x = pe.matmul(bank(k0, N)[:, k * nv:(k + 1) * nv], XT[:, b * N:(b + 1) * N],
                                          wraw[:, 2 * C:2 * C + nv], start=True, stop=True)
                        tl.pe_close(x)

                def queries_keys(c):
                    nb = NB[tag]
                    for n in range(2 * nb * c, 2 * nb * (c + 1)):
                        k = n % nb
                        if n >= 2:
                            pe.wait_ge(a("rope") if rope else a("qk_c"), n - 1)
                        xc = XT[:, (n // nb) * 4 * N:(n // nb + 1) * 4 * N]
                        x = pe.matmul(bank(4 + 2 * (n % 2))[:, 0:4 * N], wpad[:, k, :], xc, start=True, stop=True)
                        if rope:
                            x = pe.matmul(bank(5 + 2 * (n % 2))[:, 0:4 * N], wpad[:, 4 + k, :], xc, start=True, stop=True)
                        x.then_inc(a("qk_mm"), 1)

                base = moved["gT" if rope else "rv"]
                for c in range(LNC + 1):
                    if c < LNC:
                        normalised(pe, 2 if rope else 4, c)
                        turn(X if rope else X1, F32, ident[0:N, 0:N], groups=(2 * c, 2 * c + 1))
                    if c == 1:
                        pe.wait_ge(a("w_in"), 48 if rope else 64)
                    if c:
                        pe.wait_ge(S["tile_moved"], base + max(2, 4 * (c - 1)))
                        values(c - 1)
                pe.wait_ge(a("wpad"), WPAD[tag])
                for c in range(LNC):
                    queries_keys(c)

                def scores(b, u, turn):
                    pe.wait_ge(a("q_c"), b + 1)
                    pe.wait_ge(a(f"k_in{u}"), (turn + 1) * 64)
                    wait(pe, a("sub"), b - 1)
                    for g in range(2):
                        o = bank(4 + 2 * u + g, N)[:, 0:4 * N]
                        if rope:
                            pe.matmul(o, identb[0:N, 0:N], causalb[:], start=True, stop=False)
                        x = pe.matmul(o, qs[u][:, g, :], kz[u][:, g, :], start=not rope, stop=True)
                    x.then_inc(a("sc"), 1)

                def turn_p(b, u):
                    pe.wait_ge(a("exp"), b + 1)
                    wait(pe, a("pTc"), b)
                    for h in range(NH):
                        x = pe.transpose(bank(2 + h // 4, N)[:, (h % 4) * N:(h % 4 + 1) * N], pr2[u][:, h, :], ident[0:N, 0:N])
                    x.then_inc(a("pT"), 1)

                def step(b, u, turn):
                    if not known(b) or b + 2 < B:
                        scores(b + 2, u, turn + 1)
                    if not known(b) or b + 1 < B:
                        turn_p(b + 1, 1 - u)
                    pe.wait_ge(a("pTc"), b + 1)
                    if rope:
                        wait(pe, a("o_c"), b)
                        rows8 = ptT[u].rearrange("p h t -> p (h t)").rearrange("p (n k) -> p k n", k=8)
                        for k in range(8):
                            x = pe.matmul(bank(k // 4, N)[:, (k % 4) * 128:(k % 4) * 128 + 65], rows8[:, k, :],
                                          V[:, bass.ds(b, 1), 0:65], start=True, stop=True)
                    else:
                        wait(pe, a("o_c"), b - 1)
                        for h in range(NH):
                            x = pe.matmul(bank(u, N)[:, h * VW:(h + 1) * VW], ptT[u][:, h, :],
                                          Vf[:, bass.ds(b, 1), h, :], start=True, stop=True)
                    x.then_inc(a("o"), 1)

                pe.wait_ge(a("qk_c"), 8 * NB[tag])
                pe.wait_ge(S["tile_moved"], moved[tag + "v"])
                pe.wait_ge(a("ones"), 1)
                scores(0, 0, 0)
                scores(1, 1, 0)
                turn_p(0, 0)
                loop(pe, B, 2, 2, step, step=2)
                if not rope:
                    pe.wait_ge(a("o_c"), B)
                    turn(TMP, F32, ident[0:N, 0:N])
                    pe.wait_ge(S["tile_moved"], moved[tag + "o"])
                    for g in range(8):
                        if g >= 4:
                            pe.wait_ge(a("w_c"), g - 3)
                        for k in range(4):
                            b = 4 * g + k
                            x = pe.matmul(bank(4 + g % 4, N)[:, k * C:(k + 1) * C], XT[:, b * N:(b + 1) * N], wo, start=True, stop=True)
                        x.then_inc(a("w"), 1)

            attention("r", True)
            attention("f", False)

            def logits1(c):
                pe.wait_ge(S["tile_moved"], moved["fo"] + 2 * (c + 1))
                pe.wait_ge(A["fw_c"], 8)
                for k in range(8):
                    b = 8 * c + k
                    x = pe.matmul(bank(4 + c, N)[:, k * E1:(k + 1) * E1], XT[:, b * N:(b + 1) * N], wrt1[:], start=True, stop=True)
                x.then_inc(S["m_lg"], 1)

            for c in range(LNC):
                normalised(pe, 5, c)
                turn(X2, F32, ident[0:N, 0:N], groups=(2 * c, 2 * c + 1))
                if c:
                    logits1(c - 1)
            logits1(LNC - 1)
            for c in range(LNC):
                pe.wait_ge(S["m_m"], c + 1)
                pe.matmul(bank(4 + c, N), trib[:], mb[:, chunk(c), :], start=True, stop=False)
                x = pe.matmul(bank(4 + c, N), onesb[:], cumb[:, chunk(c), :], start=False, stop=True)
                x.then_inc(S["m_cum"], 1)

            def e1_turn(e, u, turn):
                v = u % 2
                pe.wait_ge(S[f"m_x{u}"], (turn + 1) * 32)
                wait(pe, S["m_xTc"], e - 1)
                for k, (a, n) in enumerate(CAPT):
                    x = pe.transpose(bank(v)[:, a:a + n], xin[u][0:n, k, 0:C], ident[0:n, 0:n])
                x.then_inc(S["m_xT"], 1)

            def e1_up(e, u, turn):
                v = u % 2
                w = u % D
                pe.wait_ge(S[f"m_w{w}"], (2 * turn + u // D + 1) * 32)
                pe.wait_ge(S["m_xTc"], e + 1)
                wait(pe, S["m_act"], (e - 1) * NJ)
                w1k = w1[w].rearrange("p (f k) -> p k f", k=NJ)
                for k in range(NJ):
                    x = pe.matmul(bank(2 + 2 * v + k // 2)[:, (k % 2) * CAP:(k % 2 + 1) * CAP], w1k[:, k, :], xinT[v],
                                  start=True, stop=True)
                x.then_inc(S["m_up"], 1)

            def e1_step(e, u, turn):
                v = u % 2
                ahead(e, u, turn, 1, e1_up, E1, DX)
                ahead(e, u, turn, 2, e1_turn, E1, DX)
                pe.wait_ge(S["m_act"], (e + 1) * NJ)
                wait(pe, S["m_out"], e - 1)
                for k, (a, n) in enumerate(CAPT):
                    for j in range(NJ):
                        x = pe.matmul(bank(6 + v, n)[:, k * C:(k + 1) * C], hT[v][:, j, a:a + n], w2[u % D][:, j, :],
                                      start=(j == 0), stop=(j == NJ - 1))
                x.then_inc(S["m_down"], 1)

            e1_turn(0, 0, 0)
            e1_up(0, 0, 0)
            e1_turn(1, 1, 0)
            loop(pe, E1, DX, DX, e1_step, step=DX)

        @block.scalar
        def _(act):
            tl = Tiles()
            copy = lambda o, i: act.activation(o, i, ACT.Copy)
            act.wait_ge(S["small_in"], 80)
            for g in range(2):
                k0 = tl.act_open(act)
                tl.act_close(copy(wtokT[:, 3 * g:3 * g + 3, :], bank(k0)[:, 0:384].rearrange("p (k e) -> p k e", k=3)))
            k0 = tl.act_open(act)
            tl.act_close(copy(wres[:, 0, :], bank(k0)))
            ev = embT.rearrange("p (t b h w) -> p t w h b", t=2, w=HP, h=HP)
            for t in range(2):
                for k in range(KT):
                    for half in range(2):
                        k0 = tl.act_open(act)
                        at_ = t * 576 + half * 288
                        tl.act_close(copy(patT[:, k, at_:at_ + 288], bank(k0)[:, 0:288]))
                for half in range(2):
                    k0 = tl.act_open(act)
                    tl.act_close(act.activation(ev[:, t, 3 * half:3 * half + 3],
                                                bank(k0)[:, 0:288].rearrange("p (w h b) -> p w h b", w=3, h=HP),
                                                ACT.Identity, bias=tokb[:, 0:1]))
            for g in range(8):
                k0 = tl.act_open(act)
                tl.act_close(copy(H[0:NI, 4 * g:4 * g + 4, :], bank(k0, NI).rearrange("p (k c) -> p k c", k=4)))

            def untile_group(g, dst, gain=None):
                k0 = tl.act_open(act)
                if dst.dtype == BF16:
                    src = bank(k0).bitcast(BF16)[:, 0:4 * (N + 1)].rearrange("p (k t) -> p k t", k=4)[:, :, 0:N]
                    o = dst[:, 4 * g * N:(4 * g + 4) * N].rearrange("p (k t) -> p k t", k=4)
                else:
                    src, o = bank(k0)[:, 0:4 * N], dst[:, 4 * g * N:(4 * g + 4) * N]
                if gain is None:
                    tl.act_close(copy(o, src))
                else:
                    tl.act_close(act.activation(o, src, ACT.Identity, scale=gains[:, gain:gain + 1],
                                                bias=gains[:, gain + 1:gain + 2]))

            def untile(dst):
                for g in range(8):
                    untile_group(g, dst)

            def layernorm(k, src, dst, after=None):
                for c in range(LNC + 2):
                    if c < LNC:
                        act.wait_ge(S["ln_var"], LNC * k + c + 1)
                        act.activation(stat[:, 1, chunk(c)], stat[:, 0, chunk(c)], ACT.Sqrt).then_inc(S["ln_std"], 1)
                    if 1 <= c <= LNC:
                        act.wait_ge(S["ln_affine"], LNC * k + c)
                        for b in range(8 * c - 8 + LND[c - 1], 8 * c):
                            x = act.activation(dst[:, b, :], src[:, b, :], ACT.Identity, scale=stat[:, 2, b:b + 1],
                                               bias=stat[:, 3, b:b + 1])
                        x.then_inc(S["ln_act"], 1)
                    if after and c >= 2:
                        after(c - 2)

            def turned(dst, gain=None):
                def f(c):
                    untile_group(2 * c, dst, gain)
                    untile_group(2 * c + 1, dst, gain)
                return f

            def relu(c):
                normalised(act, 0, c)
                act.activation(TMP[:, chunk(c)], X[:, chunk(c)], ACT.Relu, scale=NUDGE).then_inc(S["spk_relu"], 1)

            layernorm(0, H, X, relu)
            act.wait_ge(S["y0_zero"], 48)
            untile(xst)
            for j in range(3):
                act.wait_ge(S["qkv_stats"], 2 * j + 1)
                act.activation(bnag[:, 3:4], bnag[:, 2:3], ACT.Sqrt).then_inc(S["qkv_std"], 1)
                act.wait_ge(S["qkv_stats"], 2 * j + 2)
                if j == 2:
                    act.wait_ge(S["qm_ready"], 1)
                for c in range(8):
                    act.activation(rf[j % 2][:, c * 4 * N:(c + 1) * 4 * N], bank(c)[:, 0:4 * N], ACT.Relu,
                                   bias=bnag[:, 6:7], scale=bnag[:, 5:6]).then_inc(S["qkv_moved"], 1)
            for g in range(8):
                k0 = tl.act_open(act)
                tl.act_close(copy(vtok[:, 4 * g:4 * g + 4, :],
                                  bank(k0, N).bitcast(BF16)[:, 0:512].rearrange("p (k c) -> p k c", k=4)))

            def spk_out(b, u, _turn):
                act.wait_ge(S["o_ready"], b + 1)
                act.activation(TMP[:, bass.ds(b, 1), :], bank(4 + u, N)[:, 0:C].unsqueeze(1), ACT.Relu,
                               scale=NUDGE * float(HD) ** -0.5).then_inc(S["o_moved"], 1)

            loop(act, B, 2, 2, spk_out, step=2)
            untile(ost)

            layernorm(1, H, X, turned(XT[:]))
            act.wait_ge(S["lg_sub"], 1)
            act.activation(lg, lg, ACT.Exp).then_inc(S["lg_exp"], 1)
            k0 = tl.act_open(act)
            tl.act_close(copy(posi, bank(k0, K0)[:, 0:E0]))
            k0 = tl.act_open(act)
            tl.act_close(copy(gate, bank(k0, K0)[:, 0:E0]))
            k0 = tl.act_open(act)
            copy(bupT[:, 0:2, :], bank(k0)[:, 0:16].rearrange("p (k g) -> p k g", k=2))
            tl.act_close(copy(bupT[0:F0 - 256, 2, :], bank(k0, F0 - 256)[:, 16:24]))

            k0 = tl.act_open(act)
            tl.act_close(copy(b1T, bank(k0)[:, 0:NJ * E1].rearrange("p (k e) -> p k e", k=NJ)))

            def gather_waits(i):
                copy(idle[0:1, i:i + 1], cst[0:1, 0:1])

            def e0_silu(e, u, turn):
                v = u % 2
                act.wait_ge(S["e_up"], e + 1)
                wait(act, S["e_down"], e - 1)
                gather_waits(v)
                g = e // GRP if known(e) else turn
                for k, (a, n) in enumerate(F0C):
                    act.activation(act0[v][0:n, k, :], bank(2 + v, n)[:, k * K0:(k + 1) * K0], ACT.Silu,
                                   bias=bupT[0:n, k, bass.ds(g, 1)]).then_inc(S["e_act"], 1)

            act.wait_ge(S["ones_in"], 1)
            loop(act, E0, D, 0, e0_silu, step=D)
            y0_load(act, d_y0[1], TMP)

            def values_out(tag, c):
                nv = C // 2 if tag == "r" else C
                for g in (2 * c, 2 * c + 1):
                    k0 = tl.act_open(act)
                    if tag == "r":
                        tl.act_close(copy(V[:, 4 * g:4 * g + 4, 0:nv], bank(k0, N)[:, 0:4 * nv].rearrange("p (k c) -> p k c", k=4)))
                    else:
                        tl.act_close(copy(Vf[:, 4 * g:4 * g + 4, :, 0:HD],
                                          bank(k0, N).rearrange("p (k h d) -> p k h d", k=4, h=NH)))

            def turned_values(tag, gain=None):
                f = turned(XT[:], gain)

                def g(c):
                    f(c)
                    if c:
                        values_out(tag, c - 1)
                return g

            def attention(tag, rope):
                a = lambda n: A[tag + n]
                values_out(tag, LNC - 1)
                if not rope:
                    for n in range(8 * NB[tag]):
                        act.wait_ge(a("qk_mm"), n + 1)
                        copy(QK[:, n % 4, (n // 4) * 4 * N:(n // 4 + 1) * 4 * N], bank(4 + 2 * (n % 2))[:, 0:4 * N])\
                            .then_inc(a("qk_c"), 1)

                def step(b, u, _turn):
                    act.wait_ge(a("sub"), b + 1)
                    wait(act, a("pT"), b - 1)
                    act.activation(pr2[u], s2[u], ACT.Exp, scale=float(HD) ** -0.5).then_inc(a("exp"), 1)
                    act.wait_ge(a("pT"), b + 1)
                    wait(act, a("o"), b - 1)
                    copy(ptT[u].rearrange("p (a i) t -> p a (i t)", a=2), ps[0:N, 2:4, 0:4 * N]).then_inc(a("pTc"), 1)

                loop(act, B, 2, 2, step, step=2)
                if not rope:
                    untile(XT)

            layernorm(2, H, X, turned_values("r"))
            attention("r", True)
            layernorm(3, H, X)
            act.wait_ge(S["rows_in"], 112)
            layernorm(4, X, X1, turned_values("f", 0))
            attention("f", False)
            layernorm(5, X, X2, turned(XT[:], 2))
            for c in range(LNC):
                act.wait_ge(S["m_max"], c + 1)
                act.activation(lg1[:, chunk(c)], lg1[:, chunk(c)], ACT.Exp).then_inc(S["m_exp"], 1)
                normalised(act, 5, c)
                copy(X2s[:, chunk(c), 0:C], X2[:, chunk(c)]).then_inc(S["m_copied"], 1)

            def e1_gelu(e, u, turn):
                v = u % 2
                act.wait_ge(S["m_up"], e + 1)
                wait(act, S["m_down"], e - 1)
                gather_waits(2 + v)
                for k in range(NJ):
                    act.activation(hT[v][:, k, :], bank(2 + 2 * v + k // 2)[:, (k % 2) * CAP:(k % 2 + 1) * CAP],
                                   ACT.Gelu_apprx_tanh, bias=b1T[:, k, bass.ds(e, 1)]).then_inc(S["m_act"], 1)

            loop(act, E1, 2, 0, e1_gelu, step=2)
            acc_load(act, 1, TMP)

        @block.vector
        def _(dve):
            ch = Chain(dve, S["dve"])
            link = ch.link
            tt, ts, stt = dve.tensor_tensor, dve.tensor_scalar, dve.scalar_tensor_tensor

            dve.memset(XT[:], 0.0).then_inc(S["zeroed"], 1)
            link(dve.memset(zrow, 0.0))
            dve.wait_ge(S["cst_in"], 16)
            dve.memset(zrowi[:, :, C], 2 * T).then_inc(S["zrow_ready"], 1)
            link(dve.tensor_copy(identb[:], ident))
            link(dve.tensor_copy(trib[:], const("tri", N)))
            link(dve.tensor_copy(onesb[:], const("ones", N)[:, 0:N]))
            dve.tensor_copy(causalb[:], const("causal", N)).then_inc(S["consts_ready"], 1)

            for t in range(2):
                dve.wait_ge(S[f"img_in{t}"], 16 * HP)
                dve.tensor_copy(imgp[t].rearrange("p w r x -> p r w x"),
                                img[t].rearrange("p c h (w x) -> p (c h) w x", x=PS)).then_inc(S["img_packed"], 1)

            dve.wait_ge(S["tile_moved"], moved["w"])
            link(dve.tensor_copy(wsplit[:, 0, :], wres[:, 0, :]))
            link(tt(wres[:, 1, :], wres[:, 0, :], wsplit[:, 0, :], ALU.subtract))
            link(dve.tensor_copy(wsplit[:, 1, :], wres[:, 1, :]))
            link(tt(wres[:, 0, :], wres[:, 1, :], wsplit[:, 1, :], ALU.subtract))
            dve.tensor_copy(wsplit[:, 2, :], wres[:, 0, :]).then_inc(S["w_split"], 1)

            def layernorm(k, src, dst, before=None, after=None):
                for c in range(LNC + 1):
                    if c < LNC:
                        if before:
                            before(c)
                        for b in range(8 * c, 8 * c + 8):
                            x = dve.bn_stats(bst[:, b, :], src[:, b, :])
                        link(x)
                        for b in range(8 * c, 8 * c + 8):
                            x = dve.bn_aggr(mv[:, b, :], bst[:, b, :])
                        link(x)
                        ts(stat[:, 0, chunk(c)], mv[:, chunk(c), 1], EPS, None, ALU.add).then_inc(S["ln_var"], 1)
                    if c:
                        ch = chunk(c - 1)
                        dve.wait_ge(S["ln_std"], LNC * k + c)
                        link(dve.reciprocal(stat[:, 2, ch], stat[:, 1, ch]))
                        stt(out=stat[:, 3, ch], in0=mv[:, ch, 0], scalar=-1.0, in1=stat[:, 2, ch], op0=ALU.mult, op1=ALU.mult)\
                            .then_inc(S["ln_affine"], 1)
                        for b in range(8 * c - 8, 8 * c - 8 + LND[c - 1]):
                            x = ts(dst[:, b, :], src[:, b, :], mv[:, b, 0:1], stat[:, 2, b:b + 1], ALU.subtract, ALU.mult)
                        x.then_inc(S["ln_dve"], 1)
                        if after:
                            after(c - 1)

            def spikes(dst, src):
                link(ts(src, src, 4.0, FLOOR, ALU.min, ALU.add))
                return ts(dst, src, FLOOR, None, ALU.subtract)

            dve.wait_ge(S["tile_moved"], moved["H"])
            dve.wait_ge(S["txt_in"], 16)
            layernorm(0, H, X)
            for c in range(LNC):
                dve.wait_ge(S["spk_relu"], c + 1)
                spikes(xsb[:, chunk(c)], TMP[:, chunk(c)]).then_inc(S["spk_ready"], 1)
            dve.wait_ge(S["small_in"], 80)
            for j in range(3):
                for c in range(8):
                    dve.wait_ge(S["qkv_ready"], 8 * j + c + 1)
                    link(dve.bn_stats(bnst[:, c, :], bank(c)[:, 0:4 * N]))
                if j:
                    dve.wait_ge(S["qkv_moved"], 8 * j)
                link(dve.bn_aggr(bnag[:, 0:2], bnst[:].rearrange("p a b -> p (a b)")))
                ts(bnag[:, 2:3], bnag[:, 1:2], EPS, None, ALU.add).then_inc(S["qkv_stats"], 1)
                dve.wait_ge(S["qkv_std"], j + 1)
                link(dve.reciprocal(bnag[:, 4:5], bnag[:, 3:4]))
                link(ts(bnag[:, 5:6], bnag[:, 4:5], gb[:, j:j + 1], NUDGE, ALU.mult, ALU.mult))
                link(tt(bnag[:, 7:8], bnag[:, 0:1], bnag[:, 5:6], ALU.mult))
                stt(out=bnag[:, 6:7], in0=gb[:, 3 + j:4 + j], scalar=NUDGE, in1=bnag[:, 7:8],
                    op0=ALU.mult, op1=ALU.subtract).then_inc(S["qkv_stats"], 1)
                if j:
                    spikes(qkvb[:, j - 1, :], rf[(j - 1) % 2]).then_inc(S["qm_ready"], 1)
            dve.wait_ge(S["qkv_moved"], 24)
            spikes(qkvb[:, 2, :], rf[0]).then_inc(S["qm_ready"], 1)
            dve.wait_ge(S["tile_moved"], moved["xs"])
            dve.wait_ge(S["qm_ready"], 3)
            for h in range(NH):
                a_ = CONST["headmask"][0] + h
                last = ts(qm[:, h, :], qkvb[:, 0, :], cst[:, a_:a_ + 1], None, ALU.mult)
            last.then_inc(S["qm_ready"], 1)

            def spk_a(b, u, _turn):
                dve.wait_ge(S["sT_ready"], b + 1)
                wait(dve, S["o_ready"], b - 1)
                ts(aspk[:, u, :].rearrange("p (g x) -> p g x", g=2), ps[0:N, 2 * u:2 * u + 2, 0:4 * N],
                   4.0, None, ALU.min).then_inc(S["a_ready"], 1)

            loop(dve, B, 2, 2, spk_a, step=2)
            dve.wait_ge(S["o_moved"], B)
            spikes(osb, TMP[:]).then_inc(S["ob_ready"], 1)
            dve.wait_ge(S["h_biased"], 1)

            def add_banks(dst, ready, added):
                def f(c):
                    for g in (2 * c, 2 * c + 1):
                        dve.wait_ge(ready, g + 1)
                        tt(dst[:, 4 * g:4 * g + 4, :], dst[:, 4 * g:4 * g + 4, :],
                           bank(4 + g % 4, N).rearrange("p (k c) -> p k c", k=4), ALU.add).then_inc(added, 1)
                    dve.wait_ge(added, 2 * c + 2)
                return f

            def add_tmp(k):
                def f(c):
                    if c:
                        dve.wait_ge(S["h_added"], (k - 2) * (LNC - 1) + c)
                    else:
                        if k == 2:
                            dve.wait_ge(S["y0_in0"], 64)
                        link(tt(H[:, chunk(0)], H[:, chunk(0)], TMP[:, chunk(0)], ALU.add))
                return f

            layernorm(1, H, X, before=add_banks(H, S["proj_ready"], S["proj_added"]))
            dve.wait_ge(S["lg_ready"], 1)
            link(tt(lg, ps[0:N, 4:6, :].rearrange("p a (b e) -> p (a b) e", e=E0), brow(rbias[:], B), ALU.add))
            link(dve.tensor_reduce(stat[:, 6, :], lg, AXX, ALU.max))
            tt(lg, lg, bcol(stat[:, 6, :], E0), ALU.subtract).then_inc(S["lg_sub"], 1)
            dve.wait_ge(S["lg_exp"], 1)
            link(dve.tensor_reduce(stat[:, 6, :], lg, AXX, ALU.add))
            link(dve.reciprocal(stat[:, 7, :], stat[:, 6, :]))
            tt(pr.rearrange("p j q e -> p q j e"), lg.rearrange("p (q j) e -> p q j e", q=Q0),
               stat[:, 7, :].rearrange("p (q j) -> p q j", q=Q0).unsqueeze(3).broadcast_to([N, Q0, B // Q0, E0]), ALU.mult).then_inc(S["pr_ready"], 1)
            dve.wait_ge(S["lg_ready"], 2)
            link(dve.tensor_copy(sc[0].rearrange("p (a x) -> p a x", a=2), ps[:, 6:8, 0:4 * N]))
            for r in range(R8):
                v8, i8 = cv[:, 8 * r:8 * r + 8], ci[:, 8 * r:8 * r + 8]
                here, other = sc[r % 2], sc[1 - r % 2]
                link(dve.max(v8, here))
                last = dve.max_index(i8, v8, here)
                if r < R8 - 1:
                    last = dve.match_replace(other, v8, here, -1.0)
                link(last)
            link(dve.tensor_copy(cif, ci))
            link(ts(cif, cif, const("quarter"), None, ALU.add))
            dve.tensor_copy(cii, cif).then_inc(S["cand_ready"], 1)
            dve.wait_ge(S["vm_in"], 64)
            link(dve.tensor_copy(vm[1], vm[0]))
            vmq = [v.rearrange("p (q r) -> p q r", q=Q0) for v in vm]
            for r in range(R8):
                v8, i8, vr = gv[:, 8 * r:8 * r + 8], gp[:, 8 * r:8 * r + 8], vmq[r % 2][:, :, 0:8 * r + 8]
                link(dve.max(v8, vr))
                last = dve.max_index(i8, v8, vm[r % 2][:, 0:(Q0 - 1) * CQ + 8 * r + 8])
                if r < R8 - 1:
                    last = dve.match_replace(vmq[1 - r % 2][:, :, 0:8 * r + 8], v8, vr, -1.0)
                link(last)
            link(dve.tensor_copy(gpf, gp))
            ts(gpf, gpf, const("expert", E0), None, ALU.add).then_inc(S["gp_ready"], 1)
            dve.wait_ge(S["tile_moved"], moved["gT"])

            link(dve.memset(act0[0][64:128, 2, :], 1.0))
            dve.memset(act0[1][64:128, 2, :], 1.0).then_inc(S["ones_in"], 1)

            def e0_move(e, u, turn):
                v = u % 2
                dve.wait_ge(S["e_xT"], e + 1)
                wait(dve, S["e_up"], e - 1)
                dve.tensor_copy(xgT[v], bank(v)[:, 0:K0]).then_inc(S["e_xTc"], 1)

            def e0_out(e, u, turn):
                if not known(e) or e + 2 < E0:
                    e0_move(e + 2, (u + 2) % D, None)
                dve.wait_ge(S["e_down"], e + 1)
                wait(dve, S[f"e_sc{u % 2}"], (e // 2 - 1) * 16 if known(e) else (turn * 2 + (u // 2 - 1)) * 16)
                ts(yo0[u], bank(4 + u % 2, K0)[:, 0:C], gate[:, bass.ds(e, 1)], None, ALU.mult).then_inc(S["e_out"], 1)

            e0_move(0, 0, None)
            e0_move(1, 1, None)
            loop(dve, E0, D, D, e0_out, step=D)

            def rotate(c):
                for n in range(6 * c, 6 * c + 6):
                    k, u = n % 3, n % 2
                    dve.wait_ge(A["rqk_mm"], n + 1)
                    if n >= 2:
                        dve.wait_ge(A["rqk_c"], n - 1)
                    for s_, nm in enumerate(("rope_c", "rope_s")):
                        x = tt(rt[u][:, s_, :].rearrange("p (b t) -> p b t", b=4),
                               bank(4 + 2 * u + s_)[:, 0:4 * N].rearrange("p (b t) -> p b t", b=4),
                               brow(const(nm)[:, k * N:(k + 1) * N], 4), ALU.mult)
                    x.then_inc(A["rrope"], 1)

            def attention(tag, rope):
                a = lambda n: A[tag + n]

                def finish(b, u):
                    dve.wait_ge(a("o"), b + 1)
                    if rope:
                        o8 = ps[0:N, 0:2, :].rearrange("p a (k x) -> p (a k) x", k=4)
                        dve.reciprocal(rrec[u].unsqueeze(2), o8[:, :, 64:65]).then_inc(a("rec"), 1)
                        dve.wait_ge(a("rec"), b + 1)
                        tt(mg, const("regroup", N).rearrange("p (k g) -> p k g", g=4), bcol(rrec[u], 4), ALU.mult)\
                            .then_inc(a("mask"), 1)
                        dve.wait_ge(a("mask"), b + 1)
                        tt(og, o8[:, :, 0:64].rearrange("p k (g d) -> p k g d", g=4),
                           mg.unsqueeze(3).broadcast_to([N, 8, 4, HD]), ALU.mult).then_inc(a("group"), 1)
                        dve.wait_ge(a("group"), b + 1)
                        dve.tensor_reduce(TMP[:, bass.ds(b, 1), :].rearrange("p b (k d) -> p (b k) d", k=8),
                                          og.rearrange("p k g d -> p k d g"), AXX, ALU.add).then_inc(a("o_c"), 1)
                    else:
                        o = bank(u, N)[:, 0:NH * VW].rearrange("p (h d) -> p h d", h=NH)
                        dve.reciprocal(rrec[u].unsqueeze(2), o[:, :, HD:VW]).then_inc(a("rec"), 1)
                        dve.wait_ge(a("rec"), b + 1)
                        tt(TMP[:, bass.ds(b, 1), :].rearrange("p b (h d) -> p (b h) d", h=NH), o[:, :, 0:HD],
                           rrec[u].unsqueeze(2).broadcast_to([N, NH, HD]), ALU.mult).then_inc(a("o_c"), 1)

                def step(b, u, _turn):
                    if not known(b) or b < B:
                        dve.wait_ge(a("sc"), b + 1)
                        scv = ps[0:N, 4 + 2 * u:6 + 2 * u, 0:4 * N].rearrange("p g (j t) -> p g j t", j=4)
                        dve.tensor_reduce(nmx[u].rearrange("p (g j) -> p g j", g=2), scv, AXX, ALU.max).then_inc(a("max"), 1)
                        dve.wait_ge(a("max"), b + 1)
                        wait(dve, a("exp"), b - 1)
                        mv = nmx[u].rearrange("p (g j) -> p g j", g=2).unsqueeze(3).broadcast_to([N, 2, 4, N])
                        tt(s2[u].rearrange("p (g j) t -> p g j t", g=2), scv, mv, ALU.subtract).then_inc(a("sub"), 1)
                    if not known(b) or b >= 2:
                        finish(b - 2, u)

                loop(dve, B, 2, 2, step, step=2)
                step(B, 0, None)
                step(B + 1, 1, None)
                dve.wait_ge(a("o_c"), B)

            layernorm(2, H, X, before=add_tmp(2))
            for c in range(LNC):
                rotate(c)
            attention("r", True)
            layernorm(3, H, X, before=add_tmp(3))
            layernorm(4, X, X1, before=lambda c: normalised(dve, 3, c))
            attention("f", False)

            layernorm(5, X, X2, before=add_banks(X, A["fw"], A["fw_c"]))
            link(dve.memset(cumb[:, 0:1, :], 0.0))
            link(dve.tensor_copy(X2i[:, :, C], const("token", N)[:, 0:B]))
            link(dve.tensor_copy(X2si[:, :, C], const("token", N)[:, B:2 * B]))

            def shift(c):
                ch, lgc = chunk(c), bank(4 + c, N).rearrange("p (b e) -> p b e", e=E1)
                dve.wait_ge(S["m_lg"], c + 1)
                link(dve.tensor_reduce(stat[:, 6, ch], lgc, AXX, ALU.max))
                tt(lg1[:, ch], lgc, bcol(stat[:, 6, ch], E1), ALU.subtract).then_inc(S["m_max"], 1)

            def choose(c):
                ch, bs = chunk(c), range(8 * c, 8 * c + 8)
                dve.wait_ge(S["m_exp"], c + 1)
                link(dve.tensor_reduce(stat[:, 6, ch], lg1[:, ch], AXX, ALU.add))
                link(dve.reciprocal(stat[:, 7, ch], stat[:, 6, ch]))
                link(tt(pr1[:, ch], lg1[:, ch], bcol(stat[:, 7, ch], E1), ALU.mult))
                for b in bs:
                    x = dve.max(mx8[:, b, :], pr1[:, b, :])
                link(x)
                for b in bs:
                    x = dve.max_index(ix8[:, b, :], mx8[:, b, :], pr1[:, b, :])
                link(x)
                link(dve.tensor_copy(ef[:, ch], ix8[:, ch]))
                for k in range(2):
                    x = tt(oh[:, k], brow(const("iota", N), 8), bcol(ef[:, ch, k], E1), ALU.is_equal)
                link(x)
                link(tt(mb[:, ch], oh[:, 0], oh[:, 1], ALU.add))
                if c:
                    dve.wait_ge(S["m_m"], c)
                last = min(8 * c + 7, B - 2)
                for b in range(8 * c, last):
                    link(tt(cumb[:, b + 1, :], cumb[:, b, :], mb[:, b, :], ALU.add))
                tt(cumb[:, last + 1, :], cumb[:, last, :], mb[:, last, :], ALU.add).then_inc(S["m_m"], 1)

            def place(c):
                ch = chunk(c)
                kb = lambda v: v[:, ch, 0:2].rearrange("p b k -> p k b")
                cum = bank(4 + c, N).rearrange("p (b e) -> p b e", e=E1)
                link(tt(wsum[:, 0], mx8[:, ch, 0], mx8[:, ch, 1], ALU.add))
                link(dve.reciprocal(wsum[:, 1], wsum[:, 0]))
                dve.wait_ge(S["m_cum"], c + 1)
                for k in range(2):
                    x = tt(oh[:, k], cum, oh[:, k], ALU.mult)
                link(x)
                link(dve.tensor_reduce(route[:, 0], oh, AXX, ALU.add))
                link(ts(route[:, 1], route[:, 0], float(CAP), None, ALU.is_lt))
                stt(out=route[:, 2], in0=kb(ef), scalar=float(CAP), in1=route[:, 0], op0=ALU.mult, op1=ALU.add)
                link(ts(route[:, 3], route[:, 1], -float(S1), float(S1), ALU.mult, ALU.add))
                link(tt(route[:, 4], route[:, 2], route[:, 3], ALU.add))
                dve.tensor_copy(sidx[:, :, ch], route[:, 4])
                for k in range(2):
                    x = tt(route[:, 5, k], mx8[:, ch, k], wsum[:, 1], ALU.mult)
                link(x)
                for k, rows_ in enumerate((X2r, X2s)):
                    x = tt(rows_[:, ch, C + 1], route[:, 5, k], route[:, 1, k], ALU.mult)
                x.then_inc(S["m_rows"], 1)

            shift(0)
            shift(1)
            for c in range(LNC):
                choose(c)
                place(c)
                if c + 2 < LNC:
                    shift(c + 2)
            link(tt(H[:], H[:], X[:], ALU.add))
            dve.wait_ge(S["b2_in"], 16)

            def e1_move(e, u, turn):
                dve.wait_ge(S["m_xT"], e + 1)
                wait(dve, S["m_up"], e - 1)
                ts(xinT[u % 2], bank(u % 2)[:, 0:CAP], gains[:, 2:3], gains[:, 3:4], ALU.mult, ALU.add)\
                    .then_inc(S["m_xTc"], 1)

            def e1_out(e, u, turn):
                if not known(e) or e + 2 < E1:
                    e1_move(e + 2, u + 2, None)
                dve.wait_ge(S["m_down"], e + 1)
                wait(dve, S[f"m_sc{u % D}"], (2 * turn + u // D) * 32)
                for k, (a, n) in enumerate(CAPT):
                    tt(yo1[u % D][0:n, k, :], bank(6 + u % 2, n)[:, k * C:(k + 1) * C], b2[0:n, bass.ds(e * C, C)], ALU.add)\
                        .then_inc(S["m_biased"], 1)
                dve.wait_ge(S["m_biased"], e * 2 + 2)
                for k, (a, n) in enumerate(CAPT):
                    x = ts(yo1[u % D][0:n, k, :], yo1[u % D][0:n, k, :], xin[u][0:n, k, C + 1:C + 2], None, ALU.mult)
                x.then_inc(S["m_out"], 1)

            e1_move(0, 0, None)
            e1_move(1, 1, None)
            loop(dve, E1, DX, DX, e1_out, step=DX)

            q = B // 4
            for i in range(4):
                r = slice(i * q, (i + 1) * q)
                dve.wait_ge(S[f"fin_in{i}"], 64)
                link(tt(H[:, r], H[:, r], X[:, r], ALU.add))
                tt(H[:, r], H[:, r], TMP[:, r], ALU.add).then_inc(S["fin_ready"], 1)

        @block.gpsimd
        def _(pool):
            off = lambda ap: bass.IndirectOffsetOnAxis(ap=ap, axis=0)
            pool.wait_ge(S["rows_in"], 112)
            normalised(pool, 0)
            pool.tensor_tensor(H[:], H[:], brow(bproj[:], B), ALU.add).then_inc(S["h_biased"], 1)
            pool.wait_ge(S["cand_out"], 64)
            pool.wait_ge(S["tile_moved"], moved["gT"])
            def lookup(e):
                pool.indirect_dma_start(itok[:, e:e + 1], None, d_cand, off(posi[:, e:e + 1])).then_inc(S[f"itok_in{e % D}"], 16)

            def gather(e):
                pool.wait_ge(S[f"itok_in{e % D}"], 16 * (e // D + 1))
                if e >= D:
                    pool.wait_ge(S["e_xT"], e - D + 1)
                pool.indirect_dma_start(xg[e % D], None, d_x0, off(itok[:, e:e + 1])).then_inc(S[f"g_in{e % D}"], 16)

            for e in range(D):
                lookup(e)
            pool.wait_ge(S["x0_out"], 32)
            pool.wait_ge(S["h_out"], 32)
            pool.wait_ge(S["y0_zero"], 48)
            for e in range(E0 + D):
                if e < E0:
                    gather(e)
                    if e + D < E0:
                        lookup(e + D)
                if e >= D:
                    f = e - D
                    pool.wait_ge(S["e_out"], f + 1)
                    if f >= 2:
                        pool.wait_ge(S[f"e_sc{f % 2}"], 16 * (f // 2))
                    pool.indirect_dma_start(d_y0[f % 2], off(itok[:, f:f + 1]), yo0[f % D], None, compute_op=ALU.add)\
                        .then_inc(S[f"e_sc{f % 2}"], 16)

            def attention(tag, rope):
                a = lambda n: A[tag + n]
                pool.wait_ge(a("w_in"), 48 if rope else 64)
                n = [0]

                def put(dst, src):
                    n[0] += 1
                    pool.tensor_copy(dst, src).then_inc(a("wpad"), 1)

                if rope:
                    n[0] += 1
                    pool.memset(wpad, 0.0).then_inc(a("wpad"), 1)
                    for u in range(2):
                        pool.memset(kz[u], 0.0).then_inc(a("kz"), 1)
                    pool.wait_ge(a("wpad"), 1)
                def blocks(at, src, swaps):
                    put(wpad[:, at, :].rearrange("p (j d) -> p j d", j=4)[:, :, 0:HD], src)
                    if swaps:
                        d2 = wpad[:, 4 + at, :].rearrange("p (j d e) -> p j d e", j=4, e=2)
                        s2_ = src.rearrange("p j (d e) -> p j d e", e=2)
                        for par in range(2):
                            put(d2[:, :, 0:HD // 2, par], s2_[:, :, :, 1 - par])

                if rope:
                    wq = wraw[:, 0:C].rearrange("p (j g d) -> p g j d", j=4, g=2)
                    for g in range(2):
                        blocks(g, wq[:, g], True)
                    blocks(2, wraw[:, C:C + C // 2].rearrange("p (j d) -> p j d", j=4), True)
                else:
                    for g in range(2):
                        blocks(g, wraw[:, 0:C].rearrange("p (g j d) -> p g j d", g=2, j=4)[:, g], False)
                        blocks(2 + g, wraw[:, C:2 * C].rearrange("p (g j d) -> p g j d", g=2, j=4)[:, g], False)
                assert n[0] == WPAD[tag]
                if rope:
                    for n in range(24):
                        u = n % 2
                        pool.wait_ge(a("rope"), n + 1)
                        pool.tensor_tensor(QK[:, n % 3, (n // 3) * 4 * N:(n // 3 + 1) * 4 * N], rt[u][:, 0, :], rt[u][:, 1, :],
                                           ALU.add).then_inc(a("qk_c"), 1)
                    pool.memset(V[:, :, 64:65], 1.0).then_inc(a("ones"), 1)
                else:
                    pool.wait_ge(A["ro_c"], B)
                    pool.memset(Vf[:, :, :, HD:VW], 1.0).then_inc(a("ones"), 1)

                def step(b, u, _turn):
                    if known(b) and b == 0:
                        pool.wait_ge(a("qk_c"), NB[tag])
                    wait(pool, a("sc"), b - 1)
                    pool.tensor_copy(qs[u], QK[:, 0:2, bass.ds(b * N, N)]).then_inc(a("q_c"), 1)
                    if known(b) and b == 1:
                        pool.wait_ge(a("qk_c"), 8 * NB[tag])

                loop(pool, B, 2, 2, step, step=2)

            def add_tmp(c):
                pool.tensor_tensor(H[:, chunk(c)], H[:, chunk(c)], TMP[:, chunk(c)], ALU.add).then_inc(S["h_added"], 1)

            for c in range(1, LNC):
                pool.wait_ge(S[f"y0_in{c}"], 64)
                add_tmp(c)
            attention("r", True)
            pool.wait_ge(A["ro_c"], B)
            for c in range(1, LNC):
                add_tmp(c)
            attention("f", False)

            pool.wait_ge(S["buf_zeroed"], 32)
            for c in range(LNC):
                pool.wait_ge(S["m_rows"], c + 1)
                pool.wait_ge(S["m_copied"], c + 1)
                normalised(pool, 5, c)
                for k, rows_ in enumerate((X2r, X2s)):
                    for b in range(8 * c, 8 * c + 8):
                        pool.indirect_dma_start(d_buf, off(sidx[:, k, b:b + 1]), rows_[:, b, :], None,
                                                bounds_check=S1 - 1, oob_is_err=False).then_inc(S[f"m_scat{k}"], 16)
            for e in range(E1):
                pool.wait_ge(S["m_out"], e + 1)
                for k, (a, n) in enumerate(CAPT):
                    pool.indirect_dma_start(d_acc, off(xini[e % DX][0:n, k, C:C + 1]), yo1[e % D][0:n, k, :], None,
                                            bounds_check=2 * T - 1, oob_is_err=False).then_inc(S[f"m_sc{e % D}"], 16)


_INS = ["x", "txt", "L0_tok_w", "L0_tok_b", "L0_attn_Wqkv", "L0_attn_gamma", "L0_attn_beta", "L0_attn_Wproj",
        "L0_attn_bproj", "L0_ffn_W_router", "L0_ffn_b_router", "L0_ffn_W_up", "L0_ffn_b_up", "L0_ffn_W_down",
        "L0_ffn_b_down", "L1_attn_Wq", "L1_attn_Wk", "L1_attn_Wv", "L1_ffn_ln1_g", "L1_ffn_ln1_b", "L1_ffn_wq",
        "L1_ffn_wk", "L1_ffn_wv", "L1_ffn_wo", "L1_ffn_ln2_g", "L1_ffn_ln2_b", "L1_ffn_wr", "L1_ffn_w1",
        "L1_ffn_b1", "L1_ffn_w2", "L1_ffn_b2"]


def kernel(**inputs):
    import numpy as _np
    import concourse.bacc as _bacc
    from concourse import mybir as _mybir
    from concourse.bass_utils import run_bass_kernel_spmd as _run

    nc = _bacc.Bacc("TRN2", target_bir_lowering=False, num_devices=1)
    arrays, aps = {}, {}
    for name in _INS:
        a = _np.ascontiguousarray(inputs[name])
        arrays[f"in_{name}"] = a
        aps[name] = nc.dram_tensor(f"in_{name}", a.shape, _mybir.dt.from_np(a.dtype), kind="ExternalInput").ap()
    arrays["consts"] = shape_constants()
    consts = nc.dram_tensor("consts", [128, NCONST], _mybir.dt.float32, kind="ExternalInput").ap()
    out = nc.dram_tensor("out", [B, N, C], _mybir.dt.float32, kind="ExternalOutput").ap()
    program(nc, aps, out, consts)
    r = _run(nc, [arrays], core_ids=[0])
    return r.results[0]["out"]
```
